# Optimizing a Trainium2 kernel written in Bass

```python
import numpy as np
import jax
import jax.numpy as jnp

def _softmax(x, axis=-1):
    return jax.nn.softmax(x, axis=axis)

def _gelu(x):
    return jax.nn.gelu(x, approximate=True)

def _silu(x):
    return jax.nn.silu(x)

def _sigmoid(x):
    return jax.nn.sigmoid(x)

def _layernorm(x, axis=-1, eps=1e-05):
    m = jnp.mean(x, axis=axis, keepdims=True)
    v = jnp.var(x, axis=axis, keepdims=True)
    return (x - m) / jnp.sqrt(v + eps)

def _scatter_add(tgt, idx, src, axis=0):
    return tgt.at[idx].add(src)

def _segment_sum(src, seg, n):
    return jax.ops.segment_sum(src, seg, n)
kernel_name = 'mk_xattn_seq_d4_seqx_r4_843a72'

def setup_inputs(seed: int=0):
    np.random.seed(seed)
    _w = jnp.asarray

    def _rec_inputs():
        import jax
        import jax.numpy as jnp
        _rk = jax.random.key(seed)
        x = 7.22e-05 + 1 * jax.random.normal(jax.random.fold_in(_rk, 1), (8, 112, 512), jnp.float32)
        _lenS = 112 - jax.random.randint(jax.random.fold_in(_rk, 7), (8,), 0, max(1, 112 // 4) + 1, jnp.int32)
        _lenS2 = 375 - jax.random.randint(jax.random.fold_in(_rk, 8), (8,), 0, max(1, 375 // 4) + 1, jnp.int32)
        _ctx_2048P = jax.random.normal(jax.random.fold_in(_rk, 11), (8, 16, 512), jnp.float32)
        _ctx_2048c = jax.random.dirichlet(jax.random.fold_in(_rk, 511), 0.3 * jnp.ones((16,), jnp.float32), (8, 375))
        _ctx_2048t = jnp.einsum('bsk,bkd->bsd', _ctx_2048c, _ctx_2048P)
        _ctx_2048t = _ctx_2048t * jax.lax.rsqrt(jnp.mean(jnp.square(_ctx_2048t)) + 1e-12) * 0.953939
        ctx_2048 = 4.13588e-05 + 0.999923 * (_ctx_2048t + 0.3 * jax.random.normal(jax.random.fold_in(_rk, 611), (8, 375, 512), jnp.float32))
        _validS = jnp.arange(112)[None, :] < _lenS[:, None]
        _validS2 = jnp.arange(375)[None, :] < _lenS2[:, None]
        _causal = jnp.tril(jnp.ones((112, 112), dtype=bool))
        mask_Bx1xSxS2_ff0 = jnp.where(jnp.ones((8, 1, 112, 375), dtype=bool), 0.0, -1000000000.0).astype(jnp.float32)
        mask_BxS2_bf1 = jnp.ones((8, 375), dtype=bool)
        return (x, ctx_2048, mask_Bx1xSxS2_ff0, mask_BxS2_bf1)
    x, ctx_2048, mask_Bx1xSxS2_ff0, mask_BxS2_bf1 = _rec_inputs()

    def _L0_xattn_setup():
        import jax, jax.numpy as jnp
        import numpy as np
        H = 512
        NH = 32
        KVH = 8
        HD = H // NH
        GROUPS = NH // KVH
        EPS = 1e-06
        B, L, S = (4, 256, 256)

        def _gqa_forward(hidden_state, encoder_hidden_state, encoder_attention_mask, Wq, bq, Wk, bk, Wv, bv, Wo, bo, gamma, beta):
            b, l, _ = hidden_state.shape
            s = encoder_hidden_state.shape[1]
            q = hidden_state @ Wq + bq
            k = encoder_hidden_state @ Wk + bk
            v = encoder_hidden_state @ Wv + bv
            q = q.reshape(b, l, KVH, GROUPS, HD).transpose(0, 2, 3, 1, 4)
            k = k.reshape(b, s, KVH, HD).transpose(0, 2, 1, 3)
            v = v.reshape(b, s, KVH, HD).transpose(0, 2, 1, 3)
            scale = 1.0 / jnp.sqrt(jnp.asarray(HD, q.dtype))
            scores = jnp.einsum('bkgld,bksd->bkgls', q, k) * scale
            scores = scores + encoder_attention_mask[:, :, None, :, :]
            attn = jax.nn.softmax(scores, axis=-1)
            out = jnp.einsum('bkgls,bksd->bkgld', attn, v)
            out = out.transpose(0, 3, 1, 2, 4).reshape(b, l, H)
            out = out @ Wo + bo
            x = out + hidden_state
            mu = jnp.mean(x, axis=-1, keepdims=True)
            var = jnp.var(x, axis=-1, keepdims=True)
            return (x - mu) * jax.lax.rsqrt(var + EPS) * gamma + beta
        key = jax.random.key(seed)
        ks = jax.random.split(key, 12)
        sd = 0.02
        return {'hidden_state': jax.random.normal(ks[0], (B, L, H), jnp.float32), 'encoder_hidden_state': jax.random.normal(ks[1], (B, S, H), jnp.float32), 'encoder_attention_mask': jnp.zeros((B, 1, L, S), jnp.float32), 'Wq': jax.random.normal(ks[2], (H, H), jnp.float32) * sd, 'bq': jnp.zeros((H,), jnp.float32), 'Wk': jax.random.normal(ks[3], (H, KVH * HD), jnp.float32) * sd, 'bk': jnp.zeros((KVH * HD,), jnp.float32), 'Wv': jax.random.normal(ks[4], (H, KVH * HD), jnp.float32) * sd, 'bv': jnp.zeros((KVH * HD,), jnp.float32), 'Wo': jax.random.normal(ks[5], (H, H), jnp.float32) * sd, 'bo': jnp.zeros((H,), jnp.float32), 'gamma': jnp.ones((H,), jnp.float32), 'beta': jnp.zeros((H,), jnp.float32)}
    _L0_xattn_all = _L0_xattn_setup()
    _L0_xattn_in = {k: v for k, v in _L0_xattn_all.items() if k in ('Wq', 'bq', 'Wk', 'bk', 'Wv', 'bv', 'Wo', 'bo', 'gamma', 'beta')}
    del _L0_xattn_all

    def _L1_xattn_setup():
        import jax, jax.numpy as jnp
        import numpy as np
        H = 512
        NH = 32
        KVH = 8
        HD = H // NH
        GROUPS = NH // KVH
        EPS = 1e-06
        B, L, S = (4, 256, 256)

        def _gqa_forward(hidden_state, encoder_hidden_state, encoder_attention_mask, Wq, bq, Wk, bk, Wv, bv, Wo, bo, gamma, beta):
            b, l, _ = hidden_state.shape
            s = encoder_hidden_state.shape[1]
            q = hidden_state @ Wq + bq
            k = encoder_hidden_state @ Wk + bk
            v = encoder_hidden_state @ Wv + bv
            q = q.reshape(b, l, KVH, GROUPS, HD).transpose(0, 2, 3, 1, 4)
            k = k.reshape(b, s, KVH, HD).transpose(0, 2, 1, 3)
            v = v.reshape(b, s, KVH, HD).transpose(0, 2, 1, 3)
            scale = 1.0 / jnp.sqrt(jnp.asarray(HD, q.dtype))
            scores = jnp.einsum('bkgld,bksd->bkgls', q, k) * scale
            scores = scores + encoder_attention_mask[:, :, None, :, :]
            attn = jax.nn.softmax(scores, axis=-1)
            out = jnp.einsum('bkgls,bksd->bkgld', attn, v)
            out = out.transpose(0, 3, 1, 2, 4).reshape(b, l, H)
            out = out @ Wo + bo
            x = out + hidden_state
            mu = jnp.mean(x, axis=-1, keepdims=True)
            var = jnp.var(x, axis=-1, keepdims=True)
            return (x - mu) * jax.lax.rsqrt(var + EPS) * gamma + beta
        key = jax.random.key(seed)
        ks = jax.random.split(key, 12)
        sd = 0.02
        return {'hidden_state': jax.random.normal(ks[0], (B, L, H), jnp.float32), 'encoder_hidden_state': jax.random.normal(ks[1], (B, S, H), jnp.float32), 'encoder_attention_mask': jnp.zeros((B, 1, L, S), jnp.float32), 'Wq': jax.random.normal(ks[2], (H, H), jnp.float32) * sd, 'bq': jnp.zeros((H,), jnp.float32), 'Wk': jax.random.normal(ks[3], (H, KVH * HD), jnp.float32) * sd, 'bk': jnp.zeros((KVH * HD,), jnp.float32), 'Wv': jax.random.normal(ks[4], (H, KVH * HD), jnp.float32) * sd, 'bv': jnp.zeros((KVH * HD,), jnp.float32), 'Wo': jax.random.normal(ks[5], (H, H), jnp.float32) * sd, 'bo': jnp.zeros((H,), jnp.float32), 'gamma': jnp.ones((H,), jnp.float32), 'beta': jnp.zeros((H,), jnp.float32)}
    _L1_xattn_all = _L1_xattn_setup()
    _L1_xattn_in = {k: v for k, v in _L1_xattn_all.items() if k in ('Wq', 'bq', 'Wk', 'bk', 'Wv', 'bv', 'Wo', 'bo', 'gamma', 'beta')}
    del _L1_xattn_all

    def _L2_xattn_setup():
        import jax, jax.numpy as jnp
        import numpy as np
        HIDDEN = 512
        HEADS = 16
        HEAD_DIM = HIDDEN // HEADS
        LN_EPS = 1e-05
        GATE_INIT = 0.5

        def _layer_norm(x, gamma, beta):
            mu = jnp.mean(x, axis=-1, keepdims=True)
            var = jnp.mean(jnp.square(x - mu), axis=-1, keepdims=True)
            return (x - mu) * jax.lax.rsqrt(var + LN_EPS) * gamma + beta
        key = jax.random.key(seed)
        ks = jax.random.split(key, 8)
        B, T_TEXT, T_AUDIO = (4, 512, 375)
        s = 0.02
        return {'hidden_states': jax.random.normal(ks[0], (B, T_TEXT, HIDDEN), jnp.float32), 'audio_kv': jax.random.normal(ks[1], (B, T_AUDIO, HIDDEN), jnp.float32), 'audio_attention_mask': jnp.ones((B, T_AUDIO), dtype=bool), 'Wq': jax.random.normal(ks[2], (HIDDEN, HIDDEN), jnp.float32) * s, 'Wk': jax.random.normal(ks[3], (HIDDEN, HIDDEN), jnp.float32) * s, 'Wv': jax.random.normal(ks[4], (HIDDEN, HIDDEN), jnp.float32) * s, 'Wo': jax.random.normal(ks[5], (HIDDEN, HIDDEN), jnp.float32) * s, 'ln_gamma': jnp.ones((HIDDEN,), jnp.float32), 'ln_beta': jnp.zeros((HIDDEN,), jnp.float32), 'gate': jnp.array([GATE_INIT], jnp.float32)}
    _L2_xattn_all = _L2_xattn_setup()
    _L2_xattn_in = {k: v for k, v in _L2_xattn_all.items() if k in ('Wq', 'Wk', 'Wv', 'Wo', 'ln_gamma', 'ln_beta', 'gate')}
    del _L2_xattn_all

    def _L3_xattn_setup():
        import jax, jax.numpy as jnp
        import numpy as np
        B, Q, S1, S2 = (4, 64, 512, 512)
        D, H, K, F = (512, 16, 128, 2048)
        LN_EPS = 1e-05

        def _layer_norm(x, scale, offset):
            mu = jnp.mean(x, axis=-1, keepdims=True)
            var = jnp.var(x, axis=-1, keepdims=True)
            return (x - mu) * jax.lax.rsqrt(var + LN_EPS) * scale + offset

        def _cross_attention(q_in, kv_in, wq, bq, wk, bk, wv, bv, wo, bo, bias_k, bias_v):
            b, q_len, _ = q_in.shape
            t = kv_in.shape[1]
            qh = (q_in @ wq + bq).reshape(b, q_len, H, K)
            kh = (kv_in @ wk + bk).reshape(b, t, H, K)
            vh = (kv_in @ wv + bv).reshape(b, t, H, K)
            kh = jnp.concatenate([kh, jnp.broadcast_to(bias_k, (b, 1, H, K))], axis=1)
            vh = jnp.concatenate([vh, jnp.broadcast_to(bias_v, (b, 1, H, K))], axis=1)
            scale = jnp.sqrt(jnp.asarray(K, q_in.dtype))
            logits = jnp.einsum('bqhk,bthk->bhqt', qh, kh) / scale
            weights = jax.nn.softmax(logits, axis=-1)
            ctx = jnp.einsum('bhqt,bthk->bqhk', weights, vh).reshape(b, q_len, H * K)
            return ctx @ wo + bo

        def _forward(x, xf_1, xf_2, ln1_scale, ln1_offset, wq1, bq1, wk1, bk1, wv1, bv1, wo1, bo1, bias_k1, bias_v1, ln2_scale, ln2_offset, wq2, bq2, wk2, bk2, wv2, bv2, wo2, bo2, bias_k2, bias_v2, ln_mlp_scale, ln_mlp_offset, w_fc1, b_fc1, w_fc2, b_fc2):
            res = x
            h = _layer_norm(x, ln1_scale, ln1_offset)
            x = res + _cross_attention(h, xf_1, wq1, bq1, wk1, bk1, wv1, bv1, wo1, bo1, bias_k1, bias_v1)
            res = x
            h = _layer_norm(x, ln2_scale, ln2_offset)
            x = res + _cross_attention(h, xf_2, wq2, bq2, wk2, bk2, wv2, bv2, wo2, bo2, bias_k2, bias_v2)
            h = _layer_norm(x, ln_mlp_scale, ln_mlp_offset)
            h = jax.nn.gelu(h @ w_fc1 + b_fc1, approximate=False) @ w_fc2 + b_fc2
            return x + h
        key = jax.random.key(seed)
        ks = iter(jax.random.split(key, 64))

        def rn(shape, s=0.02):
            return jax.random.normal(next(ks), shape, jnp.float32) * s
        inp = {'x': rn((B, Q, D), 1.0), 'xf_1': rn((B, S1, D), 1.0), 'xf_2': rn((B, S2, D), 1.0)}
        for i in (1, 2):
            inp[f'ln{i}_scale'] = jnp.ones((D,), jnp.float32)
            inp[f'ln{i}_offset'] = jnp.zeros((D,), jnp.float32)
            inp[f'wq{i}'] = rn((D, H * K))
            inp[f'bq{i}'] = jnp.zeros((H * K,), jnp.float32)
            inp[f'wk{i}'] = rn((D, H * K))
            inp[f'bk{i}'] = jnp.zeros((H * K,), jnp.float32)
            inp[f'wv{i}'] = rn((D, H * K))
            inp[f'bv{i}'] = jnp.zeros((H * K,), jnp.float32)
            inp[f'wo{i}'] = rn((H * K, D))
            inp[f'bo{i}'] = jnp.zeros((D,), jnp.float32)
            inp[f'bias_k{i}'] = rn((1, 1, H, K))
            inp[f'bias_v{i}'] = rn((1, 1, H, K))
        inp['ln_mlp_scale'] = jnp.ones((D,), jnp.float32)
        inp['ln_mlp_offset'] = jnp.zeros((D,), jnp.float32)
        inp['w_fc1'] = rn((D, F))
        inp['b_fc1'] = jnp.zeros((F,), jnp.float32)
        inp['w_fc2'] = rn((F, D))
        inp['b_fc2'] = jnp.zeros((D,), jnp.float32)
        return inp
    _L3_xattn_all = _L3_xattn_setup()
    _L3_xattn_in = {k: v for k, v in _L3_xattn_all.items() if k in ('ln1_scale', 'ln1_offset', 'wq1', 'bq1', 'wk1', 'bk1', 'wv1', 'bv1', 'wo1', 'bo1', 'bias_k1', 'bias_v1', 'ln2_scale', 'ln2_offset', 'wq2', 'bq2', 'wk2', 'bk2', 'wv2', 'bv2', 'wo2', 'bo2', 'bias_k2', 'bias_v2', 'ln_mlp_scale', 'ln_mlp_offset', 'w_fc1', 'b_fc1', 'w_fc2', 'b_fc2')}
    del _L3_xattn_all
    return {'x': x, 'ctx_2048': ctx_2048, 'mask_Bx1xSxS2_ff0': mask_Bx1xSxS2_ff0, 'mask_BxS2_bf1': mask_BxS2_bf1, 'L0_xattn_Wq': _L0_xattn_in['Wq'], 'L0_xattn_bq': _L0_xattn_in['bq'], 'L0_xattn_Wk': _L0_xattn_in['Wk'], 'L0_xattn_bk': _L0_xattn_in['bk'], 'L0_xattn_Wv': _L0_xattn_in['Wv'], 'L0_xattn_bv': _L0_xattn_in['bv'], 'L0_xattn_Wo': _L0_xattn_in['Wo'], 'L0_xattn_bo': _L0_xattn_in['bo'], 'L0_xattn_gamma': _L0_xattn_in['gamma'], 'L0_xattn_beta': _L0_xattn_in['beta'], 'L1_xattn_Wq': _L1_xattn_in['Wq'], 'L1_xattn_bq': _L1_xattn_in['bq'], 'L1_xattn_Wk': _L1_xattn_in['Wk'], 'L1_xattn_bk': _L1_xattn_in['bk'], 'L1_xattn_Wv': _L1_xattn_in['Wv'], 'L1_xattn_bv': _L1_xattn_in['bv'], 'L1_xattn_Wo': _L1_xattn_in['Wo'], 'L1_xattn_bo': _L1_xattn_in['bo'], 'L1_xattn_gamma': _L1_xattn_in['gamma'], 'L1_xattn_beta': _L1_xattn_in['beta'], 'L2_xattn_Wq': _L2_xattn_in['Wq'], 'L2_xattn_Wk': _L2_xattn_in['Wk'], 'L2_xattn_Wv': _L2_xattn_in['Wv'], 'L2_xattn_Wo': _L2_xattn_in['Wo'], 'L2_xattn_ln_gamma': _L2_xattn_in['ln_gamma'], 'L2_xattn_ln_beta': _L2_xattn_in['ln_beta'], 'L2_xattn_gate': _L2_xattn_in['gate'], 'L3_xattn_ln1_scale': _L3_xattn_in['ln1_scale'], 'L3_xattn_ln1_offset': _L3_xattn_in['ln1_offset'], 'L3_xattn_wq1': _L3_xattn_in['wq1'], 'L3_xattn_bq1': _L3_xattn_in['bq1'], 'L3_xattn_wk1': _L3_xattn_in['wk1'], 'L3_xattn_bk1': _L3_xattn_in['bk1'], 'L3_xattn_wv1': _L3_xattn_in['wv1'], 'L3_xattn_bv1': _L3_xattn_in['bv1'], 'L3_xattn_wo1': _L3_xattn_in['wo1'], 'L3_xattn_bo1': _L3_xattn_in['bo1'], 'L3_xattn_bias_k1': _L3_xattn_in['bias_k1'], 'L3_xattn_bias_v1': _L3_xattn_in['bias_v1'], 'L3_xattn_ln2_scale': _L3_xattn_in['ln2_scale'], 'L3_xattn_ln2_offset': _L3_xattn_in['ln2_offset'], 'L3_xattn_wq2': _L3_xattn_in['wq2'], 'L3_xattn_bq2': _L3_xattn_in['bq2'], 'L3_xattn_wk2': _L3_xattn_in['wk2'], 'L3_xattn_bk2': _L3_xattn_in['bk2'], 'L3_xattn_wv2': _L3_xattn_in['wv2'], 'L3_xattn_bv2': _L3_xattn_in['bv2'], 'L3_xattn_wo2': _L3_xattn_in['wo2'], 'L3_xattn_bo2': _L3_xattn_in['bo2'], 'L3_xattn_bias_k2': _L3_xattn_in['bias_k2'], 'L3_xattn_bias_v2': _L3_xattn_in['bias_v2'], 'L3_xattn_ln_mlp_scale': _L3_xattn_in['ln_mlp_scale'], 'L3_xattn_ln_mlp_offset': _L3_xattn_in['ln_mlp_offset'], 'L3_xattn_w_fc1': _L3_xattn_in['w_fc1'], 'L3_xattn_b_fc1': _L3_xattn_in['b_fc1'], 'L3_xattn_w_fc2': _L3_xattn_in['w_fc2'], 'L3_xattn_b_fc2': _L3_xattn_in['b_fc2']}

def reference(x, ctx_2048, mask_Bx1xSxS2_ff0, mask_BxS2_bf1, L0_xattn_Wq, L0_xattn_bq, L0_xattn_Wk, L0_xattn_bk, L0_xattn_Wv, L0_xattn_bv, L0_xattn_Wo, L0_xattn_bo, L0_xattn_gamma, L0_xattn_beta, L1_xattn_Wq, L1_xattn_bq, L1_xattn_Wk, L1_xattn_bk, L1_xattn_Wv, L1_xattn_bv, L1_xattn_Wo, L1_xattn_bo, L1_xattn_gamma, L1_xattn_beta, L2_xattn_Wq, L2_xattn_Wk, L2_xattn_Wv, L2_xattn_Wo, L2_xattn_ln_gamma, L2_xattn_ln_beta, L2_xattn_gate, L3_xattn_ln1_scale, L3_xattn_ln1_offset, L3_xattn_wq1, L3_xattn_bq1, L3_xattn_wk1, L3_xattn_bk1, L3_xattn_wv1, L3_xattn_bv1, L3_xattn_wo1, L3_xattn_bo1, L3_xattn_bias_k1, L3_xattn_bias_v1, L3_xattn_ln2_scale, L3_xattn_ln2_offset, L3_xattn_wq2, L3_xattn_bq2, L3_xattn_wk2, L3_xattn_bk2, L3_xattn_wv2, L3_xattn_bv2, L3_xattn_wo2, L3_xattn_bo2, L3_xattn_bias_k2, L3_xattn_bias_v2, L3_xattn_ln_mlp_scale, L3_xattn_ln_mlp_offset, L3_xattn_w_fc1, L3_xattn_b_fc1, L3_xattn_w_fc2, L3_xattn_b_fc2):
    import jax
    import jax.numpy as jnp

    def _L0_xattn_ref(hidden_state, encoder_hidden_state, encoder_attention_mask, Wq, bq, Wk, bk, Wv, bv, Wo, bo, gamma, beta):
        import jax, jax.numpy as jnp
        import numpy as np
        H = 512
        NH = 32
        KVH = 8
        HD = H // NH
        GROUPS = NH // KVH
        EPS = 1e-06
        B, L, S = (4, 256, 256)

        def _gqa_forward(hidden_state, encoder_hidden_state, encoder_attention_mask, Wq, bq, Wk, bk, Wv, bv, Wo, bo, gamma, beta):
            b, l, _ = hidden_state.shape
            s = encoder_hidden_state.shape[1]
            q = hidden_state @ Wq + bq
            k = encoder_hidden_state @ Wk + bk
            v = encoder_hidden_state @ Wv + bv
            q = q.reshape(b, l, KVH, GROUPS, HD).transpose(0, 2, 3, 1, 4)
            k = k.reshape(b, s, KVH, HD).transpose(0, 2, 1, 3)
            v = v.reshape(b, s, KVH, HD).transpose(0, 2, 1, 3)
            scale = 1.0 / jnp.sqrt(jnp.asarray(HD, q.dtype))
            scores = jnp.einsum('bkgld,bksd->bkgls', q, k) * scale
            scores = scores + encoder_attention_mask[:, :, None, :, :]
            attn = jax.nn.softmax(scores, axis=-1)
            out = jnp.einsum('bkgls,bksd->bkgld', attn, v)
            out = out.transpose(0, 3, 1, 2, 4).reshape(b, l, H)
            out = out @ Wo + bo
            x = out + hidden_state
            mu = jnp.mean(x, axis=-1, keepdims=True)
            var = jnp.var(x, axis=-1, keepdims=True)
            return (x - mu) * jax.lax.rsqrt(var + EPS) * gamma + beta
        return _gqa_forward(hidden_state, encoder_hidden_state, encoder_attention_mask, Wq, bq, Wk, bk, Wv, bv, Wo, bo, gamma, beta)

    def _L1_xattn_ref(hidden_state, encoder_hidden_state, encoder_attention_mask, Wq, bq, Wk, bk, Wv, bv, Wo, bo, gamma, beta):
        import jax, jax.numpy as jnp
        import numpy as np
        H = 512
        NH = 32
        KVH = 8
        HD = H // NH
        GROUPS = NH // KVH
        EPS = 1e-06
        B, L, S = (4, 256, 256)

        def _gqa_forward(hidden_state, encoder_hidden_state, encoder_attention_mask, Wq, bq, Wk, bk, Wv, bv, Wo, bo, gamma, beta):
            b, l, _ = hidden_state.shape
            s = encoder_hidden_state.shape[1]
            q = hidden_state @ Wq + bq
            k = encoder_hidden_state @ Wk + bk
            v = encoder_hidden_state @ Wv + bv
            q = q.reshape(b, l, KVH, GROUPS, HD).transpose(0, 2, 3, 1, 4)
            k = k.reshape(b, s, KVH, HD).transpose(0, 2, 1, 3)
            v = v.reshape(b, s, KVH, HD).transpose(0, 2, 1, 3)
            scale = 1.0 / jnp.sqrt(jnp.asarray(HD, q.dtype))
            scores = jnp.einsum('bkgld,bksd->bkgls', q, k) * scale
            scores = scores + encoder_attention_mask[:, :, None, :, :]
            attn = jax.nn.softmax(scores, axis=-1)
            out = jnp.einsum('bkgls,bksd->bkgld', attn, v)
            out = out.transpose(0, 3, 1, 2, 4).reshape(b, l, H)
            out = out @ Wo + bo
            x = out + hidden_state
            mu = jnp.mean(x, axis=-1, keepdims=True)
            var = jnp.var(x, axis=-1, keepdims=True)
            return (x - mu) * jax.lax.rsqrt(var + EPS) * gamma + beta
        return _gqa_forward(hidden_state, encoder_hidden_state, encoder_attention_mask, Wq, bq, Wk, bk, Wv, bv, Wo, bo, gamma, beta)

    def _L2_xattn_ref(hidden_states, audio_kv, audio_attention_mask, Wq, Wk, Wv, Wo, ln_gamma, ln_beta, gate):
        import jax, jax.numpy as jnp
        import numpy as np
        HIDDEN = 512
        HEADS = 16
        HEAD_DIM = HIDDEN // HEADS
        LN_EPS = 1e-05
        GATE_INIT = 0.5

        def _layer_norm(x, gamma, beta):
            mu = jnp.mean(x, axis=-1, keepdims=True)
            var = jnp.mean(jnp.square(x - mu), axis=-1, keepdims=True)
            return (x - mu) * jax.lax.rsqrt(var + LN_EPS) * gamma + beta
        B, Tt, D = hidden_states.shape
        Ta = audio_kv.shape[1]
        scale = HEAD_DIM ** (-0.5)
        a = _layer_norm(audio_kv, ln_gamma, ln_beta)
        Q = (hidden_states @ Wq.T).reshape(B, Tt, HEADS, HEAD_DIM).transpose(0, 2, 1, 3)
        K = (a @ Wk.T).reshape(B, Ta, HEADS, HEAD_DIM).transpose(0, 2, 1, 3)
        V = (a @ Wv.T).reshape(B, Ta, HEADS, HEAD_DIM).transpose(0, 2, 1, 3)
        scores = jnp.einsum('bhtd,bhsd->bhts', Q, K) * scale
        mask = audio_attention_mask[:, None, None, :]
        scores = jnp.where(mask, scores, jnp.float32(-jnp.inf))
        attn = jax.nn.softmax(scores, axis=-1)
        out = jnp.einsum('bhts,bhsd->bhtd', attn, V)
        out = out.transpose(0, 2, 1, 3).reshape(B, Tt, D)
        out = out @ Wo.T
        return hidden_states + jnp.tanh(gate) * out

    def _L3_xattn_ref(x, xf_1, xf_2, ln1_scale, ln1_offset, wq1, bq1, wk1, bk1, wv1, bv1, wo1, bo1, bias_k1, bias_v1, ln2_scale, ln2_offset, wq2, bq2, wk2, bk2, wv2, bv2, wo2, bo2, bias_k2, bias_v2, ln_mlp_scale, ln_mlp_offset, w_fc1, b_fc1, w_fc2, b_fc2):
        import jax, jax.numpy as jnp
        import numpy as np
        B, Q, S1, S2 = (4, 64, 512, 512)
        D, H, K, F = (512, 16, 128, 2048)
        LN_EPS = 1e-05

        def _layer_norm(x, scale, offset):
            mu = jnp.mean(x, axis=-1, keepdims=True)
            var = jnp.var(x, axis=-1, keepdims=True)
            return (x - mu) * jax.lax.rsqrt(var + LN_EPS) * scale + offset

        def _cross_attention(q_in, kv_in, wq, bq, wk, bk, wv, bv, wo, bo, bias_k, bias_v):
            b, q_len, _ = q_in.shape
            t = kv_in.shape[1]
            qh = (q_in @ wq + bq).reshape(b, q_len, H, K)
            kh = (kv_in @ wk + bk).reshape(b, t, H, K)
            vh = (kv_in @ wv + bv).reshape(b, t, H, K)
            kh = jnp.concatenate([kh, jnp.broadcast_to(bias_k, (b, 1, H, K))], axis=1)
            vh = jnp.concatenate([vh, jnp.broadcast_to(bias_v, (b, 1, H, K))], axis=1)
            scale = jnp.sqrt(jnp.asarray(K, q_in.dtype))
            logits = jnp.einsum('bqhk,bthk->bhqt', qh, kh) / scale
            weights = jax.nn.softmax(logits, axis=-1)
            ctx = jnp.einsum('bhqt,bthk->bqhk', weights, vh).reshape(b, q_len, H * K)
            return ctx @ wo + bo

        def _forward(x, xf_1, xf_2, ln1_scale, ln1_offset, wq1, bq1, wk1, bk1, wv1, bv1, wo1, bo1, bias_k1, bias_v1, ln2_scale, ln2_offset, wq2, bq2, wk2, bk2, wv2, bv2, wo2, bo2, bias_k2, bias_v2, ln_mlp_scale, ln_mlp_offset, w_fc1, b_fc1, w_fc2, b_fc2):
            res = x
            h = _layer_norm(x, ln1_scale, ln1_offset)
            x = res + _cross_attention(h, xf_1, wq1, bq1, wk1, bk1, wv1, bv1, wo1, bo1, bias_k1, bias_v1)
            res = x
            h = _layer_norm(x, ln2_scale, ln2_offset)
            x = res + _cross_attention(h, xf_2, wq2, bq2, wk2, bk2, wv2, bv2, wo2, bo2, bias_k2, bias_v2)
            h = _layer_norm(x, ln_mlp_scale, ln_mlp_offset)
            h = jax.nn.gelu(h @ w_fc1 + b_fc1, approximate=False) @ w_fc2 + b_fc2
            return x + h
        return _forward(x, xf_1, xf_2, ln1_scale, ln1_offset, wq1, bq1, wk1, bk1, wv1, bv1, wo1, bo1, bias_k1, bias_v1, ln2_scale, ln2_offset, wq2, bq2, wk2, bk2, wv2, bv2, wo2, bo2, bias_k2, bias_v2, ln_mlp_scale, ln_mlp_offset, w_fc1, b_fc1, w_fc2, b_fc2)
    x = _L0_xattn_ref(x, ctx_2048, mask_Bx1xSxS2_ff0, L0_xattn_Wq, L0_xattn_bq, L0_xattn_Wk, L0_xattn_bk, L0_xattn_Wv, L0_xattn_bv, L0_xattn_Wo, L0_xattn_bo, L0_xattn_gamma, L0_xattn_beta)
    x = _L1_xattn_ref(x, ctx_2048, mask_Bx1xSxS2_ff0, L1_xattn_Wq, L1_xattn_bq, L1_xattn_Wk, L1_xattn_bk, L1_xattn_Wv, L1_xattn_bv, L1_xattn_Wo, L1_xattn_bo, L1_xattn_gamma, L1_xattn_beta)
    x = _L2_xattn_ref(x, ctx_2048, mask_BxS2_bf1, L2_xattn_Wq, L2_xattn_Wk, L2_xattn_Wv, L2_xattn_Wo, L2_xattn_ln_gamma, L2_xattn_ln_beta, L2_xattn_gate)
    x = _L3_xattn_ref(x, ctx_2048, ctx_2048, L3_xattn_ln1_scale, L3_xattn_ln1_offset, L3_xattn_wq1, L3_xattn_bq1, L3_xattn_wk1, L3_xattn_bk1, L3_xattn_wv1, L3_xattn_bv1, L3_xattn_wo1, L3_xattn_bo1, L3_xattn_bias_k1, L3_xattn_bias_v1, L3_xattn_ln2_scale, L3_xattn_ln2_offset, L3_xattn_wq2, L3_xattn_bq2, L3_xattn_wk2, L3_xattn_bk2, L3_xattn_wv2, L3_xattn_bv2, L3_xattn_wo2, L3_xattn_bo2, L3_xattn_bias_k2, L3_xattn_bias_v2, L3_xattn_ln_mlp_scale, L3_xattn_ln_mlp_offset, L3_xattn_w_fc1, L3_xattn_b_fc1, L3_xattn_w_fc2, L3_xattn_b_fc2)
    return x

_drawn_inputs = setup_inputs


def setup_inputs(seed=0):
    import zlib

    import numpy as np

    out = dict(_drawn_inputs(seed))
    spreads = {'L0_xattn_bq': (0.0, 0.8),
     'L0_xattn_bk': (0.0, 2.0),
     'L0_xattn_bv': (0.0, 0.1),
     'L0_xattn_bo': (0.0, 0.1),
     'L0_xattn_gamma': (1.0, 0.2),
     'L0_xattn_beta': (0.0, 0.1),
     'L1_xattn_bq': (0.0, 0.8),
     'L1_xattn_bk': (0.0, 2.0),
     'L1_xattn_bv': (0.0, 0.1),
     'L1_xattn_bo': (0.0, 0.1),
     'L1_xattn_gamma': (1.0, 0.2),
     'L1_xattn_beta': (0.0, 0.1),
     'L2_xattn_ln_gamma': (1.0, 0.6),
     'L2_xattn_ln_beta': (0.0, 0.8),
     'L3_xattn_ln1_scale': (1.0, 0.6),
     'L3_xattn_ln1_offset': (0.0, 0.8),
     'L3_xattn_bq1': (0.0, 0.8),
     'L3_xattn_bk1': (0.0, 2.0),
     'L3_xattn_bv1': (0.0, 0.1),
     'L3_xattn_bo1': (0.0, 0.1),
     'L3_xattn_ln2_scale': (1.0, 0.6),
     'L3_xattn_ln2_offset': (0.0, 0.8),
     'L3_xattn_bq2': (0.0, 0.8),
     'L3_xattn_bk2': (0.0, 2.0),
     'L3_xattn_bv2': (0.0, 0.1),
     'L3_xattn_bo2': (0.0, 0.1),
     'L3_xattn_ln_mlp_scale': (1.0, 0.2),
     'L3_xattn_ln_mlp_offset': (0.0, 0.379),
     'L3_xattn_b_fc1': (0.0, 0.1),
     'L3_xattn_b_fc2': (0.0, 0.1)}
    factors = {'L0_xattn_Wq': 8.0,
     'L0_xattn_Wk': 7.991,
     'L1_xattn_Wq': 8.0,
     'L1_xattn_Wk': 7.878,
     'L2_xattn_Wq': 8.0,
     'L2_xattn_Wk': 8.0,
     'L3_xattn_wq1': 3.985,
     'L3_xattn_wk1': 3.902,
     'L3_xattn_bias_k1': 64.0,
     'L3_xattn_bias_v1': 64.0,
     'L3_xattn_wq2': 3.968,
     'L3_xattn_wk2': 3.89,
     'L3_xattn_bias_k2': 64.0,
     'L3_xattn_bias_v2': 64.0}
    for name, (base, spread) in spreads.items():
        noise = np.random.default_rng([zlib.crc32(name.encode()), seed]).standard_normal(out[name].shape)
        drawn = base * np.exp(spread * noise) if base else spread * noise
        out[name] = jnp.asarray(drawn.astype(out[name].dtype))
    for name, factor in factors.items():
        out[name] = (out[name] * factor).astype(out[name].dtype)
    return out
```

```python
from contextlib import ExitStack

import concourse.bass as bass
from concourse import mybir

F32 = mybir.dt.float32
F32R = mybir.dt.float32r
U8 = mybir.dt.uint8
ALU = mybir.AluOpType
ACT = mybir.ActivationFunctionType
AX = mybir.AxisListType

P = 128
B, L, D, S = 8, 112, 512, 375
DC = D // P
KEYS = S + 1
ROWS = [P, P, S - 2 * P]
F = 2048
FT = F // P
FLT_MAX = 3.4e38


class Layer:

    def __init__(self, name, groups, qt, kt, vw, dh, heads, keys, scale, links, masked=False):
        self.name, self.groups, self.qt, self.kt, self.vw, self.dh = name, groups, qt, kt, vw, dh
        self.heads, self.keys, self.scale, self.masked = heads, keys, scale, masked
        self.gqa, self.last = name in ("L0", "L1"), name.startswith("L3")
        self.quads = len(heads) // 4
        self.chunks = [(0, P), (P, P), (2 * P, keys - 2 * P)]
        self.wq_parts = 8 if self.gqa else 1
        self.per = dict(
            q_ready=qt // 4, k_ready=kt, v_ready=3, s_ready=len(heads), pt_ready=3 * self.quads,
            o_ready=1, ot_ready=1, out_ready=1,
            q_taken=qt // 4, k_taken=kt, v_taken=3, max_ready=len(heads), exp_done=len(heads),
            pt_first=self.quads, pt_rest=2 * self.quads, o_taken=1, ot_hi=1, ot_lo=1, x_done=1,
            ctx_split=2, ctx_landed=16, mask_landed=16 if masked else 0,
            mask_made=1 if masked and not self.gqa else 0, link=links)


def gqa_heads():
    out = []
    for t in range(8):
        for j in range(4):
            kv = 2 * j + t // 4
            n = 4 * kv + t % 4
            out.append(dict(q=t, k=0, row=32 * j, rows=32, v=16 * kv, o=16 * n, n=n))
    return out


LAYERS = [
    Layer("L0", 1, 8, 1, P, 16, gqa_heads(), S, 0.25, 7, True),
    Layer("L1", 1, 8, 1, P, 16, gqa_heads(), S, 0.25, 7, True),
    Layer("L2", 1, 4, 4, D, 32,
          [dict(q=h // 4, k=h // 4, row=32 * (h % 4), rows=32, v=32 * h, o=32 * h, n=h) for h in range(16)],
          S, 32 ** -0.5, 2, True),
] + [
    Layer(f"L3_{i}", 4, 4, 4, D, P, [dict(q=h, k=h, row=0, rows=P, v=P * h, o=P * h, n=h) for h in range(4)],
          KEYS, P ** -0.5, 1) for i in (1, 2)]

NO_START = ("q_ready", "k_ready", "v_ready", "s_ready", "pt_ready", "o_ready", "ot_ready", "out_ready",
            "ctx_landed", "mask_landed")


def at(i, name, step, count):
    before = sum(ly.per[name] * ly.groups * B for ly in LAYERS[:i]) + (name not in NO_START)
    return step * LAYERS[i].per[name] + (before + count)


def weights_at(i, group, count):
    before = sum((6 + ly.wq_parts) * ly.groups for ly in LAYERS[:i]) + 1
    return group * (6 + LAYERS[i].wq_parts) + (before + count)


def rows_of(vector, n=P):
    return vector.rearrange("(o d) -> o d", o=1).broadcast_to([n, D])


def build(nc, a, out):
    scratch_ctx = nc.dram_tensor("ctx_transposed", [B, P, DC * KEYS], F32, kind="Internal").ap()
    scratch_norm = nc.dram_tensor("ctx_norm_transposed", [B, P, DC * KEYS], F32, kind="Internal").ap()
    scratch_w = nc.dram_tensor("gated_weights_transposed", [4, D, D], F32, kind="Internal").ap()
    with ExitStack() as ctx:
        X = ctx.enter_context(nc.sbuf_tensor("X", [L, B, D], F32))
        ident = ctx.enter_context(nc.sbuf_tensor("ident", [P, P], F32))
        minus_half = ctx.enter_context(nc.sbuf_tensor("minus_half", [P, 3], F32))
        prepare_context(nc, a, scratch_ctx, scratch_norm, scratch_w, ident, minus_half)
        attend(nc, a, scratch_ctx, scratch_norm, scratch_w, X, ident, minus_half)
        feed_forward(nc, a, X, ident, minus_half, out)


def prepare_context(nc, a, scratch_ctx, scratch_norm, scratch_w, ident, minus_half):
    with ExitStack() as ctx:
        def sb(name, shape, dt=F32):
            return ctx.enter_context(nc.sbuf_tensor(name, shape, dt))

        def sem(name):
            return ctx.enter_context(nc.semaphore(name))

        nat = sb("nat", [P, 2, 3, D])
        normed = sb("normed", [P, 3, D])
        ctx_t = sb("ctx_t", [P, DC, KEYS])
        norm_t = sb("norm_t", [P, DC, KEYS])
        gamma = sb("ctx_gamma", [P, D])
        beta = sb("ctx_beta", [P, D])
        stats = sb("ctx_stats", [P, 3, 6])
        moments = sb("ctx_moments", [P, 3, 2])
        rstd = sb("ctx_rstd", [P, 3])
        w_nat = sb("w_nat", [P, 4, DC, D])
        w_t = sb("w_t", [P, 4, DC, D])
        bank = [ctx.enter_context(nc.psum_tensor(f"ctx_bank{i}", [P, 512], F32)) for i in range(8)]
        nat_landed = [sem(f"nat{half}_landed") for half in range(2)]
        vectors_landed, w_landed = sem("ctx_vectors_landed"), sem("w_landed")
        var_ready, rstd_ready = sem("ctx_var_ready"), sem("ctx_rstd_ready")
        cleared, ident_made, link = sem("cleared"), sem("ident_made"), sem("ctx_link")
        normed_ready, ctx_turned, norm_turned = sem("normed_ready"), sem("ctx_turned"), sem("norm_turned")
        ctx_copied, norm_copied = sem("ctx_copied"), sem("norm_copied")
        ctx_stored, norm_stored, w_stored = sem("ctx_stored"), sem("norm_stored"), sem("w_stored")
        w_turned, w_copied = sem("w_turned"), sem("w_copied")

        settled = sem("head_settled")

        def settle(eng):
            eng.sem_inc(settled, 1)

        LINKS = 10
        block = ctx.enter_context(nc.Block())

        @block.sync
        def _(sp):
            sp.sem_inc(ctx_stored, 16)
            sp.sem_inc(norm_stored, 16)
            sp.dma_start(gamma[:], rows_of(a["L2_xattn_ln_gamma"])).then_inc(vectors_landed, 16)
            sp.dma_start(beta[:], rows_of(a["L2_xattn_ln_beta"])).then_inc(vectors_landed, 16)
            sp.wait_ge(cleared, 1)

            def load(b, half):
                c = a["ctx_2048"]
                sp.dma_start(nat[:, half, 0:2, :], c[b, 0:2 * P, :].rearrange("(t p) d -> p t d", p=P))\
                  .then_inc(nat_landed[half], 16)
                sp.dma_start(nat[0:ROWS[2], half, 2, :], c[b, 2 * P:S, :]).then_inc(nat_landed[half], 16)

            def store(b):
                sp.wait_ge(ctx_copied, 4 * b + 5)
                sp.dma_start(scratch_ctx[b], ctx_t[:].rearrange("p c k -> p (c k)")).then_inc(ctx_stored, 16)
                sp.wait_ge(norm_copied, 4 * b + 5)
                sp.dma_start(scratch_norm[b], norm_t[:].rearrange("p c k -> p (c k)")).then_inc(norm_stored, 16)

            load(0, 0)
            for i, n in enumerate(("Wq", "Wk", "Wv", "Wo")):
                sp.dma_start(w_nat[:, i, :, :], a[f"L2_xattn_{n}"].rearrange("(t p) d -> p t d", p=P))\
                  .then_inc(w_landed, 16)
            load(1, 1)
            with sp.Fori(0, B // 2 - 1) as pair:
                for half in range(2):
                    store(pair * 2 + half)
                    load(pair * 2 + half + 2, half)
            store(B - 2)
            store(B - 1)
            for i in range(4):
                sp.wait_ge(w_copied, 4 * (i + 1))
                sp.dma_start(scratch_w[i].rearrange("(c p) n -> p c n", p=P), w_t[:, i, :, :])\
                  .then_inc(w_stored, 16)
            sp.wait_ge(ctx_stored, 16 * (1 + B))
            sp.wait_ge(norm_stored, 16 * (1 + B))
            sp.wait_ge(w_stored, 16 * 4)

        @block.gpsimd
        def _(pool):
            pool.memset(ident[:], 0.0).then_inc(ident_made, 1)
            pool.wait_ge(ident_made, 1)
            pool.affine_select(out=ident[:], in_=ident[:], compare_op=ALU.not_equal, fill=1.0, base=0,
                               pattern=[[-1, P]], channel_multiplier=1).then_inc(ident_made, 1)
            pool.memset(minus_half[:], -0.5).then_inc(ident_made, 1)
            pool.wait_ge(ident_made, 3)
            with pool.Fori(0, B) as b:
                pool.wait_ge(var_ready, b + 1)
                pool.tensor_tensor(rstd[:], rstd[:], minus_half[:], ALU.pow).then_inc(rstd_ready, 1)

        @block.vector
        def _(vec):
            vec.sem_inc(norm_copied, 1)
            vec.memset(nat[:, :, 2, :], 0.0).then_inc(cleared, 1)
            vec.memset(ctx_t[:, :, S:KEYS], 0.0).then_inc(cleared, 1)
            vec.memset(norm_t[:, :, S:KEYS], 0.0).then_inc(cleared, 1)
            vec.wait_ge(vectors_landed, 32)
            with vec.Fori(0, B // 2) as pair:
                for half in range(2):
                    b = pair * 2 + half
                    x = nat[:, half, :, :]
                    vec.wait_ge(nat_landed[half], 32 * pair + 32)
                    for t in range(3):
                        vec.bn_stats(stats[:, t, :], x[:, t, :]).then_inc(link, 1)
                    vec.wait_ge(link, LINKS * b + 3)
                    settle(vec)
                    for t in range(3):
                        vec.bn_aggr(moments[:, t, :], stats[:, t, :]).then_inc(link, 1)
                    vec.wait_ge(link, LINKS * b + 6)
                    vec.tensor_scalar(rstd[:], moments[:, :, 1], 1e-5, None, ALU.add).then_inc(var_ready, 1)
                    vec.wait_ge(rstd_ready, b + 1)
                    if half == 1:
                        vec.wait_ge(norm_turned, 4 * b)
                    else:
                        vec.wait_ge(norm_copied, 4 * b + 1)
                    for t in range(3):
                        vec.tensor_scalar(normed[:, t, :], x[:, t, :], moments[:, t, 0:1], rstd[:, t:t + 1],
                                          ALU.subtract, ALU.mult).then_inc(link, 1)
                    vec.wait_ge(link, LINKS * b + 9)
                    vec.tensor_tensor(normed[:], normed[:], gamma[:].unsqueeze(1).broadcast_to([P, 3, D]), ALU.mult)\
                       .then_inc(link, 1)
                    vec.wait_ge(link, LINKS * b + 10)
                    vec.tensor_tensor(normed[:], normed[:], beta[:].unsqueeze(1).broadcast_to([P, 3, D]), ALU.add)\
                       .then_inc(normed_ready, 1)
                    vec.wait_ge(norm_stored, 16 * b + 16)
                    for c in range(DC):
                        vec.wait_ge(norm_turned, 4 * b + c + 1)
                        vec.tensor_copy(norm_t[:, c, 0:S], bank[4 + c][:, 0:S]).then_inc(norm_copied, 1)

        @block.scalar
        def _(act):
            act.sem_inc(ctx_copied, 1)
            act.wait_ge(cleared, 3)
            with act.Fori(0, B) as b:
                act.wait_ge(ctx_stored, 16 * b + 16)
                for c in range(DC):
                    act.wait_ge(ctx_turned, 4 * b + c + 1)
                    act.activation(ctx_t[:, c, 0:S], bank[c][:, 0:S], ACT.Copy).then_inc(ctx_copied, 1)
            for n in range(16):
                act.wait_ge(w_turned, n + 1)
                act.activation(w_t[:, n // 4, n % 4, :], bank[n % 8][:, :], ACT.Copy).then_inc(w_copied, 1)

        @block.tensor
        def _(pe):
            pe.wait_ge(ident_made, 2)
            with pe.Fori(0, B // 2) as pair:
                for half in range(2):
                    b = pair * 2 + half
                    pe.wait_ge(nat_landed[half], 32 * pair + 32)
                    pe.wait_ge(ctx_copied, 4 * b + 1)
                    for c in range(DC):
                        for t in range(3):
                            last = pe.transpose(bank[c][:, t * P:t * P + ROWS[t]],
                                                nat[0:ROWS[t], half, t, c * P:(c + 1) * P],
                                                ident[0:ROWS[t], 0:ROWS[t]])
                        last.then_inc(ctx_turned, 1)
                    pe.wait_ge(normed_ready, b + 1)
                    pe.wait_ge(norm_copied, 4 * b + 1)
                    for c in range(DC):
                        for t in range(3):
                            last = pe.transpose(bank[4 + c][:, t * P:t * P + ROWS[t]],
                                                normed[0:ROWS[t], t, c * P:(c + 1) * P],
                                                ident[0:ROWS[t], 0:ROWS[t]])
                        last.then_inc(norm_turned, 1)
            pe.wait_ge(ctx_copied, 4 * B + 1)
            pe.wait_ge(norm_copied, 4 * B + 1)
            for n in range(16):
                i, c = n // 4, n % 4
                if c == 0:
                    pe.wait_ge(w_landed, 64)
                if n >= 8:
                    pe.wait_ge(w_copied, n - 7)
                for t in range(DC):
                    last = pe.transpose(bank[n % 8][:, t * P:(t + 1) * P], w_nat[:, i, t, c * P:(c + 1) * P], ident[:])
                last.then_inc(w_turned, 1)


PREP_LINKS = 5




def norm_rows(vec, chain, stats, x, y, eps, var_ready, rstd_ready, value, settle):
    chain(vec.bn_stats(stats[:, 0:6], x), settle)
    chain(vec.bn_aggr(stats[:, 6:8], stats[:, 0:6]))
    vec.tensor_scalar(stats[:, 8:9], stats[:, 7:8], eps, None, ALU.add).then_inc(var_ready, 1)
    vec.wait_ge(rstd_ready, value)
    chain(vec.tensor_scalar(y, x, stats[:, 6:7], stats[:, 8:9], ALU.subtract, ALU.mult))


def attend(nc, a, scratch_ctx, scratch_norm, scratch_w, X, ident, minus_half):
    with ExitStack() as ctx:
        def sb(name, shape, dt=F32):
            return ctx.enter_context(nc.sbuf_tensor(name, shape, dt))

        def psum(name):
            return ctx.enter_context(nc.psum_tensor(name, [P, 512], F32))

        def sem(name):
            return ctx.enter_context(nc.semaphore(name))

        h_rows = sb("h_rows", [L, 2, D])
        h_t = sb("h_t", [P, B, DC, L])
        ctx_raw = sb("ctx_raw", [P, DC, KEYS])
        ctx_h, ctx_l = (sb(n, [P, DC, KEYS], F32R) for n in ("ctx_h", "ctx_l"))
        stage = [sb(f"stage{i}", [P, DC, D]) for i in range(2)]
        wq = sb("wq", [P, DC, 2 * D])
        wk_h, wk_l, wv_h, wv_l, wo_h, wo_l = (
            sb(n, [P, DC, D], F32R) for n in ("wk_h", "wk_l", "wv_h", "wv_l", "wo_h", "wo_l"))
        q_t = sb("q_t", [P, 8, L])
        k_t = sb("k_t", [P, 4, KEYS])
        v = sb("v", [P, 3, D])
        masked = sb("masked", [L, 2, 4, S])
        probs = sb("probs", [L, 2, 4, KEYS])
        probs_t = sb("probs_t", [P, 2, 3, 4 * L])
        o = sb("o", [L, D])
        o_h, o_l = (sb(n, [P, DC, L], F32R) for n in ("o_h", "o_l"))
        y = sb("y", [L, D])
        bv, bo, gamma, beta = (sb(n, [P, D]) for n in ("bv", "bo", "gamma", "beta"))
        bq = sb("bq", [P, 8])
        bk = sb("bk", [P, 4])
        mask_u8 = sb("mask_u8", [L, S], U8)
        mask_f = sb("mask_f", [L, S])
        mask = sb("mask", [L, S])
        neg_max = sb("neg_max", [L, 32])
        row_sum = sb("row_sum", [L, 32])
        inv_sum = sb("inv_sum", [L, 32])
        stats = sb("stats", [L, 9])
        gate = sb("gate", [L, 1])
        tanh_gate = sb("tanh_gate", [L, 1])

        A = [psum(f"A{i}") for i in range(2)]
        Sb = [psum(f"S{i}") for i in range(3)]
        T = [psum(f"T{i}") for i in range(2)]
        O = psum("O")

        s = {n: sem(n) for n in LAYERS[0].per}
        weights_split, h_made, h_turned, h_copied = (
            sem(n) for n in ("weights_split", "h_made", "h_turned", "h_copied"))
        var_ready, rstd_ready = sem("var_ready"), sem("rstd_ready")
        NORMED = {"L0": 0, "L1": B, "L3_1": 2 * B, "L3_2": 3 * B}
        staged = [sem("stage0_landed"), sem("stage1_landed")]
        x_landed, gate_landed, gate_done, bq_cleared = (
            sem(n) for n in ("x_landed", "gate_landed", "gate_done", "bq_cleared"))
        vectors_landed, norm_landed, prep = sem("vectors_landed"), sem("norm_landed"), sem("prep_link")

        VECTORS = {"L0": 10, "L1": 10, "L2": 0, "L3_1": 5, "L3_2": 5}
        NORMS = {"L0": 3, "L1": 3, "L2": 0, "L3_1": 3, "L3_2": 3}

        def vectors_at(i, g):
            before = sum(VECTORS[ly.name] * ly.groups for ly in LAYERS[:i])
            return g * (16 * VECTORS[LAYERS[i].name]) + 16 * (before + VECTORS[LAYERS[i].name])

        def norms_at(i):
            return 16 * sum(NORMS[ly.name] for ly in LAYERS[:i + 1])

        def steps(eng, ly, body):
            if ly.groups == 1:
                with eng.Fori(0, B) as b:
                    body(0, b, b)
            else:
                with eng.Fori(0, ly.groups) as g:
                    with eng.Fori(0, B) as b:
                        body(g, b, g * B + b)

        def groups(eng, ly, body):
            if ly.groups == 1:
                body(0)
            else:
                with eng.Fori(0, ly.groups) as g:
                    body(g)

        settled = sem("attend_settled")

        def settle(eng):
            eng.sem_inc(settled, 1)

        block = ctx.enter_context(nc.Block())

        @block.sync
        def _(sp):
            sp.dma_start(X[:], a["x"].rearrange("b l d -> l b d")).then_inc(x_landed, 16)
            sp.dma_start(gate[:], a["L2_xattn_gate"].rearrange("(o d) -> o d", o=1).broadcast_to([L, 1]))\
              .then_inc(gate_landed, 16)
            sp.wait_ge(bq_cleared, 1)
            for i, ly in enumerate(LAYERS):
                pre = "L3_xattn_" if ly.last else ly.name + "_xattn_"
                post = ly.name[-1] if ly.last else ""

                def step_loads(b, n, i=i, ly=ly):
                    sp.wait_ge(s["ctx_split"], at(i, "ctx_split", n, 0))
                    settle(sp)
                    src = (scratch_norm if ly.name == "L2" else scratch_ctx)[b]
                    sp.dma_start(ctx_raw[:].rearrange("p c k -> p (c k)"), src).then_inc(s["ctx_landed"], 16)
                    if ly.gqa:
                        sp.wait_ge(s["max_ready"], at(i, "max_ready", n, 0))
                        settle(sp)
                        sp.dma_start(mask[:], a["mask_Bx1xSxS2_ff0"][b, 0]).then_inc(s["mask_landed"], 16)
                    elif ly.masked:
                        sp.wait_ge(s["mask_made"], at(i, "mask_made", n, 0))
                        settle(sp)
                        sp.dma_start(mask_u8[:], a["mask_BxS2_bf1"][bass.ds(b, 1), :].broadcast_to([L, S]))\
                          .then_inc(s["mask_landed"], 16)

                sp.wait_ge(s["x_done"], at(i, "x_done", 0, 0))
                sp.wait_ge(s["link"], at(i, "link", 0, 0))
                if ly.last:
                    sp.wait_ge(h_made, 1 + B * i)
                for dst, name in ([(bo, "bo" + post)] + (
                        [(gamma, f"ln{post}_scale"), (beta, f"ln{post}_offset")] if ly.last
                        else [(gamma, "gamma"), (beta, "beta")]) if ly.name != "L2" else []):
                    sp.dma_start(dst[:], rows_of(a[pre + name])).then_inc(norm_landed, 16)

                def group(g, i=i, ly=ly, pre=pre, post=post):
                    n = g * B
                    cols = bass.ds(g * D, D)
                    if ly.name == "L2":
                        w = [scratch_w[j].rearrange("(c p) n -> p c n", p=P) for j in range(4)]
                    elif ly.last:
                        w = [a[f"{pre}w{x}{post}"].rearrange("(c p) n -> p c n", p=P)[:, :, cols] for x in "qkv"]
                        w.append(a[f"{pre}wo{post}"].rearrange("(g c p) n -> g p c n", g=4, p=P)[g])
                    else:
                        w = [a[f"{pre}W{x}"].rearrange("(c p) n -> p c n", p=P) for x in "qkvo"]
                    kw = P if ly.gqa else D
                    sp.wait_ge(weights_split, weights_at(i, g, 0))
                    settle(sp)
                    sp.dma_start(stage[0][:, :, 0:kw], w[1]).then_inc(staged[0], 16)
                    sp.dma_start(stage[1][:, :, 0:ly.vw], w[2]).then_inc(staged[1], 16)
                    step_loads(0, n)
                    if ly.gqa:
                        sp.wait_ge(s["q_taken"], at(i, "q_taken", n, 0))
                        settle(sp)
                        src = a[pre + "bq"].rearrange("(kv g d) -> kv d g", g=4, d=16)
                        for kv in range(8):
                            j, p = kv // 2, kv % 2
                            sp.dma_start(bq[32 * j + 16 * p:32 * j + 16 * p + 16, 4 * p:4 * p + 4], src[kv],
                                         allow_slow_non_contiguous=True).then_inc(vectors_landed, 16)
                        sp.wait_ge(s["k_taken"], at(i, "k_taken", n, 0))
                        settle(sp)
                        sp.dma_start(bk[:, 0:1], a[pre + "bk"].rearrange("(p o) -> p o", o=1),
                                     allow_slow_non_contiguous=True)\
                          .then_inc(vectors_landed, 16)
                        sp.wait_ge(s["v_taken"], at(i, "v_taken", n, 0))
                        settle(sp)
                        sp.dma_start(bv[:, 0:P], a[pre + "bv"].rearrange("(o d) -> o d", o=1).broadcast_to([P, P]))\
                          .then_inc(vectors_landed, 16)
                    elif ly.last:
                        def part(name):
                            return a[pre + name + post].rearrange("(g c p) -> g p c", g=4, p=P)[g]
                        sp.wait_ge(s["q_taken"], at(i, "q_taken", n, 0))
                        settle(sp)
                        sp.dma_start(bq[:, 0:4], part("bq"), allow_slow_non_contiguous=True).then_inc(vectors_landed, 16)
                        sp.wait_ge(s["k_taken"], at(i, "k_taken", n, 0))
                        settle(sp)
                        sp.dma_start(bk[:], part("bk"), allow_slow_non_contiguous=True).then_inc(vectors_landed, 16)
                        sp.wait_ge(s["v_taken"], at(i, "v_taken", n, 0))
                        settle(sp)
                        sp.dma_start(bv[:], a[f"{pre}bv{post}"].rearrange("(g o d) -> g o d", g=4, o=1)[g]
                                     .broadcast_to([P, D])).then_inc(vectors_landed, 16)
                        sp.wait_ge(s["s_ready"], at(i, "s_ready", n, 0))
                        settle(sp)
                        sp.dma_start(k_t[:, :, S:KEYS],
                                     a[f"{pre}bias_k{post}"].rearrange("x y (g c) (p o) -> (x y g) p c o", g=4, o=1)[g],
                                     allow_slow_non_contiguous=True)\
                          .then_inc(vectors_landed, 16)
                        sp.wait_ge(s["o_ready"], at(i, "o_ready", n, 0))
                        settle(sp)
                        sp.dma_start(v[ROWS[2]:ROWS[2] + 1, 2, :],
                                     a[f"{pre}bias_v{post}"].rearrange("x y (g c) p -> (x y g) (c p)", g=4)[
                                         bass.ds(g, 1), :])\
                          .then_inc(vectors_landed, 16)
                    sp.wait_ge(weights_split, weights_at(i, g, 2))
                    settle(sp)
                    sp.dma_start(stage[0][:], w[0]).then_inc(staged[0], 16)
                    sp.wait_ge(weights_split, weights_at(i, g, 4))
                    settle(sp)
                    sp.dma_start(stage[1][:], w[3]).then_inc(staged[1], 16)
                    with sp.Fori(1, B) as b:
                        step_loads(b, n + b)

                groups(sp, ly, group)

        @block.gpsimd
        def _(pool):
            pool.sem_inc(s["ctx_split"], 1)
            pool.sem_inc(weights_split, 1)
            pool.memset(bq[:], 0.0).then_inc(bq_cleared, 1)
            pool.memset(wq[:], 0.0).then_inc(bq_cleared, 1)
            pool.wait_ge(bq_cleared, 2)
            staged_before = [0, 0]
            for i, ly in enumerate(LAYERS):

                def split(hi, lo, raw, done, value):
                    pool.tensor_copy(hi, raw).then_inc(done, 1)
                    pool.wait_ge(done, value)
                    pool.tensor_tensor(lo, raw, hi, ALU.subtract).then_inc(done, 1)

                def split_context(n, i=i):
                    pool.wait_ge(s["ctx_landed"], at(i, "ctx_landed", n, 16))
                    if not isinstance(n, int) or at(i, "v_ready", n, 0) > 0:
                        pool.wait_ge(s["v_ready"], at(i, "v_ready", n, 0))
                    settle(pool)
                    split(ctx_h[:], ctx_l[:], ctx_raw[:], s["ctx_split"], at(i, "ctx_split", n, 1))

                def power(b, ly=ly):
                    pool.wait_ge(var_ready, b + (NORMED[ly.name] + 1))
                    pool.tensor_tensor(stats[:, 8:9], stats[:, 8:9], minus_half[0:L, 0:1], ALU.pow)\
                        .then_inc(rstd_ready, 1)

                if ly.last:
                    with pool.Fori(0, B) as b:
                        power(b)

                def group(g, i=i, ly=ly, base=staged_before[0]):
                    n = g * B
                    kw = P if ly.gqa else D

                    def used(name):
                        if i > 0:
                            pool.wait_ge(s[name], at(i, name, n, 0))

                    pool.wait_ge(staged[0], g * 32 + base + 16)
                    used("k_ready")
                    settle(pool)
                    split(wk_h[:, :, 0:kw], wk_l[:, :, 0:kw], stage[0][:, :, 0:kw], weights_split, weights_at(i, g, 1))
                    pool.wait_ge(staged[1], g * 32 + base + 16)
                    used("v_ready")
                    settle(pool)
                    split(wv_h[:, :, 0:ly.vw], wv_l[:, :, 0:ly.vw], stage[1][:, :, 0:ly.vw], weights_split,
                          weights_at(i, g, 3))
                    split_context(n)
                    pool.wait_ge(staged[0], g * 32 + base + 32)
                    used("q_ready")
                    settle(pool)
                    if ly.gqa:
                        for t in range(8):
                            p, gg = t // 4, t % 4
                            dst = wq[:, :, t * P:(t + 1) * P].rearrange("c k (j p d) -> c k j p d", j=4, p=2)[:, :, :, p, :]
                            src = stage[0][:].rearrange("c k (j p g d) -> c k j p g d", j=4, p=2, g=4)[:, :, :, p, gg, :]
                            pool.tensor_copy(dst, src).then_inc(weights_split, 1)
                    else:
                        pool.tensor_copy(wq[:, :, 0:D], stage[0][:]).then_inc(weights_split, 1)
                    pool.wait_ge(staged[1], g * 32 + base + 32)
                    used("out_ready")
                    settle(pool)
                    split(wo_h[:], wo_l[:], stage[1][:], weights_split, weights_at(i, g, 5 + ly.wq_parts))
                    with pool.Fori(1, B) as b:
                        split_context(n + b)
                        if ly.gqa:
                            power(b - 1)
                    if ly.gqa:
                        power(B - 1)

                groups(pool, ly, group)
                staged_before[0] += 32 * ly.groups

        @block.scalar
        def _(act):
            for name in ("k_taken", "exp_done", "pt_first", "ot_hi"):
                act.sem_inc(s[name], 1)
            act.sem_inc(h_copied, 2)
            act.wait_ge(gate_landed, 16)
            act.activation(tanh_gate[:], gate[:], ACT.Tanh).then_inc(gate_done, 1)
            for i, ly in enumerate(LAYERS):
                with act.Fori(0, B // 2) as pair:
                    for u in range(2):
                        b = pair * 2 + u
                        act.wait_ge(h_turned, b + (B * i + 3))
                        act.activation(h_t[:, b, :, :], A[u][:, 0:DC * L].rearrange("p (c l) -> p c l", c=DC),
                                       ACT.Copy).then_inc(h_copied, 1)

                def step(g, b, n, i=i, ly=ly):
                    if VECTORS[ly.name]:
                        act.wait_ge(vectors_landed, vectors_at(i, g))
                    for t in range(ly.kt):
                        act.wait_ge(s["k_ready"], at(i, "k_ready", n, t + 1))
                        if ly.name == "L2":
                            act.activation(k_t[:, t, 0:S], A[(ly.qt // 4 + t) % 2][:, 0:S], ACT.Copy)\
                               .then_inc(s["k_taken"], 1)
                        else:
                            act.activation(k_t[:, t, 0:S], A[(ly.qt // 4 + t) % 2][:, 0:S], ACT.Identity,
                                           bias=bk[:, t:t + 1]).then_inc(s["k_taken"], 1)

                    def exps(q):
                        for j in range(4):
                            h = 4 * q + j
                            c = ly.heads[h]["n"]
                            act.wait_ge(s["max_ready"], at(i, "max_ready", n, h + 1))
                            src = masked[:, q % 2, j, :] if ly.masked else Sb[h % 3][0:L, 0:KEYS]
                            act.activation(probs[:, q % 2, j, 0:ly.keys], src, ACT.Exp, bias=neg_max[:, c:c + 1],
                                           scale=-1.0 if ly.masked else 1.0, accum_out=row_sum[:, c:c + 1])\
                               .then_inc(s["exp_done"], 1)

                    exps(0)
                    for q in range(ly.quads):
                        act.wait_ge(s["pt_ready"], at(i, "pt_ready", n, 3 * q + 1))
                        act.activation(probs_t[:, q % 2, 0, :], T[3 * q % 2][:, 0:4 * L], ACT.Copy)\
                           .then_inc(s["pt_first"], 1)
                        if q + 1 < ly.quads:
                            exps(q + 1)
                    act.wait_ge(s["ot_ready"], at(i, "ot_ready", n, 1))
                    ot = A[(ly.qt // 4 + ly.kt + 3) % 2]
                    act.activation(o_h[:], ot[:, 0:DC * L].rearrange("p (c l) -> p c l", c=DC), ACT.Copy)\
                       .then_inc(s["ot_hi"], 1)

                steps(act, ly, step)

        @block.tensor
        def _(pe):
            pe.sem_inc(h_turned, 2)

            def product(out, pairs, end=None):
                terms = [(l, r) for (lh, ll), (rh, rl) in pairs for l, r in ((ll, rh), (lh, rl), (lh, rh))]
                for k, (l, r) in enumerate(terms):
                    last = pe.matmul(out, l, r, start=k == 0, stop=k == len(terms) - 1)
                return last

            for i, ly in enumerate(LAYERS):
                pe.wait_ge(s["ot_lo"], at(i, "ot_lo", 0, 0))
                pe.wait_ge(s["x_done"], at(i, "x_done", 0, 0))
                with pe.Fori(0, B // 2) as pair:
                    for u in range(2):
                        b = pair * 2 + u
                        pe.wait_ge(h_made, b + (B * i + 2))
                        pe.wait_ge(h_copied, b + (B * i + 1))
                        for c in range(DC):
                            last = pe.transpose(A[u][:, c * L:(c + 1) * L], h_rows[:, u, c * P:(c + 1) * P],
                                                ident[0:L, 0:L])
                        last.then_inc(h_turned, 1)
                pe.wait_ge(h_copied, B * (i + 1) + 2)

                uses = ["q_taken"] * (ly.qt // 4) + ["k_taken"] * ly.kt + ["v_taken"] * 3 + ["ot_lo", "x_done"]

                def step(g, b, n, i=i, ly=ly, uses=uses):
                    use = [0]

                    def bank():
                        u = use[0]
                        use[0] += 1
                        name = uses[u - 2]
                        count = uses[:u - 1].count(name) if u >= 2 else 0
                        pe.wait_ge(s[name], at(i, name, n, count))
                        return A[u % 2]

                    pe.wait_ge(weights_split, weights_at(i, g, 4 + ly.wq_parts))
                    for t0 in range(0, ly.qt, 4):
                        to = bank()
                        for t in range(t0, t0 + 4):
                            for c in range(DC):
                                last = pe.matmul(to[:, (t - t0) * L:(t - t0 + 1) * L], wq[:, c, t * P:(t + 1) * P],
                                                 h_t[:, b, c, :], start=c == 0, stop=c == DC - 1)
                        last.then_inc(s["q_ready"], 1)
                    pe.wait_ge(s["ctx_split"], at(i, "ctx_split", n, 2))
                    for t in range(ly.kt):
                        to = bank()
                        product(to[:, 0:KEYS],
                                [((wk_h[:, c, t * P:(t + 1) * P], wk_l[:, c, t * P:(t + 1) * P]),
                                  (ctx_h[:, c, :], ctx_l[:, c, :])) for c in range(DC)]).then_inc(s["k_ready"], 1)

                    def scores(q):
                        for h in range(4 * q, 4 * q + 4):
                            x = ly.heads[h]
                            if h == 0:
                                pe.wait_ge(s["q_taken"], at(i, "q_taken", n, ly.qt // 4))
                                pe.wait_ge(s["k_taken"], at(i, "k_taken", n, ly.kt))
                                if ly.last:
                                    pe.wait_ge(vectors_landed, vectors_at(i, g))
                            name = "max_ready" if ly.masked else "exp_done"
                            pe.wait_ge(s[name], at(i, name, n, max(h - 2, 0)))
                            r = slice(x["row"], x["row"] + x["rows"])
                            pe.matmul(Sb[h % 3][0:L, 0:ly.keys], q_t[r, x["q"], :], k_t[r, x["k"], 0:ly.keys],
                                      start=True, stop=True).then_inc(s["s_ready"], 1)

                    def values(t):
                        to = bank()
                        rows = ROWS[t]
                        product(to[0:rows, 0:ly.vw],
                                [((ctx_h[:, c, t * P:t * P + rows], ctx_l[:, c, t * P:t * P + rows]),
                                  (wv_h[:, c, 0:ly.vw], wv_l[:, c, 0:ly.vw])) for c in range(DC)])\
                            .then_inc(s["v_ready"], 1)

                    def turn(q):
                        pe.wait_ge(s["exp_done"], at(i, "exp_done", n, 4 * q + 4))
                        for c, (k0, kn) in enumerate(ly.chunks):
                            k = 3 * q + c
                            if k < 2:
                                pe.wait_ge(s["pt_first"], at(i, "pt_first", n, 0))
                                pe.wait_ge(s["pt_rest"], at(i, "pt_rest", n, 0))
                            elif c == 2:
                                pe.wait_ge(s["pt_first"], at(i, "pt_first", n, q + 1))
                            else:
                                pe.wait_ge(s["pt_rest"], at(i, "pt_rest", n, 2 * (q - 1) + 1 + c))
                            for j in range(4):
                                last = pe.transpose(T[k % 2][0:kn, j * L:(j + 1) * L],
                                                    probs[:, q % 2, j, k0:k0 + kn], ident[0:L, 0:L])
                            last.then_inc(s["pt_ready"], 1)

                    def weigh(q):
                        pe.wait_ge(s["pt_first"], at(i, "pt_first", n, q + 1))
                        pe.wait_ge(s["pt_rest"], at(i, "pt_rest", n, 2 * q + 2))
                        if q == 0:
                            pe.wait_ge(s["v_taken"], at(i, "v_taken", n, 3))
                            pe.wait_ge(s["o_taken"], at(i, "o_taken", n, 0))
                        for j in range(4):
                            x = ly.heads[4 * q + j]
                            for c, (k0, kn) in enumerate(ly.chunks):
                                last = pe.matmul(O[0:L, x["o"]:x["o"] + ly.dh], probs_t[0:kn, q % 2, c, j * L:(j + 1) * L],
                                                 v[0:kn, c, x["v"]:x["v"] + ly.dh], start=c == 0, stop=c == 2)
                        if q == ly.quads - 1:
                            last.then_inc(s["o_ready"], 1)

                    scores(0)
                    values(0)
                    values(1)
                    if ly.quads == 1:
                        turn(0)
                        values(2)
                    else:
                        values(2)
                        for q in range(ly.quads):
                            if q + 1 < ly.quads:
                                scores(q + 1)
                            turn(q)
                            if q >= 1:
                                weigh(q - 1)
                    weigh(ly.quads - 1)
                    to = bank()
                    pe.wait_ge(s["o_taken"], at(i, "o_taken", n, 1))
                    for c in range(DC):
                        last = pe.transpose(to[:, c * L:(c + 1) * L], o[:, c * P:(c + 1) * P], ident[0:L, 0:L])
                    last.then_inc(s["ot_ready"], 1)
                    to = bank()
                    pe.wait_ge(weights_split, weights_at(i, g, 6 + ly.wq_parts))
                    pe.wait_ge(s["ot_lo"], at(i, "ot_lo", n, 1))
                    product(to[0:L, :], [((o_h[:, c, :], o_l[:, c, :]), (wo_h[:, c, :], wo_l[:, c, :]))
                                         for c in range(DC)]).then_inc(s["out_ready"], 1)

                steps(pe, ly, step)

        @block.vector
        def _(vec):
            for name in ("q_taken", "v_taken", "max_ready", "pt_rest", "o_taken", "ot_lo", "x_done", "mask_made", "link"):
                vec.sem_inc(s[name], 1)
            vec.sem_inc(h_made, 1)
            vec.wait_ge(x_landed, 16)

            for i, ly in enumerate(LAYERS):
                vec.wait_ge(s["x_done"], at(i, "x_done", 0, 0))
                vec.wait_ge(s["link"], at(i, "link", 0, 0))
                if NORMS[ly.name]:
                    vec.wait_ge(norm_landed, norms_at(i))
                with vec.Fori(0, B // 2) as pair:
                    for u in range(2):
                        b = pair * 2 + u
                        vec.wait_ge(h_turned, b + (B * i + 1))
                        if not ly.last:
                            vec.tensor_copy(h_rows[:, u, :], X[:, b, :]).then_inc(h_made, 1)
                            continue
                        before = PREP_LINKS * B * (i - 3)
                        links = [0]

                        def chain(ins, settle=None, b=b, before=before, links=links):
                            links[0] += 1
                            ins.then_inc(prep, 1)
                            vec.wait_ge(prep, b * PREP_LINKS + (before + links[0]))
                            if settle:
                                settle(vec)

                        norm_rows(vec, chain, stats, X[:, b, :], h_rows[:, u, :], 1e-5, var_ready, rstd_ready,
                                  b + (NORMED[ly.name] + 1), settle)
                        chain(vec.tensor_tensor(h_rows[:, u, :], h_rows[:, u, :], gamma[0:L, :], ALU.mult))
                        chain(vec.tensor_tensor(X[:, b, :], X[:, b, :], bo[0:L, :], ALU.add))
                        vec.tensor_tensor(h_rows[:, u, :], h_rows[:, u, :], beta[0:L, :], ALU.add).then_inc(h_made, 1)
                        assert links[0] == PREP_LINKS

                def step(g, b, n, i=i, ly=ly):
                    links = [0]

                    def chain(ins, settle=None):
                        links[0] += 1
                        ins.then_inc(s["link"], 1)
                        vec.wait_ge(s["link"], at(i, "link", n, links[0]))
                        if settle:
                            settle(vec)

                    if ly.masked:
                        vec.wait_ge(s["mask_landed"], at(i, "mask_landed", n, 16))
                    if ly.masked and not ly.gqa:
                        chain(vec.tensor_scalar(mask_f[:], mask_u8[:], 1.0, FLT_MAX, ALU.subtract, ALU.mult))
                        vec.tensor_scalar(mask[:], mask_f[:], 10.0, None, ALU.mult).then_inc(s["mask_made"], 1)
                        vec.wait_ge(s["mask_made"], at(i, "mask_made", n, 1))
                    if VECTORS[ly.name]:
                        vec.wait_ge(vectors_landed, vectors_at(i, g))
                    for k in range(ly.qt // 4):
                        vec.wait_ge(s["q_ready"], at(i, "q_ready", n, k + 1))
                        for t in range(4 * k, 4 * k + 4):
                            last = vec.tensor_scalar(q_t[:, t, :], A[k % 2][:, (t - 4 * k) * L:(t - 4 * k + 1) * L],
                                                     0.0 if ly.name == "L2" else bq[:, t:t + 1], ly.scale,
                                                     ALU.add, ALU.mult)
                        last.then_inc(s["q_taken"], 1)

                    def maxima(q):
                        for j in range(4):
                            h = 4 * q + j
                            c = ly.heads[h]["n"]
                            vec.wait_ge(s["s_ready"], at(i, "s_ready", n, h + 1))
                            if ly.masked:
                                settle(vec)
                                vec.tensor_tensor_reduce(masked[:, q % 2, j, :], Sb[h % 3][0:L, 0:S], mask[:], -1.0,
                                                         FLT_MAX, ALU.add, ALU.min, neg_max[:, c:c + 1])\
                                   .then_inc(s["max_ready"], 1)
                            else:
                                vec.tensor_reduce(neg_max[:, c:c + 1], Sb[h % 3][0:L, 0:KEYS], AX.X, ALU.max,
                                                  negate=True).then_inc(s["max_ready"], 1)

                    def values(t):
                        vec.wait_ge(s["v_ready"], at(i, "v_ready", n, t + 1))
                        src = A[(ly.qt // 4 + ly.kt + t) % 2][0:ROWS[t], 0:ly.vw]
                        dst = v[0:ROWS[t], t, 0:ly.vw]
                        if ly.name == "L2":
                            vec.tensor_copy(dst, src).then_inc(s["v_taken"], 1)
                        else:
                            vec.tensor_tensor(dst, src, bv[0:ROWS[t], 0:ly.vw], ALU.add).then_inc(s["v_taken"], 1)

                    def turned(q):
                        for c in (1, 2):
                            kn = ly.chunks[c][1]
                            vec.wait_ge(s["pt_ready"], at(i, "pt_ready", n, 3 * q + c + 1))
                            vec.tensor_copy(probs_t[0:kn, q % 2, c, :], T[(3 * q + c) % 2][0:kn, 0:4 * L])\
                               .then_inc(s["pt_rest"], 1)

                    maxima(0)
                    values(0)
                    values(1)
                    if ly.quads == 1:
                        turned(0)
                        values(2)
                    else:
                        values(2)
                        for q in range(ly.quads):
                            if q + 1 < ly.quads:
                                maxima(q + 1)
                            turned(q)
                    heads = len(ly.heads)
                    vec.wait_ge(s["exp_done"], at(i, "exp_done", n, heads))
                    chain(vec.reciprocal(inv_sum[:, 0:heads], row_sum[:, 0:heads]))
                    vec.wait_ge(s["o_ready"], at(i, "o_ready", n, 1))
                    vec.tensor_tensor(o[:].rearrange("l (h d) -> l h d", h=heads),
                                      O[0:L, :].rearrange("l (h d) -> l h d", h=heads),
                                      inv_sum[:, 0:heads].unsqueeze(2).broadcast_to([L, heads, ly.dh]), ALU.mult)\
                       .then_inc(s["o_taken"], 1)
                    vec.wait_ge(s["ot_hi"], at(i, "ot_hi", n, 1))
                    u = ly.qt // 4 + ly.kt + 3
                    vec.tensor_tensor(o_l[:], A[u % 2][:, 0:DC * L].rearrange("p (c l) -> p c l", c=DC), o_h[:],
                                      ALU.subtract).then_inc(s["ot_lo"], 1)
                    vec.wait_ge(s["out_ready"], at(i, "out_ready", n, 1))
                    res = A[(u + 1) % 2][0:L, :]
                    if ly.last:
                        vec.tensor_tensor(X[:, b, :], res, X[:, b, :], ALU.add).then_inc(s["x_done"], 1)
                    elif ly.name == "L2":
                        if i == 2:
                            vec.wait_ge(gate_done, 1)
                        vec.scalar_tensor_tensor(X[:, b, :], res, tanh_gate[:, 0:1], X[:, b, :], ALU.mult, ALU.add)\
                           .then_inc(s["x_done"], 1)
                    else:
                        vec.tensor_tensor(y[:], res, X[:, b, :], ALU.add).then_inc(s["x_done"], 1)
                        vec.wait_ge(s["x_done"], at(i, "x_done", n, 1))
                        chain(vec.tensor_tensor(y[:], y[:], bo[0:L, :], ALU.add))
                        norm_rows(vec, chain, stats, y[:], y[:], 1e-6, var_ready, rstd_ready, b + (NORMED[ly.name] + 1), settle)
                        chain(vec.tensor_tensor(y[:], y[:], gamma[0:L, :], ALU.mult))
                        chain(vec.tensor_tensor(X[:, b, :], y[:], beta[0:L, :], ALU.add))
                    assert links[0] == ly.per["link"]

                steps(vec, ly, step)


def feed_forward(nc, a, X, ident, minus_half, out):
    HB = B // 2
    HL = HB * L
    with ExitStack() as ctx:
        def sb(name, shape, dt=F32):
            return ctx.enter_context(nc.sbuf_tensor(name, shape, dt))

        def psum(name):
            return ctx.enter_context(nc.psum_tensor(name, [P, 512], F32))

        def sem(name):
            return ctx.enter_context(nc.semaphore(name))

        rows = sb("mlp_rows", [L, 2, D])
        in_h, in_l = (sb(n, [P, B, DC, L], F32R) for n in ("in_h", "in_l"))
        gamma, beta, b2 = (sb(n, [L, D]) for n in ("mlp_gamma", "mlp_beta", "b2"))
        b1 = sb("b1", [P, FT])
        w1_raw = sb("w1_raw", [P, 2, DC, P])
        w2_raw = sb("w2_raw", [P, 2, D])
        w1_h, w1_l = (sb(n, [P, 2, DC, P], F32R) for n in ("w1_h", "w1_l"))
        w2_h, w2_l = (sb(n, [P, 2, D], F32R) for n in ("w2_h", "w2_l"))
        g = sb("g", [P, 2, HL])
        g_h, g_l = (sb(n, [P, 2, HL], F32R) for n in ("g_h", "g_l"))
        y = sb("mlp_y", [L, HB, D])
        stats = sb("mlp_stats", [L, 9])
        A = [psum(f"mlp_A{i}") for i in range(2)]
        R = [psum(f"mlp_R{i}") for i in range(HB)]
        (vectors_landed, link, rows_made, rows_turned, rows_hi, rows_lo, w_split, fc1_ready, gelu_done, g_hi, g_lo,
         fc2_done, taken, y_made, stored, var_ready, rstd_ready) = (sem("mlp_" + n) for n in (
             "vectors_landed", "link", "rows_made", "rows_turned", "rows_hi", "rows_lo", "w_split", "fc1_ready",
             "gelu_done", "g_hi", "g_lo", "fc2_done", "taken", "y_made", "stored", "var_ready",
             "rstd_ready"))
        w_landed = [sem(f"mlp_w_landed{u}") for u in range(2)]

        settled = sem("mlp_settled")

        def settle(eng):
            eng.sem_inc(settled, 1)

        block = ctx.enter_context(nc.Block())

        def pairs(eng, half, body):
            body(True, False, half * (FT // 2))
            with eng.Fori(1, FT // 2 - 1) as pair:
                body(False, False, half * (FT // 2) + pair)
            body(False, True, half * (FT // 2) + (FT // 2 - 1))

        @block.sync
        def _(sp):
            for dst, name in ((gamma, "ln_mlp_scale"), (beta, "ln_mlp_offset"), (b2, "b_fc2")):
                sp.dma_start(dst[:], rows_of(a["L3_xattn_" + name], L)).then_inc(vectors_landed, 16)
            sp.dma_start(b1[:], a["L3_xattn_b_fc1"].rearrange("(t p) -> p t", p=P),
                         allow_slow_non_contiguous=True).then_inc(vectors_landed, 16)
            sp.sem_inc(stored, 16)
            w1 = a["L3_xattn_w_fc1"].rearrange("(c p) (t n) -> t p c n", p=P, n=P)
            w2 = a["L3_xattn_w_fc2"].rearrange("(t p) n -> t p n", p=P)
            with sp.Fori(0, 2) as half:
                with sp.Fori(0, FT // 2) as pair:
                    for u in range(2):
                        t = pair * 2 + u
                        sp.wait_ge(w_split, half * (4 * FT) + t * 4 + 1)
                        settle(sp)
                        sp.dma_start(w1_raw[:, u, :, :], w1[t]).then_inc(w_landed[u], 16)
                        sp.dma_start(w2_raw[:, u, :], w2[t]).then_inc(w_landed[u], 16)
                for j in range(HB):
                    sp.wait_ge(y_made, half * HB + (j + 1))
                    settle(sp)
                    sp.dma_start(out[half * HB + j], y[:, j, :]).then_inc(stored, 16)
            sp.wait_ge(stored, 16 * (1 + B))

        @block.gpsimd
        def _(pool):
            pool.sem_inc(w_split, 5)
            with pool.Fori(0, B) as b:
                pool.wait_ge(var_ready, b + 1)
                pool.tensor_tensor(stats[:, 8:9], stats[:, 8:9], minus_half[0:L, 0:1], ALU.pow)\
                    .then_inc(rstd_ready, 1)

            def pair_of(first, last, pair):
                for u in range(2):
                    k = pair * 2 + u
                    pool.wait_ge(w_landed[u], pair * 32 + 32)
                    pool.wait_ge(fc2_done, k + 1)
                    settle(pool)
                    pool.tensor_copy(w1_h[:, u], w1_raw[:, u]).then_inc(w_split, 1)
                    pool.tensor_copy(w2_h[:, u], w2_raw[:, u]).then_inc(w_split, 1)
                    pool.wait_ge(w_split, k * 4 + 7)
                    pool.tensor_tensor(w1_l[:, u], w1_raw[:, u], w1_h[:, u], ALU.subtract).then_inc(w_split, 1)
                    pool.tensor_tensor(w2_l[:, u], w2_raw[:, u], w2_h[:, u], ALU.subtract).then_inc(w_split, 1)

            with pool.Fori(0, FT) as pair:
                pair_of(False, False, pair)

        @block.scalar
        def _(act):
            act.sem_inc(rows_hi, 2)
            act.sem_inc(gelu_done, 2)
            with act.Fori(0, B // 2) as pair:
                for u in range(2):
                    b = pair * 2 + u
                    act.wait_ge(rows_turned, b + 3)
                    act.activation(in_h[:, b], A[u][:, 0:DC * L].rearrange("p (c l) -> p c l", c=DC), ACT.Copy)\
                       .then_inc(rows_hi, 1)
            act.wait_ge(vectors_landed, 64)
            with act.Fori(0, 2) as half:
                with act.Fori(0, FT // 2) as pair:
                    for u in range(2):
                        t = pair * 2 + u
                        k = half * FT + t
                        act.wait_ge(fc1_ready, k + 1)
                        act.wait_ge(fc2_done, k + 1)
                        act.activation(g[:, u, :], A[u][:, 0:HL], ACT.Gelu, bias=b1[:, bass.ds(t, 1)])\
                           .then_inc(gelu_done, 1)
                        act.wait_ge(gelu_done, k + 3)
                        act.activation(g_h[:, u, :], g[:, u, :], ACT.Copy).then_inc(g_hi, 1)

        @block.tensor
        def _(pe):
            pe.sem_inc(rows_turned, 2)
            pe.sem_inc(fc2_done, 2)
            with pe.Fori(0, B // 2) as pair:
                for u in range(2):
                    b = pair * 2 + u
                    pe.wait_ge(rows_made, b + 1)
                    pe.wait_ge(rows_hi, b + 1)
                    pe.wait_ge(rows_lo, b + 1)
                    for c in range(DC):
                        last = pe.transpose(A[u][:, c * L:(c + 1) * L], rows[:, u, c * P:(c + 1) * P], ident[0:L, 0:L])
                    last.then_inc(rows_turned, 1)
            pe.wait_ge(rows_lo, B + 2)
            with pe.Fori(0, 2) as half:
                def second(u, k, first, last):
                    pe.wait_ge(g_lo, k + 1)
                    if first:
                        pe.wait_ge(taken, half * HB + 1)
                    for j in range(HB):
                        cols = slice(j * L, (j + 1) * L)
                        terms = [(g_l, w2_h), (g_h, w2_l), (g_h, w2_h)]
                        for m, (l, r) in enumerate(terms):
                            mm = pe.matmul(R[j][0:L, :], l[:, u, cols], r[:, u, :], start=first and m == 0,
                                           stop=last and m == 2)
                    mm.then_inc(fc2_done, 1)

                def pair_of(first, last, pair):
                    for u in range(2):
                        k = pair * 2 + u
                        pe.wait_ge(w_split, k * 4 + 9)
                        pe.wait_ge(gelu_done, k + 1)
                        terms = [(l[:, u, c, :], r[:, bass.ds(half * HB, HB), c, :]) for c in range(DC)
                                 for l, r in ((w1_l, in_h), (w1_h, in_l), (w1_h, in_h))]
                        for m, (l, r) in enumerate(terms):
                            mm = pe.matmul(A[u][:, 0:HL], l, r, start=m == 0, stop=m == len(terms) - 1)
                        mm.then_inc(fc1_ready, 1)
                        if not (first and u == 0):
                            second(1 - u, k - 1, first and u == 1, False)
                    if last:
                        second(1, pair * 2 + 1, False, True)

                pairs(pe, half, pair_of)

        @block.vector
        def _(vec):
            vec.sem_inc(rows_lo, 2)
            vec.sem_inc(taken, 1)
            vec.wait_ge(vectors_landed, 64)
            with vec.Fori(0, B // 2) as pair:
                for u in range(2):
                    b = pair * 2 + u
                    links = [0]

                    def chain(ins, settle=None, b=b, links=links):
                        links[0] += 1
                        ins.then_inc(link, 1)
                        vec.wait_ge(link, b * 4 + links[0])
                        if settle:
                            settle(vec)

                    vec.wait_ge(rows_turned, b + 1)
                    norm_rows(vec, chain, stats, X[:, b, :], rows[:, u, :], 1e-5, var_ready, rstd_ready, b + 1,
                              settle)
                    chain(vec.tensor_tensor(rows[:, u, :], rows[:, u, :], gamma[:], ALU.mult))
                    vec.tensor_tensor(rows[:, u, :], rows[:, u, :], beta[:], ALU.add).then_inc(rows_made, 1)
                    vec.wait_ge(rows_hi, b + 3)
                    vec.tensor_tensor(in_l[:, b], A[u][:, 0:DC * L].rearrange("p (c l) -> p c l", c=DC), in_h[:, b],
                                      ALU.subtract).then_inc(rows_lo, 1)
            with vec.Fori(0, 2) as half:
                with vec.Fori(0, FT // 2) as pair:
                    for u in range(2):
                        k = half * FT + pair * 2 + u
                        vec.wait_ge(g_hi, k + 1)
                        vec.tensor_tensor(g_l[:, u, :], g[:, u, :], g_h[:, u, :], ALU.subtract).then_inc(g_lo, 1)
                vec.wait_ge(fc2_done, half * FT + (FT + 2))
                vec.wait_ge(stored, half * (16 * HB) + 16)
                for j in range(HB):
                    b = half * HB + j
                    vec.tensor_tensor(y[:, j, :], R[j][0:L, :], X[:, b, :], ALU.add).then_inc(taken, 1)
                    vec.wait_ge(taken, b + 2)
                    vec.tensor_tensor(y[:, j, :], y[:, j, :], b2[:], ALU.add).then_inc(y_made, 1)


def kernel(**inputs):
    import numpy as _np
    import concourse.bacc as _bacc
    from concourse import mybir as _mybir
    from concourse.bass_utils import run_bass_kernel_spmd as _run

    nc = _bacc.Bacc("TRN2", target_bir_lowering=False, num_devices=1)
    arrays, args = {}, {}
    for name, value in inputs.items():
        array = _np.ascontiguousarray(value)
        if array.dtype == _np.bool_:
            array = array.view(_np.uint8)
        arrays[f"in_{name}"] = array
        args[name] = nc.dram_tensor(f"in_{name}", array.shape, _mybir.dt.from_np(array.dtype),
                                    kind="ExternalInput").ap()
    out = nc.dram_tensor("out", [B, L, D], F32, kind="ExternalOutput").ap()
    build(nc, args, out)
    r = _run(nc, [arrays], core_ids=[0])
    return r.results[0]["out"]
```

```python
from contextlib import ExitStack

import concourse.bass as bass
from concourse import mybir

F32 = mybir.dt.float32
F32R = mybir.dt.float32r
U8 = mybir.dt.uint8
ALU = mybir.AluOpType
ACT = mybir.ActivationFunctionType
AX = mybir.AxisListType

P = 128
B, L, D, S = 8, 112, 512, 375
DC = D // P
KEYS = S + 1
ROWS = [P, P, S - 2 * P]
F = 2048
FT = F // P
FLT_MAX = 3.4e38


class Layer:

    def __init__(self, name, groups, qt, kt, vw, dh, heads, keys, scale, links, masked=False):
        self.name, self.groups, self.qt, self.kt, self.vw, self.dh = name, groups, qt, kt, vw, dh
        self.heads, self.keys, self.scale, self.masked = heads, keys, scale, masked
        self.gqa, self.last = name in ("L0", "L1"), name.startswith("L3")
        self.quads = len(heads) // 4
        self.chunks = [(0, P), (P, P), (2 * P, keys - 2 * P)]
        self.wq_parts = 8 if self.gqa else 1
        self.per = dict(
            q_ready=qt // 4, k_ready=kt, v_ready=3, s_ready=len(heads), pt_ready=3 * self.quads,
            o_ready=1, ot_ready=1, out_ready=1,
            q_taken=qt // 4, k_taken=kt, v_taken=3, max_ready=len(heads), exp_done=len(heads),
            pt_first=self.quads, pt_rest=2 * self.quads, o_taken=1, ot_hi=1, ot_lo=1, x_done=1,
            ctx_split=2, ctx_landed=16, link=links)


def gqa_heads():
    out = []
    for t in range(8):
        for j in range(4):
            kv = 2 * j + t // 4
            n = 4 * kv + t % 4
            out.append(dict(q=t, k=0, row=32 * j, rows=32, v=16 * kv, o=16 * n, n=n))
    return out


LAYERS = [
    Layer(f"L3_{i}", 4, 4, 4, D, P, [dict(q=h, k=h, row=0, rows=P, v=P * h, o=P * h, n=h) for h in range(4)],
          KEYS, P ** -0.5, 1) for i in (1, 2)]

NO_START = ("q_ready", "k_ready", "v_ready", "s_ready", "pt_ready", "o_ready", "ot_ready", "out_ready",
            "ctx_landed")


def at(i, name, step, count):
    before = sum(ly.per[name] * ly.groups * B for ly in LAYERS[:i]) + (name not in NO_START)
    return step * LAYERS[i].per[name] + (before + count)


def weights_at(i, group, count):
    before = sum((6 + ly.wq_parts) * ly.groups for ly in LAYERS[:i]) + 1
    return group * (6 + LAYERS[i].wq_parts) + (before + count)


def rows_of(vector, n=P):
    return vector.rearrange("(o d) -> o d", o=1).broadcast_to([n, D])


def build(nc, a, out):
    scratch_ctx = nc.dram_tensor("ctx_transposed", [B, P, DC * KEYS], F32, kind="Internal").ap()
    scratch_norm = nc.dram_tensor("ctx_norm_transposed", [B, P, DC * KEYS], F32, kind="Internal").ap()
    scratch_w = nc.dram_tensor("gated_weights_transposed", [4, D, D], F32, kind="Internal").ap()
    with ExitStack() as ctx:
        X = ctx.enter_context(nc.sbuf_tensor("X", [L, B, D], F32))
        ident = ctx.enter_context(nc.sbuf_tensor("ident", [P, P], F32))
        minus_half = ctx.enter_context(nc.sbuf_tensor("minus_half", [P, 3], F32))
        prepare_context(nc, a, scratch_ctx, scratch_norm, scratch_w, X, ident, minus_half)
        for ly in (Small("L0", True, 0.25), Small("L1", True, 0.25), Small("L2", False, 32 ** -0.5)):
            small_attention(nc, a, ly, scratch_ctx if ly.gqa else scratch_norm, scratch_w, X, ident, minus_half)
        attend(nc, a, scratch_ctx, scratch_norm, scratch_w, X, ident, minus_half)
        feed_forward(nc, a, X, ident, minus_half, out)


def prepare_context(nc, a, scratch_ctx, scratch_norm, scratch_w, X, ident, minus_half):
    with ExitStack() as ctx:
        def sb(name, shape, dt=F32):
            return ctx.enter_context(nc.sbuf_tensor(name, shape, dt))

        def sem(name):
            return ctx.enter_context(nc.semaphore(name))

        nat = sb("nat", [P, 2, 3, D])
        normed = sb("normed", [P, 3, D])
        ctx_t = sb("ctx_t", [P, DC, KEYS])
        norm_t = sb("norm_t", [P, DC, KEYS])
        gamma = sb("ctx_gamma", [P, D])
        beta = sb("ctx_beta", [P, D])
        stats = sb("ctx_stats", [P, 3, 6])
        moments = sb("ctx_moments", [P, 3, 2])
        rstd = sb("ctx_rstd", [P, 3])
        w_nat = sb("w_nat", [P, 4, DC, D])
        w_t = sb("w_t", [P, 4, DC, D])
        bank = [ctx.enter_context(nc.psum_tensor(f"ctx_bank{i}", [P, 512], F32)) for i in range(8)]
        nat_landed = [sem(f"nat{half}_landed") for half in range(2)]
        vectors_landed, w_landed = sem("ctx_vectors_landed"), sem("w_landed")
        var_ready, rstd_ready = sem("ctx_var_ready"), sem("ctx_rstd_ready")
        cleared, ident_made, link = sem("cleared"), sem("ident_made"), sem("ctx_link")
        normed_ready, ctx_turned, norm_turned = sem("normed_ready"), sem("ctx_turned"), sem("norm_turned")
        ctx_copied, norm_copied = sem("ctx_copied"), sem("norm_copied")
        ctx_stored, norm_stored, w_stored = sem("ctx_stored"), sem("norm_stored"), sem("w_stored")
        w_turned, w_copied, x_landed = sem("w_turned"), sem("w_copied"), sem("x_landed")

        settled = sem("head_settled")

        def settle(eng):
            eng.sem_inc(settled, 1)

        LINKS = 10
        block = ctx.enter_context(nc.Block())

        @block.sync
        def _(sp):
            sp.sem_inc(ctx_stored, 16)
            sp.sem_inc(norm_stored, 16)
            sp.dma_start(gamma[:], rows_of(a["L2_xattn_ln_gamma"])).then_inc(vectors_landed, 16)
            sp.dma_start(beta[:], rows_of(a["L2_xattn_ln_beta"])).then_inc(vectors_landed, 16)
            sp.wait_ge(cleared, 1)

            def load(b, half):
                c = a["ctx_2048"]
                sp.dma_start(nat[:, half, 0:2, :], c[b, 0:2 * P, :].rearrange("(t p) d -> p t d", p=P))\
                  .then_inc(nat_landed[half], 16)
                sp.dma_start(nat[0:ROWS[2], half, 2, :], c[b, 2 * P:S, :]).then_inc(nat_landed[half], 16)

            def store(b):
                sp.wait_ge(ctx_copied, 4 * b + 5)
                sp.dma_start(scratch_ctx[b], ctx_t[:].rearrange("p c k -> p (c k)")).then_inc(ctx_stored, 16)
                sp.wait_ge(norm_copied, 4 * b + 5)
                sp.dma_start(scratch_norm[b], norm_t[:].rearrange("p c k -> p (c k)")).then_inc(norm_stored, 16)

            load(0, 0)
            sp.dma_start(X[:], a["x"].rearrange("b l d -> l b d")).then_inc(x_landed, 16)
            for i, n in enumerate(("Wq", "Wk", "Wv", "Wo")):
                sp.dma_start(w_nat[:, i, :, :], a[f"L2_xattn_{n}"].rearrange("(t p) d -> p t d", p=P))\
                  .then_inc(w_landed, 16)
            load(1, 1)
            with sp.Fori(0, B // 2 - 1) as pair:
                for half in range(2):
                    store(pair * 2 + half)
                    load(pair * 2 + half + 2, half)
            store(B - 2)
            store(B - 1)
            for i in range(4):
                sp.wait_ge(w_copied, 4 * (i + 1))
                sp.dma_start(scratch_w[i].rearrange("(c p) n -> p c n", p=P), w_t[:, i, :, :])\
                  .then_inc(w_stored, 16)
            sp.wait_ge(ctx_stored, 16 * (1 + B))
            sp.wait_ge(norm_stored, 16 * (1 + B))
            sp.wait_ge(w_stored, 16 * 4)
            sp.wait_ge(x_landed, 16)

        @block.gpsimd
        def _(pool):
            pool.memset(ident[:], 0.0).then_inc(ident_made, 1)
            pool.wait_ge(ident_made, 1)
            pool.affine_select(out=ident[:], in_=ident[:], compare_op=ALU.not_equal, fill=1.0, base=0,
                               pattern=[[-1, P]], channel_multiplier=1).then_inc(ident_made, 1)
            pool.memset(minus_half[:], -0.5).then_inc(ident_made, 1)
            pool.wait_ge(ident_made, 3)
            with pool.Fori(0, B) as b:
                pool.wait_ge(var_ready, b + 1)
                pool.tensor_tensor(rstd[:], rstd[:], minus_half[:], ALU.pow).then_inc(rstd_ready, 1)

        @block.vector
        def _(vec):
            vec.sem_inc(norm_copied, 1)
            vec.memset(nat[:, :, 2, :], 0.0).then_inc(cleared, 1)
            vec.memset(ctx_t[:, :, S:KEYS], 0.0).then_inc(cleared, 1)
            vec.memset(norm_t[:, :, S:KEYS], 0.0).then_inc(cleared, 1)
            vec.wait_ge(vectors_landed, 32)
            with vec.Fori(0, B // 2) as pair:
                for half in range(2):
                    b = pair * 2 + half
                    x = nat[:, half, :, :]
                    vec.wait_ge(nat_landed[half], 32 * pair + 32)
                    for t in range(3):
                        vec.bn_stats(stats[:, t, :], x[:, t, :]).then_inc(link, 1)
                    vec.wait_ge(link, LINKS * b + 3)
                    settle(vec)
                    for t in range(3):
                        vec.bn_aggr(moments[:, t, :], stats[:, t, :]).then_inc(link, 1)
                    vec.wait_ge(link, LINKS * b + 6)
                    vec.tensor_scalar(rstd[:], moments[:, :, 1], 1e-5, None, ALU.add).then_inc(var_ready, 1)
                    vec.wait_ge(rstd_ready, b + 1)
                    if half == 1:
                        vec.wait_ge(norm_turned, 4 * b)
                    else:
                        vec.wait_ge(norm_copied, 4 * b + 1)
                    for t in range(3):
                        vec.tensor_scalar(normed[:, t, :], x[:, t, :], moments[:, t, 0:1], rstd[:, t:t + 1],
                                          ALU.subtract, ALU.mult).then_inc(link, 1)
                    vec.wait_ge(link, LINKS * b + 9)
                    vec.tensor_tensor(normed[:], normed[:], gamma[:].unsqueeze(1).broadcast_to([P, 3, D]), ALU.mult)\
                       .then_inc(link, 1)
                    vec.wait_ge(link, LINKS * b + 10)
                    vec.tensor_tensor(normed[:], normed[:], beta[:].unsqueeze(1).broadcast_to([P, 3, D]), ALU.add)\
                       .then_inc(normed_ready, 1)
                    vec.wait_ge(norm_stored, 16 * b + 16)
                    for c in range(DC):
                        vec.wait_ge(norm_turned, 4 * b + c + 1)
                        vec.tensor_copy(norm_t[:, c, 0:S], bank[4 + c][:, 0:S]).then_inc(norm_copied, 1)

        @block.scalar
        def _(act):
            act.sem_inc(ctx_copied, 1)
            act.wait_ge(cleared, 3)
            with act.Fori(0, B) as b:
                act.wait_ge(ctx_stored, 16 * b + 16)
                for c in range(DC):
                    act.wait_ge(ctx_turned, 4 * b + c + 1)
                    act.activation(ctx_t[:, c, 0:S], bank[c][:, 0:S], ACT.Copy).then_inc(ctx_copied, 1)
            for n in range(16):
                act.wait_ge(w_turned, n + 1)
                act.activation(w_t[:, n // 4, n % 4, :], bank[n % 8][:, :], ACT.Copy).then_inc(w_copied, 1)

        @block.tensor
        def _(pe):
            pe.wait_ge(ident_made, 2)
            with pe.Fori(0, B // 2) as pair:
                for half in range(2):
                    b = pair * 2 + half
                    pe.wait_ge(nat_landed[half], 32 * pair + 32)
                    pe.wait_ge(ctx_copied, 4 * b + 1)
                    for c in range(DC):
                        for t in range(3):
                            last = pe.transpose(bank[c][:, t * P:t * P + ROWS[t]],
                                                nat[0:ROWS[t], half, t, c * P:(c + 1) * P],
                                                ident[0:ROWS[t], 0:ROWS[t]])
                        last.then_inc(ctx_turned, 1)
                    pe.wait_ge(normed_ready, b + 1)
                    pe.wait_ge(norm_copied, 4 * b + 1)
                    for c in range(DC):
                        for t in range(3):
                            last = pe.transpose(bank[4 + c][:, t * P:t * P + ROWS[t]],
                                                normed[0:ROWS[t], t, c * P:(c + 1) * P],
                                                ident[0:ROWS[t], 0:ROWS[t]])
                        last.then_inc(norm_turned, 1)
            pe.wait_ge(ctx_copied, 4 * B + 1)
            pe.wait_ge(norm_copied, 4 * B + 1)
            for n in range(16):
                i, c = n // 4, n % 4
                if c == 0:
                    pe.wait_ge(w_landed, 64)
                if n >= 8:
                    pe.wait_ge(w_copied, n - 7)
                for t in range(DC):
                    last = pe.transpose(bank[n % 8][:, t * P:(t + 1) * P], w_nat[:, i, t, c * P:(c + 1) * P], ident[:])
                last.then_inc(w_turned, 1)


PREP_LINKS = 5




def norm_rows(vec, chain, stats, x, y, eps, var_ready, rstd_ready, value, settle):
    chain(vec.bn_stats(stats[:, 0:6], x), settle)
    chain(vec.bn_aggr(stats[:, 6:8], stats[:, 0:6]))
    vec.tensor_scalar(stats[:, 8:9], stats[:, 7:8], eps, None, ALU.add).then_inc(var_ready, 1)
    vec.wait_ge(rstd_ready, value)
    chain(vec.tensor_scalar(y, x, stats[:, 6:7], stats[:, 8:9], ALU.subtract, ALU.mult))


class Small:

    def __init__(self, name, gqa, scale):
        self.name, self.gqa, self.scale = name, gqa, scale
        self.heads = 32 if gqa else 16
        self.quads = self.heads // 4
        self.qt = 8 if gqa else 4
        self.kt = 1 if gqa else 4
        self.vw = P if gqa else D
        self.halves = self.quads // 4
        self.links = 6
        work = [("q", k, t) for k in range(self.qt // 4) for t in range(4)]
        work += [("k", t, p) for t in range(self.kt) for p in range(3)]
        slots = 3 * (5 if gqa else 4)
        slot = [i * slots // len(work) for i in range(len(work))]
        self.fill = [[w for w, at in zip(work, slot) if at == n] for n in range(3 * self.quads)]
        self.query_after = [slot[4 * k + 3] // 3 for k in range(self.qt // 4)]
        self.key_after = [slot[self.qt + 3 * t + 2] // 3 for t in range(self.kt)]
        q, s = self.qt // 4, self.quads
        self.per = dict(
            q_ready=q, k_ready=self.kt, v_ready=3, s_ready=self.heads, pt_ready=3 * s, o_ready=s,
            inv_turned=1, spread=self.halves, out_ready=1,
            ctx_landed=16, mask_landed=16, q_stacked=16 * 12, k_stacked=16 * 12,
            q_hi=q, k_hi=self.kt, v_hi=3, exp_done=self.heads, pt_hi=3 * s, inv_copied=1, o_hi=1,
            q_lo=q, k_lo=self.kt, v_taken=3, max_ready=self.heads, pt_lo=3 * s, o_copied=s, inv_made=1,
            o_scaled=self.halves, o_lo=1, x_done=1, mask_made=1, link=self.links,
            ctx_split=2)

    ZERO = ("q_ready", "k_ready", "v_ready", "s_ready", "pt_ready", "o_ready", "inv_turned", "spread",
            "out_ready", "ctx_landed", "mask_landed")
    BY = dict(
        act=("q_hi", "k_hi", "v_hi", "exp_done", "pt_hi", "inv_copied", "o_hi"),
        vec=("q_lo", "k_lo", "v_taken", "max_ready", "pt_lo", "o_copied", "inv_made", "o_scaled", "o_lo", "x_done",
             "mask_made", "link"),
        pool=("ctx_split",), sp=("q_stacked", "k_stacked"))

    def at(self, name, step, count):
        start = 0 if name in self.ZERO else 1
        return step * self.per[name] + (start + count)

    def query(self, q, j):
        return (q // 2, 4 * (q % 2) + j) if self.gqa else (j, q)

    def key(self, q, j):
        return (q // 2, 0) if self.gqa else (j, q)


def load_small(nc, a, ly, scratch_w, X, ident, w, h_t, sems):
    with ExitStack() as ctx:
        def sb(name, shape, dt=F32):
            return ctx.enter_context(nc.sbuf_tensor(f"{ly.name}_{name}", shape, dt))

        def sem(name):
            sems.append(nc.alloc_semaphore(f"{ly.name}_{name}"))
            return sems[-1]

        h_rows = sb("h_rows", [L, 2, D])
        stage = {n: sb(f"stage_{n}", [P, DC, ly.vw if n in "kv" else D]) for n in "qkv"}
        stage_o = sb("stage_o", [P, ly.halves, 4, D])
        bank = [ctx.enter_context(nc.psum_tensor(f"{ly.name}_turn{i}", [P, 512], F32)) for i in range(4)]
        landed = {n: sem(f"{n}_landed") for n in "qkvo"}
        h_made, h_turned, h_copied = sem("h_made"), sem("h_turned"), sem("h_copied")
        w_high, w_cleared, sel_made = sem("w_high"), sem("w_cleared"), sem("sel_made")
        w_low, v_landed, sel_cleared = sem("w_low"), sem("vectors_landed"), sem("sel_cleared")
        pre = ly.name + "_xattn_"
        gqa = ly.gqa
        block = ctx.enter_context(nc.Block())

        @block.sync
        def _(sp):
            if gqa:
                src = {n: a[f"{pre}W{n}"].rearrange("(c p) n -> p c n", p=P) for n in "qkv"}
                wo = a[pre + "Wo"].rearrange("(kv g d) n -> kv d g n", g=4, d=16)
            else:
                src = {n: scratch_w[i].rearrange("(c p) n -> p c n", p=P) for i, n in enumerate("qkv")}
                wo = scratch_w[3].rearrange("(q j d) n -> q d j n", q=4, j=4)
            for n in "kvq":
                sp.dma_start(stage[n][:], src[n]).then_inc(landed[n], 16)
            if gqa:
                for kv in range(8):
                    for half in range(2):
                        r = 32 * (kv % 4) + 16 * half
                        sp.dma_start(stage_o[r:r + 16, kv // 4, :, :], wo[kv]).then_inc(landed["o"], 16)
                sp.wait_ge(w_cleared, 2)
                bq = a[pre + "bq"].rearrange("(kv g d) -> kv d g", g=4, d=16)
                for kv in range(8):
                    r = 16 * kv
                    sp.dma_start(w["bq"][r:r + 16, 4 * (kv % 2):4 * (kv % 2) + 4], bq[kv],
                                 allow_slow_non_contiguous=True).then_inc(v_landed, 16)
                sp.dma_start(w["bk"][:], a[pre + "bk"].rearrange("(p o) -> p o", o=1),
                             allow_slow_non_contiguous=True).then_inc(v_landed, 16)
                sp.dma_start(w["bv"][:], a[pre + "bv"].rearrange("(o d) -> o d", o=1).broadcast_to([P, P]))\
                  .then_inc(v_landed, 16)
                for n in ("bo", "gamma", "beta"):
                    sp.dma_start(w[n][:], rows_of(a[pre + n], L)).then_inc(v_landed, 16)
                sp.wait_ge(v_landed, 16 * 13)
            else:
                for q in range(4):
                    sp.dma_start(stage_o[32 * q:32 * q + 32, 0, :, :], wo[q]).then_inc(landed["o"], 16)
                sp.dma_start(w["gate"][:], a["L2_xattn_gate"].rearrange("(o d) -> o d", o=1).broadcast_to([L, 1]))\
                  .then_inc(v_landed, 16)

        @block.gpsimd
        def _(pool):
            pool.memset(w["sel"][:], 0.0).then_inc(sel_cleared, 1)
            pool.wait_ge(sel_cleared, 1)
            for half in range(ly.halves):
                view = w["sel"][:, half, :, :].rearrange("h j (q r) -> h j q r", r=32)
                pool.affine_select(out=view, in_=view, compare_op=ALU.not_equal, fill=1.0, base=-16 * half,
                                   pattern=[[-1, 4], [-4, 4], [0, 32]], channel_multiplier=1).then_inc(sel_made, 1)
            pool.wait_ge(sel_made, ly.halves)

        @block.scalar
        def _(act):
            act.sem_inc(h_copied, 4)
            if gqa:
                act.wait_ge(w_cleared, 2)
            act.wait_ge(landed["k"], 16)
            act.activation(w["wk_h"][:], stage["k"][:], ACT.Copy).then_inc(w_high, 1)
            act.wait_ge(landed["v"], 16)
            act.activation(w["wv_h"][:], stage["v"][:], ACT.Copy).then_inc(w_high, 1)
            act.wait_ge(landed["o"], 16 * (16 if gqa else 4))
            act.activation(w["wo_h"][:], stage_o[:], ACT.Copy).then_inc(w_high, 1)
            with act.Fori(0, B // 4) as four:
                for u in range(4):
                    b = four * 4 + u
                    act.wait_ge(h_turned, b + 5)
                    act.activation(h_t[:, b, :, :], bank[u][:, 0:DC * L].rearrange("p (c l) -> p c l", c=DC),
                                   ACT.Copy).then_inc(h_copied, 1)
            if not gqa:
                act.wait_ge(v_landed, 16)
                act.activation(w["tanh_gate"][:], w["gate"][:], ACT.Tanh).then_inc(w_high, 1)

        @block.vector
        def _(vec):
            if gqa:
                vec.memset(w["wq"][:], 0.0).then_inc(w_cleared, 1)
                vec.memset(w["bq"][:], 0.0).then_inc(w_cleared, 1)
            with vec.Fori(0, B // 2) as pair:
                for u in range(2):
                    b = pair * 2 + u
                    vec.wait_ge(h_turned, b + 3)
                    vec.tensor_copy(h_rows[:, u, :], X[:, b, :]).then_inc(h_made, 1)
            vec.wait_ge(landed["q"], 16)
            if gqa:
                vec.wait_ge(w_cleared, 2)
                for t in range(8):
                    p, g = t // 4, t % 4
                    for c in range(DC):
                        dst = w["wq"][:, c, t * P:(t + 1) * P].rearrange("k (s p d) -> k s p d", s=4, p=2)[:, :, p, :]
                        src = stage["q"][:, c, :].rearrange("k (s p g d) -> k s p g d", s=4, p=2, g=4)[:, :, p, g, :]
                        vec.tensor_scalar(dst, src, ly.scale, None, ALU.mult).then_inc(w_low, 1)
            else:
                vec.tensor_copy(w["wq"][:], stage["q"][:]).then_inc(w_low, 1)
            for n, raw in enumerate((stage["k"], stage["v"], stage_o)):
                vec.wait_ge(w_high, n + 1)
                name = "kvo"[n]
                vec.tensor_tensor(w[f"w{name}_l"][:], raw[:], w[f"w{name}_h"][:], ALU.subtract).then_inc(w_low, 1)
            if gqa:
                vec.wait_ge(v_landed, 16 * 13)
                vec.tensor_scalar(w["bq"][:], w["bq"][:], ly.scale, None, ALU.mult).then_inc(w_low, 1)

        @block.tensor
        def _(pe):
            pe.sem_inc(h_turned, 4)
            with pe.Fori(0, B // 4) as four:
                for u in range(4):
                    b = four * 4 + u
                    pe.wait_ge(h_made, b + 1)
                    pe.wait_ge(h_copied, b + 1)
                    for c in range(DC):
                        last = pe.transpose(bank[u][:, c * L:(c + 1) * L], h_rows[:, u % 2, c * P:(c + 1) * P],
                                            ident[0:L, 0:L])
                    last.then_inc(h_turned, 1)


def small_attention(nc, a, ly, scratch, scratch_w, X, ident, minus_half):
    sems = []
    with ExitStack() as ctx:
        def sb(name, shape, dt=F32):
            return ctx.enter_context(nc.sbuf_tensor(f"{ly.name}_{name}", shape, dt))

        h_t = sb("h_t", [P, B, DC, L])
        w = dict(wq=sb("wq", [P, DC, ly.qt * P]), sel=sb("sel", [ly.heads, ly.halves, 4, P]))
        for n, shape in (("wk", [P, DC, ly.vw]), ("wv", [P, DC, ly.vw]), ("wo", [P, ly.halves, 4, D])):
            w[n + "_h"], w[n + "_l"] = sb(n + "_h", shape, F32R), sb(n + "_l", shape, F32R)
        if ly.gqa:
            w |= dict(bq=sb("bq", [P, 8]), bk=sb("bk", [P, 1]), bv=sb("bv", [P, P]))
            w |= {n: sb(n, [L, D]) for n in ("bo", "gamma", "beta")}
        else:
            w |= dict(gate=sb("gate", [L, 1]), tanh_gate=sb("tanh_gate", [L, 1]))
        load_small(nc, a, ly, scratch_w, X, ident, w, h_t, sems)
        small_steps(nc, a, ly, scratch, X, ident, minus_half, w, h_t, sems)
    nc.clear_and_free_semaphores(sems)
    nc.all_engine_barrier()


def small_steps(nc, a, ly, scratch, X, ident, minus_half, w, h_t, sems):
    gqa, quads, heads, at = ly.gqa, ly.quads, ly.heads, ly.at
    with ExitStack() as ctx:
        def sb(name, shape, dt=F32):
            return ctx.enter_context(nc.sbuf_tensor(f"{ly.name}_{name}", shape, dt))

        def psum(name):
            return ctx.enter_context(nc.psum_tensor(f"{ly.name}_{name}", [P, 512], F32))

        def sem(name):
            sems.append(nc.alloc_semaphore(f"{ly.name}_{name}"))
            return sems[-1]

        ctx_raw = sb("ctx_raw", [P, DC, KEYS])
        ctx_h, ctx_l = (sb(n, [P, DC, KEYS], F32R) for n in ("ctx_h", "ctx_l"))
        q_h, q_l = (sb(n, [P, ly.qt, L], F32R) for n in ("q_h", "q_l"))
        k_h, k_l = (sb(n, [P, ly.kt, KEYS], F32R) for n in ("k_h", "k_l"))
        q_s = sb("q_s", [96, 4, ly.qt, L], F32R)
        k_s = sb("k_s", [96, 4, ly.kt, KEYS], F32R)
        if gqa:
            v_raw = sb("v_raw", [P, 3, P])
            v_s = sb("v_s", [P, 3, 8, 2, 16], F32R)
        else:
            v_h, v_l = (sb(n, [P, 3, D], F32R) for n in ("v_h", "v_l"))
            mask_u8 = sb("mask_u8", [L, S], U8)
        mask = sb("mask", [L, S])
        probs = sb("probs", [L, 2, 4, S])
        pt_h, pt_l = (sb(n, [P, 2, 3, 4 * L], F32R) for n in ("pt_h", "pt_l"))
        o = sb("o", [P, ly.halves, 4 * L])
        o_h, o_l = (sb(n, [P, ly.halves, 4 * L], F32R) for n in ("o_h", "o_l"))
        y = sb("y", [L, D]) if gqa else None
        neg_max, row_sum, inv_sum = (sb(n, [L, heads]) for n in ("neg_max", "row_sum", "inv_sum"))
        inv_t = sb("inv_t", [heads, L])
        stats = sb("stats", [L, 9])
        A = [psum(f"A{i}") for i in range(2)]
        Sb = [psum(f"S{i}") for i in range(2)]
        T = [psum(f"T{i}") for i in range(2)]
        O = [psum(f"O{i}") for i in range(2)]
        s = {n: sem(n) for n in ly.per}
        var_ready, rstd_ready, settled, v_link, mask_half = (
            sem(n) for n in ("var_ready", "rstd_ready", "settled", "v_link", "mask_half"))

        def settle(eng):
            eng.sem_inc(settled, 1)

        def wait(eng, name, step, count):
            eng.wait_ge(s[name], at(name, step, count))

        def all_steps(eng, body):
            with eng.Fori(0, B - 1) as n:
                body(n, True)
            body(B - 1, False)

        ahead = [("q_lo", 1, k + 1) for k in range(ly.qt // 4)] + [("k_lo", 1, k + 1) for k in range(ly.kt)]
        values_ahead = [("v_taken", 1, t + 1) for t in range(3)]
        spreads = [("o_scaled", 0, k + 1) for k in range(ly.halves)]
        USES = ahead + [("inv_copied", 0, 1)] + values_ahead + spreads + [("x_done", 0, 1)]
        LAST_USES = [("inv_copied", 0, 1)] + spreads + [("x_done", 0, 1)]

        def bank_of(use, more):
            uses = USES if more else LAST_USES
            return A[uses.index(use) % 2]

        FIRST = [(name, k) for name, _, k in ahead + values_ahead]
        block = ctx.enter_context(nc.Block())

        @block.sync
        def _(sp):
            for name in ly.BY["sp"]:
                sp.sem_inc(s[name], 1)

            def load_context(n):
                wait(sp, "ctx_split", n, 0)
                settle(sp)
                sp.dma_start(ctx_raw[:].rearrange("p c k -> p (c k)"), scratch[n]).then_inc(s["ctx_landed"], 16)

            def load_mask(n):
                if gqa:
                    wait(sp, "max_ready", n, 0)
                    settle(sp)
                    sp.dma_start(mask[:], a["mask_Bx1xSxS2_ff0"][n, 0]).then_inc(s["mask_landed"], 16)
                else:
                    wait(sp, "mask_made", n, 0)
                    settle(sp)
                    sp.dma_start(mask_u8[:], a["mask_BxS2_bf1"][bass.ds(n, 1), :].broadcast_to([L, S]))\
                      .then_inc(s["mask_landed"], 16)

            def stack(n, name, low, hi, lo, dst, order):
                wait(sp, low, n, ly.per[low])
                settle(sp)
                if not isinstance(n, int) or n > 0:
                    wait(sp, "s_ready", n, 0)
                    settle(sp)
                for part, src in enumerate(order):
                    for slot in range(4):
                        sp.dma_start(dst[32 * part:32 * part + 32, slot, :, :].bitcast(F32),
                                     (hi if src == "h" else lo)[32 * slot:32 * slot + 32, :, :].bitcast(F32))\
                          .then_inc(s[name], 16)

            load_context(0)
            load_mask(0)
            stack(0, "q_stacked", "q_lo", q_h, q_l, q_s, "hhl")
            stack(0, "k_stacked", "k_lo", k_h, k_l, k_s, "hlh")
            with sp.Fori(0, B - 1) as n:
                load_context(n + 1)
                load_mask(n + 1)
                stack(n + 1, "k_stacked", "k_lo", k_h, k_l, k_s, "hlh")
                stack(n + 1, "q_stacked", "q_lo", q_h, q_l, q_s, "hhl")

        @block.gpsimd
        def _(pool):
            for name in ly.BY["pool"]:
                pool.sem_inc(s[name], 1)

            def split_context(n):
                wait(pool, "ctx_landed", n, 16)
                if not isinstance(n, int) or n > 0:
                    wait(pool, "v_ready", n, 0)
                settle(pool)
                pool.tensor_copy(ctx_h[:], ctx_raw[:]).then_inc(s["ctx_split"], 1)
                wait(pool, "ctx_split", n, 1)
                pool.tensor_tensor(ctx_l[:], ctx_raw[:], ctx_h[:], ALU.subtract).then_inc(s["ctx_split"], 1)

            def norm(n):
                pool.wait_ge(var_ready, n + 1)
                pool.tensor_tensor(stats[:, 8:9], stats[:, 8:9], minus_half[0:L, 0:1], ALU.pow)\
                    .then_inc(rstd_ready, 1)

            split_context(0)
            split_context(1)
            with pool.Fori(1, B - 1) as n:
                if gqa:
                    norm(n - 1)
                split_context(n + 1)
            if gqa:
                norm(B - 2)
                norm(B - 1)

        @block.scalar
        def _(act):
            for name in ly.BY["act"]:
                act.sem_inc(s[name], 1)

            def project(n, bank, quad=None):
                for k in range(ly.qt // 4):
                    if quad not in (None, ly.query_after[k]):
                        continue
                    wait(act, "q_ready", n, k + 1)
                    if k == 0:
                        wait(act, "q_stacked", n, 0)
                    for t in range(4 * k, 4 * k + 4):
                        src = bank("q_lo", k + 1)[:, (t - 4 * k) * L:(t - 4 * k + 1) * L]
                        if gqa:
                            last = act.activation(q_h[:, t, :], src, ACT.Identity, bias=w["bq"][:, t:t + 1])
                        else:
                            last = act.activation(q_h[:, t, :], src, ACT.Copy)
                    last.then_inc(s["q_hi"], 1)
                for t in range(ly.kt):
                    if quad not in (None, ly.key_after[t]):
                        continue
                    wait(act, "k_ready", n, t + 1)
                    if t == 0:
                        wait(act, "k_stacked", n, 0)
                    src = bank("k_lo", t + 1)[:, 0:KEYS]
                    if gqa:
                        last = act.activation(k_h[:, t, :], src, ACT.Identity, bias=w["bk"][:])
                    else:
                        last = act.activation(k_h[:, t, :], src, ACT.Copy)
                    last.then_inc(s["k_hi"], 1)

            def values(n, bank):
                if gqa:
                    return
                if not isinstance(n, int):
                    wait(act, "o_ready", n, 0)
                for t in range(3):
                    wait(act, "v_ready", n, t + 1)
                    act.activation(v_h[0:ROWS[t], t, :], bank("v_taken", t + 1)[0:ROWS[t], :], ACT.Copy)\
                       .then_inc(s["v_hi"], 1)

            def step(n, more):
                def exp(q, j):
                    if q == quads:
                        return
                    c = 4 * q + j
                    wait(act, "max_ready", n, c + 1)
                    p = probs[:, q % 2, j, :]
                    act.activation(p, p, ACT.Exp, bias=neg_max[:, c:c + 1], scale=-1.0,
                                   accum_out=row_sum[:, c:c + 1]).then_inc(s["exp_done"], 1)

                def turned(q, c):
                    rows = ROWS[c]
                    wait(act, "pt_ready", n, 3 * q + c + 1)
                    if q >= 2 and c == 0:
                        wait(act, "o_ready", n, q - 1)
                    act.activation(pt_h[0:rows, q % 2, c, :], T[(3 * q + c) % 2][0:rows, 0:4 * L], ACT.Copy)\
                       .then_inc(s["pt_hi"], 1)

                for j in range(4):
                    exp(0, j)
                for q in range(quads):
                    turned(q, 0)
                    exp(q + 1, 0)
                    turned(q, 1)
                    exp(q + 1, 1)
                    exp(q + 1, 2)
                    turned(q, 2)
                    exp(q + 1, 3)
                    if more:
                        project(n + 1, lambda name, k: bank_of((name, 1, k), more), q)
                wait(act, "inv_turned", n, 1)
                act.activation(inv_t[:], bank_of(("inv_copied", 0, 1), more)[0:heads, 0:L], ACT.Copy)\
                   .then_inc(s["inv_copied"], 1)
                if more:
                    values(n + 1, lambda name, k: bank_of((name, 1, k), more))
                wait(act, "o_scaled", n, ly.halves)
                act.activation(o_h[:], o[:], ACT.Copy).then_inc(s["o_hi"], 1)

            first = lambda name, k: A[FIRST.index((name, k)) % 2]
            project(0, first)
            values(0, first)
            all_steps(act, step)

        @block.tensor
        def _(pe):
            def product(out, pairs):
                terms = [(l, r) for (lh, ll), (rh, rl) in pairs for l, r in ((ll, rh), (lh, rl), (lh, rh))]
                for k, (l, r) in enumerate(terms):
                    last = pe.matmul(out, l, r, start=k == 0, stop=k == len(terms) - 1)
                return last

            def queries(n, k, j, to):
                t = 4 * k + j
                for c in range(DC):
                    last = pe.matmul(to[:, j * L:(j + 1) * L], w["wq"][:, c, t * P:(t + 1) * P], h_t[:, n, c, :],
                                     start=c == 0, stop=c == DC - 1)
                if j == 3:
                    last.then_inc(s["q_ready"], 1)

            def keys(n, t, part, to):
                if t == 0 and part == 0:
                    wait(pe, "ctx_split", n, 2)
                wk = w["wk_l" if part == 0 else "wk_h"]
                right = ctx_l if part == 1 else ctx_h
                for c in range(DC):
                    last = pe.matmul(to[:, 0:KEYS], wk[:, c, t * P:(t + 1) * P], right[:, c, :],
                                     start=part == 0 and c == 0, stop=part == 2 and c == DC - 1)
                if part == 2:
                    last.then_inc(s["k_ready"], 1)

            def values(n, t, to):
                rows = ROWS[t]
                product(to[0:rows, 0:ly.vw],
                        [((ctx_h[:, c, t * P:t * P + rows], ctx_l[:, c, t * P:t * P + rows]),
                          (w["wv_h"][:, c, :], w["wv_l"][:, c, :])) for c in range(DC)]).then_inc(s["v_ready"], 1)

            for i, (name, k) in enumerate(FIRST):
                if i >= 2:
                    wait(pe, *(FIRST[i - 2][0], 0, FIRST[i - 2][1]))
                if name == "q_lo":
                    for j in range(4):
                        queries(0, k - 1, j, A[i % 2])
                elif name == "k_lo":
                    for part in range(3):
                        keys(0, k - 1, part, A[i % 2])
                else:
                    values(0, k - 1, A[i % 2])

            def step(n, more):
                uses = USES if more else LAST_USES

                def bank(use):
                    i = uses.index(use)
                    if i >= 2:
                        name, d, k = uses[i - 2]
                        wait(pe, name, n + d, k)
                    else:
                        j = max(j for j in range(len(USES)) if j % 2 == i % 2)
                        name, d, k = USES[j]
                        wait(pe, name, n + d, k - ly.per[name])
                        wait(pe, "v_taken", n, 3)
                    return A[i % 2]

                def score(q, j):
                    if q == quads:
                        return
                    h = 4 * q + j
                    if h == 0:
                        wait(pe, "k_stacked", n, ly.per["k_stacked"])
                        wait(pe, "q_stacked", n, ly.per["q_stacked"])
                    wait(pe, "max_ready", n, max(h - 1, 0))
                    (qs, qt), (ks, kt) = ly.query(q, j), ly.key(q, j)
                    pe.matmul(Sb[h % 2][0:L, 0:KEYS], q_s[:, qs, qt, :], k_s[:, ks, kt, :],
                              start=True, stop=True).then_inc(s["s_ready"], 1)

                def turn(q, c):
                    k = 3 * q + c
                    if c == 0:
                        wait(pe, "exp_done", n, 4 * q + 4)
                    wait(pe, "pt_lo", n, max(k - 1, 0))
                    for j in range(4):
                        last = pe.transpose(T[k % 2][0:ROWS[c], j * L:(j + 1) * L],
                                            probs[:, q % 2, j, c * P:c * P + ROWS[c]], ident[0:L, 0:L])
                    last.then_inc(s["pt_ready"], 1)

                def weigh(q):
                    wait(pe, "pt_lo", n, 3 * q + 3)
                    wait(pe, "o_copied", n, max(q - 1, 0))
                    if q == 0:
                        wait(pe, "v_taken", n, 3)
                    to = O[q % 2]
                    if gqa:
                        terms = [(v_s[0:ROWS[c], c, q, :, :], p[0:ROWS[c], q % 2, c, :]) for c in range(3) for p in (pt_l, pt_h)]
                        for i, (l, r) in enumerate(terms):
                            last = pe.matmul(to[0:32, 0:4 * L], l, r, start=i == 0, stop=i == len(terms) - 1)
                    else:
                        for j in range(4):
                            col = slice(32 * (4 * q + j), 32 * (4 * q + j) + 32)
                            last = product(to[0:32, j * L:(j + 1) * L],
                                           [((v_h[0:ROWS[c], c, col], v_l[0:ROWS[c], c, col]),
                                             (pt_h[0:ROWS[c], q % 2, c, j * L:(j + 1) * L],
                                              pt_l[0:ROWS[c], q % 2, c, j * L:(j + 1) * L]))
                                            for c in range(3)])
                    last.then_inc(s["o_ready"], 1)

                def fill(slot):
                    for kind, k, part in ly.fill[slot] if more else ():
                        use = ("q_lo" if kind == "q" else "k_lo", 1, k + 1)
                        to = bank(use) if part == 0 else bank_of(use, more)
                        (queries if kind == "q" else keys)(n + 1, k, part, to)

                for j in range(4):
                    score(0, j)
                for q in range(quads):
                    score(q + 1, 0)
                    score(q + 1, 1)
                    turn(q, 0)
                    fill(3 * q)
                    turn(q, 1)
                    score(q + 1, 2)
                    fill(3 * q + 1)
                    if q >= 1:
                        weigh(q - 1)
                    score(q + 1, 3)
                    turn(q, 2)
                    fill(3 * q + 2)
                weigh(quads - 1)
                wait(pe, "inv_made", n, 1)
                pe.transpose(bank(("inv_copied", 0, 1))[0:heads, 0:L], inv_sum[:], ident[0:L, 0:L])\
                  .then_inc(s["inv_turned"], 1)
                if more:
                    for use in values_ahead:
                        values(n + 1, use[2] - 1, bank(use))
                wait(pe, "inv_copied", n, 1)
                for half, use in enumerate(spreads):
                    to = bank(use)
                    for j in range(4):
                        last = pe.matmul(to[:, j * L:(j + 1) * L], w["sel"][:, half, j, :], inv_t[:], start=True, stop=True)
                    last.then_inc(s["spread"], 1)
                to = bank(("x_done", 0, 1))
                wait(pe, "o_lo", n, 1)
                product(to[0:L, :], [((o_h[:, half, j * L:(j + 1) * L], o_l[:, half, j * L:(j + 1) * L]),
                                      (w["wo_h"][:, half, j, :], w["wo_l"][:, half, j, :]))
                                     for half in range(ly.halves) for j in range(4)]).then_inc(s["out_ready"], 1)

            all_steps(pe, step)

        @block.vector
        def _(vec):
            for name in ly.BY["vec"]:
                vec.sem_inc(s[name], 1)

            def project(n, bank, quad=None):
                for k in range(ly.qt // 4):
                    if quad not in (None, ly.query_after[k]):
                        continue
                    wait(vec, "q_hi", n, k + 1)
                    for t in range(4 * k, 4 * k + 4):
                        src = bank("q_lo", k + 1)[:, (t - 4 * k) * L:(t - 4 * k + 1) * L]
                        last = vec.scalar_tensor_tensor(q_l[:, t, :], src, w["bq"][:, t:t + 1] if gqa else 0.0,
                                                        q_h[:, t, :], ALU.add, ALU.subtract)
                    last.then_inc(s["q_lo"], 1)
                for t in range(ly.kt):
                    if quad not in (None, ly.key_after[t]):
                        continue
                    wait(vec, "k_hi", n, t + 1)
                    vec.scalar_tensor_tensor(k_l[:, t, :], bank("k_lo", t + 1)[:, 0:KEYS], w["bk"][:] if gqa else 0.0,
                                             k_h[:, t, :], ALU.add, ALU.subtract).then_inc(s["k_lo"], 1)

            def values(n, bank, chain):
                if gqa:
                    wait(vec, "v_taken", n, 0)
                for t in range(3):
                    rows = ROWS[t]
                    src = bank("v_taken", t + 1)[0:rows, 0:ly.vw]
                    if gqa:
                        wait(vec, "v_ready", n, t + 1)
                        chain(vec.tensor_tensor(v_raw[0:rows, t, :], src, w["bv"][0:rows, :], ALU.add))
                        raw = v_raw[0:rows, t, :].rearrange("k (h d) -> k h d", h=8)
                        chain(vec.tensor_copy(v_s[0:rows, t, :, 0, :], raw))
                        vec.tensor_tensor(v_s[0:rows, t, :, 1, :], raw, v_s[0:rows, t, :, 0, :], ALU.subtract)\
                           .then_inc(s["v_taken"], 1)
                    else:
                        wait(vec, "v_hi", n, t + 1)
                        vec.tensor_tensor(v_l[0:rows, t, :], src, v_h[0:rows, t, :], ALU.subtract)\
                           .then_inc(s["v_taken"], 1)

            def chain_of(n, start=0):
                count = [start]

                def chain(ins, settle=None):
                    count[0] += 1
                    ins.then_inc(s["link"], 1)
                    wait(vec, "link", n, count[0])
                    if settle:
                        settle(vec)
                return chain, count

            def value_chain(n):
                count = [0]

                def chain(ins):
                    count[0] += 1
                    ins.then_inc(v_link, 1)
                    vec.wait_ge(v_link, n * 6 + count[0])
                return chain

            def new_rows(n):
                chain, count = chain_of(n)
                wait(vec, "x_done", n, 1)
                chain(vec.tensor_tensor(y[:], y[:], w["bo"][:], ALU.add))
                norm_rows(vec, chain, stats, y[:], y[:], 1e-6, var_ready, rstd_ready, n + 1, settle)
                chain(vec.tensor_tensor(y[:], y[:], w["gamma"][:], ALU.mult))
                chain(vec.tensor_tensor(X[:, n, :], y[:], w["beta"][:], ALU.add))
                assert count[0] == ly.links

            def step(n, first, more):
                wait(vec, "mask_landed", n, 16)
                if not gqa:
                    vec.tensor_scalar(mask[:], mask_u8[:], 1.0, FLT_MAX, ALU.subtract, ALU.mult).then_inc(mask_half, 1)
                    vec.wait_ge(mask_half, n + 1)
                    vec.tensor_scalar(mask[:], mask[:], 10.0, None, ALU.mult).then_inc(s["mask_made"], 1)
                    wait(vec, "mask_made", n, 1)

                def maximum(q, j):
                    if q == quads:
                        return
                    c = 4 * q + j
                    wait(vec, "s_ready", n, c + 1)
                    settle(vec)
                    vec.tensor_tensor_reduce(probs[:, q % 2, j, :], Sb[c % 2][0:L, 0:S], mask[:],
                                             -1.0 if gqa else -ly.scale, FLT_MAX, ALU.add, ALU.min,
                                             neg_max[:, c:c + 1]).then_inc(s["max_ready"], 1)

                def turned(q, c):
                    rows = ROWS[c]
                    wait(vec, "pt_hi", n, 3 * q + c + 1)
                    vec.tensor_tensor(pt_l[0:rows, q % 2, c, :], T[(3 * q + c) % 2][0:rows, 0:4 * L],
                                      pt_h[0:rows, q % 2, c, :], ALU.subtract).then_inc(s["pt_lo"], 1)

                def copy_output(q):
                    wait(vec, "o_ready", n, q + 1)
                    vec.tensor_copy(o[32 * (q % 4):32 * (q % 4) + 32, q // 4, :], O[q % 2][0:32, 0:4 * L])\
                       .then_inc(s["o_copied"], 1)

                for j in range(4):
                    maximum(0, j)
                if gqa and not first:
                    new_rows(n - 1)
                for q in range(quads):
                    maximum(q + 1, 0)
                    maximum(q + 1, 1)
                    turned(q, 0)
                    maximum(q + 1, 2)
                    turned(q, 1)
                    maximum(q + 1, 3)
                    if q >= 1:
                        copy_output(q - 1)
                    turned(q, 2)
                    if more:
                        project(n + 1, lambda name, k: bank_of((name, 1, k), more), q)
                wait(vec, "exp_done", n, heads)
                vec.reciprocal(inv_sum[:], row_sum[:]).then_inc(s["inv_made"], 1)
                copy_output(quads - 1)
                if more:
                    values(n + 1, lambda name, k: bank_of((name, 1, k), more), value_chain(n + 1))
                wait(vec, "o_copied", n, quads)
                for half in range(ly.halves):
                    wait(vec, "spread", n, half + 1)
                    vec.tensor_tensor(o[:, half, :], bank_of(("o_scaled", 0, half + 1), more)[:, 0:4 * L], o[:, half, :],
                                      ALU.mult).then_inc(s["o_scaled"], 1)
                wait(vec, "o_hi", n, 1)
                vec.tensor_tensor(o_l[:], o[:], o_h[:], ALU.subtract).then_inc(s["o_lo"], 1)
                wait(vec, "out_ready", n, 1)
                res = bank_of(("x_done", 0, 1), more)[0:L, :]
                if gqa:
                    vec.tensor_tensor(y[:], res, X[:, n, :], ALU.add).then_inc(s["x_done"], 1)
                else:
                    vec.scalar_tensor_tensor(X[:, n, :], res, w["tanh_gate"][:], X[:, n, :], ALU.mult, ALU.add)\
                       .then_inc(s["x_done"], 1)

            first = lambda name, k: A[FIRST.index((name, k)) % 2]
            project(0, first)
            values(0, first, value_chain(0))
            step(0, True, True)
            with vec.Fori(1, B - 1) as n:
                step(n, False, True)
            step(B - 1, False, False)
            if gqa:
                new_rows(B - 1)


def attend(nc, a, scratch_ctx, scratch_norm, scratch_w, X, ident, minus_half):
    with ExitStack() as ctx:
        def sb(name, shape, dt=F32):
            return ctx.enter_context(nc.sbuf_tensor(name, shape, dt))

        def psum(name):
            return ctx.enter_context(nc.psum_tensor(name, [P, 512], F32))

        def sem(name):
            return ctx.enter_context(nc.semaphore(name))

        h_rows = sb("h_rows", [L, 2, D])
        h_t = sb("h_t", [P, B, DC, L])
        ctx_raw = sb("ctx_raw", [P, DC, KEYS])
        ctx_h, ctx_l = (sb(n, [P, DC, KEYS], F32R) for n in ("ctx_h", "ctx_l"))
        stage = [sb(f"stage{i}", [P, DC, D]) for i in range(2)]
        wq = sb("wq", [P, DC, D])
        wk_h, wk_l, wv_h, wv_l, wo_h, wo_l = (
            sb(n, [P, DC, D], F32R) for n in ("wk_h", "wk_l", "wv_h", "wv_l", "wo_h", "wo_l"))
        q_t = sb("q_t", [P, 4, L])
        k_t = sb("k_t", [P, 4, KEYS])
        v = sb("v", [P, 3, D])
        probs = sb("probs", [L, 2, 4, KEYS])
        probs_t = sb("probs_t", [P, 2, 3, 4 * L])
        o = sb("o", [L, D])
        o_h, o_l = (sb(n, [P, DC, L], F32R) for n in ("o_h", "o_l"))
        y = sb("y", [L, D])
        bv, bo, gamma, beta = (sb(n, [P, D]) for n in ("bv", "bo", "gamma", "beta"))
        bq = sb("bq", [P, 4])
        bk = sb("bk", [P, 4])
        neg_max = sb("neg_max", [L, 4])
        row_sum = sb("row_sum", [L, 4])
        inv_sum = sb("inv_sum", [L, 4])
        stats = sb("stats", [L, 9])

        A = [psum(f"A{i}") for i in range(2)]
        Sb = [psum(f"S{i}") for i in range(3)]
        T = [psum(f"T{i}") for i in range(2)]
        O = psum("O")

        s = {n: sem(n) for n in LAYERS[0].per}
        weights_split, h_made, h_turned, h_copied = (
            sem(n) for n in ("weights_split", "h_made", "h_turned", "h_copied"))
        var_ready, rstd_ready = sem("var_ready"), sem("rstd_ready")
        NORMED = {"L3_1": 0, "L3_2": B}
        staged = [sem("stage0_landed"), sem("stage1_landed")]
        vectors_landed, norm_landed, prep = sem("vectors_landed"), sem("norm_landed"), sem("prep_link")

        VECTORS = {"L3_1": 5, "L3_2": 5}
        NORMS = {"L3_1": 3, "L3_2": 3}

        def vectors_at(i, g):
            before = sum(VECTORS[ly.name] * ly.groups for ly in LAYERS[:i])
            return g * (16 * VECTORS[LAYERS[i].name]) + 16 * (before + VECTORS[LAYERS[i].name])

        def norms_at(i):
            return 16 * sum(NORMS[ly.name] for ly in LAYERS[:i + 1])

        def steps(eng, ly, body):
            if ly.groups == 1:
                with eng.Fori(0, B) as b:
                    body(0, b, b)
            else:
                with eng.Fori(0, ly.groups) as g:
                    with eng.Fori(0, B) as b:
                        body(g, b, g * B + b)

        def groups(eng, ly, body):
            if ly.groups == 1:
                body(0)
            else:
                with eng.Fori(0, ly.groups) as g:
                    body(g)

        settled = sem("attend_settled")

        def settle(eng):
            eng.sem_inc(settled, 1)

        block = ctx.enter_context(nc.Block())

        @block.sync
        def _(sp):
            for i, ly in enumerate(LAYERS):
                pre, post = "L3_xattn_", ly.name[-1]

                def step_loads(b, n, i=i, ly=ly):
                    sp.wait_ge(s["ctx_split"], at(i, "ctx_split", n, 0))
                    settle(sp)
                    src = scratch_ctx[b]
                    sp.dma_start(ctx_raw[:].rearrange("p c k -> p (c k)"), src).then_inc(s["ctx_landed"], 16)

                sp.wait_ge(s["x_done"], at(i, "x_done", 0, 0))
                sp.wait_ge(s["link"], at(i, "link", 0, 0))
                sp.wait_ge(h_made, 1 + B * i)
                for dst, name in (bo, "bo" + post), (gamma, f"ln{post}_scale"), (beta, f"ln{post}_offset"):
                    sp.dma_start(dst[:], rows_of(a[pre + name])).then_inc(norm_landed, 16)

                def group(g, i=i, ly=ly, pre=pre, post=post):
                    n = g * B
                    cols = bass.ds(g * D, D)
                    w = [a[f"{pre}w{x}{post}"].rearrange("(c p) n -> p c n", p=P)[:, :, cols] for x in "qkv"]
                    w.append(a[f"{pre}wo{post}"].rearrange("(g c p) n -> g p c n", g=4, p=P)[g])
                    sp.wait_ge(weights_split, weights_at(i, g, 0))
                    settle(sp)
                    sp.dma_start(stage[0][:], w[1]).then_inc(staged[0], 16)
                    sp.dma_start(stage[1][:], w[2]).then_inc(staged[1], 16)
                    step_loads(0, n)
                    def part(name):
                        return a[pre + name + post].rearrange("(g c p) -> g p c", g=4, p=P)[g]
                    sp.wait_ge(s["q_taken"], at(i, "q_taken", n, 0))
                    settle(sp)
                    sp.dma_start(bq[:, 0:4], part("bq"), allow_slow_non_contiguous=True).then_inc(vectors_landed, 16)
                    sp.wait_ge(s["k_taken"], at(i, "k_taken", n, 0))
                    settle(sp)
                    sp.dma_start(bk[:], part("bk"), allow_slow_non_contiguous=True).then_inc(vectors_landed, 16)
                    sp.wait_ge(s["v_taken"], at(i, "v_taken", n, 0))
                    settle(sp)
                    sp.dma_start(bv[:], a[f"{pre}bv{post}"].rearrange("(g o d) -> g o d", g=4, o=1)[g]
                                 .broadcast_to([P, D])).then_inc(vectors_landed, 16)
                    sp.wait_ge(s["s_ready"], at(i, "s_ready", n, 0))
                    settle(sp)
                    sp.dma_start(k_t[:, :, S:KEYS],
                                 a[f"{pre}bias_k{post}"].rearrange("x y (g c) (p o) -> (x y g) p c o", g=4, o=1)[g],
                                 allow_slow_non_contiguous=True)\
                      .then_inc(vectors_landed, 16)
                    sp.wait_ge(s["o_ready"], at(i, "o_ready", n, 0))
                    settle(sp)
                    sp.dma_start(v[ROWS[2]:ROWS[2] + 1, 2, :],
                                 a[f"{pre}bias_v{post}"].rearrange("x y (g c) p -> (x y g) (c p)", g=4)[
                                     bass.ds(g, 1), :])\
                      .then_inc(vectors_landed, 16)
                    sp.wait_ge(weights_split, weights_at(i, g, 2))
                    settle(sp)
                    sp.dma_start(stage[0][:], w[0]).then_inc(staged[0], 16)
                    sp.wait_ge(weights_split, weights_at(i, g, 4))
                    settle(sp)
                    sp.dma_start(stage[1][:], w[3]).then_inc(staged[1], 16)
                    with sp.Fori(1, B) as b:
                        step_loads(b, n + b)

                groups(sp, ly, group)

        @block.gpsimd
        def _(pool):
            pool.sem_inc(s["ctx_split"], 1)
            pool.sem_inc(weights_split, 1)
            staged_before = [0, 0]
            for i, ly in enumerate(LAYERS):

                def split(hi, lo, raw, done, value):
                    pool.tensor_copy(hi, raw).then_inc(done, 1)
                    pool.wait_ge(done, value)
                    pool.tensor_tensor(lo, raw, hi, ALU.subtract).then_inc(done, 1)

                def split_context(n, i=i):
                    pool.wait_ge(s["ctx_landed"], at(i, "ctx_landed", n, 16))
                    if not isinstance(n, int) or at(i, "v_ready", n, 0) > 0:
                        pool.wait_ge(s["v_ready"], at(i, "v_ready", n, 0))
                    settle(pool)
                    split(ctx_h[:], ctx_l[:], ctx_raw[:], s["ctx_split"], at(i, "ctx_split", n, 1))

                def power(b, ly=ly):
                    pool.wait_ge(var_ready, b + (NORMED[ly.name] + 1))
                    pool.tensor_tensor(stats[:, 8:9], stats[:, 8:9], minus_half[0:L, 0:1], ALU.pow)\
                        .then_inc(rstd_ready, 1)

                with pool.Fori(0, B) as b:
                    power(b)

                def group(g, i=i, ly=ly, base=staged_before[0]):
                    n = g * B

                    def used(name):
                        if i > 0 or not isinstance(n, int):
                            pool.wait_ge(s[name], at(i, name, n, 0))

                    pool.wait_ge(staged[0], g * 32 + base + 16)
                    used("k_ready")
                    settle(pool)
                    split(wk_h[:], wk_l[:], stage[0][:], weights_split, weights_at(i, g, 1))
                    pool.wait_ge(staged[1], g * 32 + base + 16)
                    used("v_ready")
                    settle(pool)
                    split(wv_h[:], wv_l[:], stage[1][:], weights_split,
                          weights_at(i, g, 3))
                    split_context(n)
                    pool.wait_ge(staged[0], g * 32 + base + 32)
                    used("q_ready")
                    settle(pool)
                    pool.tensor_copy(wq[:], stage[0][:]).then_inc(weights_split, 1)
                    pool.wait_ge(staged[1], g * 32 + base + 32)
                    used("out_ready")
                    settle(pool)
                    split(wo_h[:], wo_l[:], stage[1][:], weights_split, weights_at(i, g, 5 + ly.wq_parts))
                    with pool.Fori(1, B) as b:
                        split_context(n + b)

                groups(pool, ly, group)
                staged_before[0] += 32 * ly.groups

        @block.scalar
        def _(act):
            for name in ("k_taken", "exp_done", "pt_first", "ot_hi"):
                act.sem_inc(s[name], 1)
            act.sem_inc(h_copied, 2)
            for i, ly in enumerate(LAYERS):
                with act.Fori(0, B // 2) as pair:
                    for u in range(2):
                        b = pair * 2 + u
                        act.wait_ge(h_turned, b + (B * i + 3))
                        act.activation(h_t[:, b, :, :], A[u][:, 0:DC * L].rearrange("p (c l) -> p c l", c=DC),
                                       ACT.Copy).then_inc(h_copied, 1)

                def step(g, b, n, i=i, ly=ly):
                    act.wait_ge(vectors_landed, vectors_at(i, g))
                    for t in range(ly.kt):
                        act.wait_ge(s["k_ready"], at(i, "k_ready", n, t + 1))
                        act.activation(k_t[:, t, 0:S], A[(1 + t) % 2][:, 0:S], ACT.Identity,
                                       bias=bk[:, t:t + 1]).then_inc(s["k_taken"], 1)

                    def exps(q):
                        for j in range(4):
                            h = 4 * q + j
                            c = ly.heads[h]["n"]
                            act.wait_ge(s["max_ready"], at(i, "max_ready", n, h + 1))
                            src = masked[:, q % 2, j, :] if ly.masked else Sb[h % 3][0:L, 0:KEYS]
                            act.activation(probs[:, q % 2, j, 0:ly.keys], src, ACT.Exp, bias=neg_max[:, c:c + 1],
                                           scale=-1.0 if ly.masked else 1.0, accum_out=row_sum[:, c:c + 1])\
                               .then_inc(s["exp_done"], 1)

                    exps(0)
                    for q in range(ly.quads):
                        act.wait_ge(s["pt_ready"], at(i, "pt_ready", n, 3 * q + 1))
                        act.activation(probs_t[:, q % 2, 0, :], T[3 * q % 2][:, 0:4 * L], ACT.Copy)\
                           .then_inc(s["pt_first"], 1)
                        if q + 1 < ly.quads:
                            exps(q + 1)
                    act.wait_ge(s["ot_ready"], at(i, "ot_ready", n, 1))
                    ot = A[(ly.qt // 4 + ly.kt + 3) % 2]
                    act.activation(o_h[:], ot[:, 0:DC * L].rearrange("p (c l) -> p c l", c=DC), ACT.Copy)\
                       .then_inc(s["ot_hi"], 1)

                steps(act, ly, step)

        @block.tensor
        def _(pe):
            pe.sem_inc(h_turned, 2)

            def product(out, pairs, end=None):
                terms = [(l, r) for (lh, ll), (rh, rl) in pairs for l, r in ((ll, rh), (lh, rl), (lh, rh))]
                for k, (l, r) in enumerate(terms):
                    last = pe.matmul(out, l, r, start=k == 0, stop=k == len(terms) - 1)
                return last

            for i, ly in enumerate(LAYERS):
                pe.wait_ge(s["ot_lo"], at(i, "ot_lo", 0, 0))
                pe.wait_ge(s["x_done"], at(i, "x_done", 0, 0))
                with pe.Fori(0, B // 2) as pair:
                    for u in range(2):
                        b = pair * 2 + u
                        pe.wait_ge(h_made, b + (B * i + 2))
                        pe.wait_ge(h_copied, b + (B * i + 1))
                        for c in range(DC):
                            last = pe.transpose(A[u][:, c * L:(c + 1) * L], h_rows[:, u, c * P:(c + 1) * P],
                                                ident[0:L, 0:L])
                        last.then_inc(h_turned, 1)
                pe.wait_ge(h_copied, B * (i + 1) + 2)

                uses = ["q_taken"] * (ly.qt // 4) + ["k_taken"] * ly.kt + ["v_taken"] * 3 + ["ot_lo", "x_done"]

                def step(g, b, n, i=i, ly=ly, uses=uses):
                    use = [0]

                    def bank():
                        u = use[0]
                        use[0] += 1
                        name = uses[u - 2]
                        count = uses[:u - 1].count(name) if u >= 2 else 0
                        pe.wait_ge(s[name], at(i, name, n, count))
                        return A[u % 2]

                    pe.wait_ge(weights_split, weights_at(i, g, 4 + ly.wq_parts))
                    for t0 in range(0, ly.qt, 4):
                        to = bank()
                        for t in range(t0, t0 + 4):
                            for c in range(DC):
                                last = pe.matmul(to[:, (t - t0) * L:(t - t0 + 1) * L], wq[:, c, t * P:(t + 1) * P],
                                                 h_t[:, b, c, :], start=c == 0, stop=c == DC - 1)
                        last.then_inc(s["q_ready"], 1)
                    pe.wait_ge(s["ctx_split"], at(i, "ctx_split", n, 2))
                    for t in range(ly.kt):
                        to = bank()
                        product(to[:, 0:KEYS],
                                [((wk_h[:, c, t * P:(t + 1) * P], wk_l[:, c, t * P:(t + 1) * P]),
                                  (ctx_h[:, c, :], ctx_l[:, c, :])) for c in range(DC)]).then_inc(s["k_ready"], 1)

                    def scores(q):
                        for h in range(4 * q, 4 * q + 4):
                            x = ly.heads[h]
                            if h == 0:
                                pe.wait_ge(s["q_taken"], at(i, "q_taken", n, ly.qt // 4))
                                pe.wait_ge(s["k_taken"], at(i, "k_taken", n, ly.kt))
                                if ly.last:
                                    pe.wait_ge(vectors_landed, vectors_at(i, g))
                            name = "max_ready" if ly.masked else "exp_done"
                            pe.wait_ge(s[name], at(i, name, n, max(h - 2, 0)))
                            r = slice(x["row"], x["row"] + x["rows"])
                            pe.matmul(Sb[h % 3][0:L, 0:ly.keys], q_t[r, x["q"], :], k_t[r, x["k"], 0:ly.keys],
                                      start=True, stop=True).then_inc(s["s_ready"], 1)

                    def values(t):
                        to = bank()
                        rows = ROWS[t]
                        product(to[0:rows, 0:ly.vw],
                                [((ctx_h[:, c, t * P:t * P + rows], ctx_l[:, c, t * P:t * P + rows]),
                                  (wv_h[:, c, 0:ly.vw], wv_l[:, c, 0:ly.vw])) for c in range(DC)])\
                            .then_inc(s["v_ready"], 1)

                    def turn(q):
                        pe.wait_ge(s["exp_done"], at(i, "exp_done", n, 4 * q + 4))
                        for c, (k0, kn) in enumerate(ly.chunks):
                            k = 3 * q + c
                            if k < 2:
                                pe.wait_ge(s["pt_first"], at(i, "pt_first", n, 0))
                                pe.wait_ge(s["pt_rest"], at(i, "pt_rest", n, 0))
                            elif c == 2:
                                pe.wait_ge(s["pt_first"], at(i, "pt_first", n, q + 1))
                            else:
                                pe.wait_ge(s["pt_rest"], at(i, "pt_rest", n, 2 * (q - 1) + 1 + c))
                            for j in range(4):
                                last = pe.transpose(T[k % 2][0:kn, j * L:(j + 1) * L],
                                                    probs[:, q % 2, j, k0:k0 + kn], ident[0:L, 0:L])
                            last.then_inc(s["pt_ready"], 1)

                    def weigh(q):
                        pe.wait_ge(s["pt_first"], at(i, "pt_first", n, q + 1))
                        pe.wait_ge(s["pt_rest"], at(i, "pt_rest", n, 2 * q + 2))
                        if q == 0:
                            pe.wait_ge(s["v_taken"], at(i, "v_taken", n, 3))
                            pe.wait_ge(s["o_taken"], at(i, "o_taken", n, 0))
                        for j in range(4):
                            x = ly.heads[4 * q + j]
                            for c, (k0, kn) in enumerate(ly.chunks):
                                last = pe.matmul(O[0:L, x["o"]:x["o"] + ly.dh], probs_t[0:kn, q % 2, c, j * L:(j + 1) * L],
                                                 v[0:kn, c, x["v"]:x["v"] + ly.dh], start=c == 0, stop=c == 2)
                        if q == ly.quads - 1:
                            last.then_inc(s["o_ready"], 1)

                    scores(0)
                    values(0)
                    values(1)
                    if ly.quads == 1:
                        turn(0)
                        values(2)
                    else:
                        values(2)
                        for q in range(ly.quads):
                            if q + 1 < ly.quads:
                                scores(q + 1)
                            turn(q)
                            if q >= 1:
                                weigh(q - 1)
                    weigh(ly.quads - 1)
                    to = bank()
                    pe.wait_ge(s["o_taken"], at(i, "o_taken", n, 1))
                    for c in range(DC):
                        last = pe.transpose(to[:, c * L:(c + 1) * L], o[:, c * P:(c + 1) * P], ident[0:L, 0:L])
                    last.then_inc(s["ot_ready"], 1)
                    to = bank()
                    pe.wait_ge(weights_split, weights_at(i, g, 6 + ly.wq_parts))
                    pe.wait_ge(s["ot_lo"], at(i, "ot_lo", n, 1))
                    product(to[0:L, :], [((o_h[:, c, :], o_l[:, c, :]), (wo_h[:, c, :], wo_l[:, c, :]))
                                         for c in range(DC)]).then_inc(s["out_ready"], 1)

                steps(pe, ly, step)

        @block.vector
        def _(vec):
            for name in ("q_taken", "v_taken", "max_ready", "pt_rest", "o_taken", "ot_lo", "x_done", "link"):
                vec.sem_inc(s[name], 1)
            vec.sem_inc(h_made, 1)

            for i, ly in enumerate(LAYERS):
                vec.wait_ge(s["x_done"], at(i, "x_done", 0, 0))
                vec.wait_ge(s["link"], at(i, "link", 0, 0))
                if NORMS[ly.name]:
                    vec.wait_ge(norm_landed, norms_at(i))
                with vec.Fori(0, B // 2) as pair:
                    for u in range(2):
                        b = pair * 2 + u
                        vec.wait_ge(h_turned, b + (B * i + 1))
                        if not ly.last:
                            vec.tensor_copy(h_rows[:, u, :], X[:, b, :]).then_inc(h_made, 1)
                            continue
                        before = PREP_LINKS * B * i
                        links = [0]

                        def chain(ins, settle=None, b=b, before=before, links=links):
                            links[0] += 1
                            ins.then_inc(prep, 1)
                            vec.wait_ge(prep, b * PREP_LINKS + (before + links[0]))
                            if settle:
                                settle(vec)

                        norm_rows(vec, chain, stats, X[:, b, :], h_rows[:, u, :], 1e-5, var_ready, rstd_ready,
                                  b + (NORMED[ly.name] + 1), settle)
                        chain(vec.tensor_tensor(h_rows[:, u, :], h_rows[:, u, :], gamma[0:L, :], ALU.mult))
                        chain(vec.tensor_tensor(X[:, b, :], X[:, b, :], bo[0:L, :], ALU.add))
                        vec.tensor_tensor(h_rows[:, u, :], h_rows[:, u, :], beta[0:L, :], ALU.add).then_inc(h_made, 1)
                        assert links[0] == PREP_LINKS

                def step(g, b, n, i=i, ly=ly):
                    links = [0]

                    def chain(ins, settle=None):
                        links[0] += 1
                        ins.then_inc(s["link"], 1)
                        vec.wait_ge(s["link"], at(i, "link", n, links[0]))
                        if settle:
                            settle(vec)

                    if ly.masked:
                        vec.wait_ge(s["mask_landed"], at(i, "mask_landed", n, 16))
                    if ly.masked and not ly.gqa:
                        chain(vec.tensor_scalar(mask_f[:], mask_u8[:], 1.0, FLT_MAX, ALU.subtract, ALU.mult))
                        vec.tensor_scalar(mask[:], mask_f[:], 10.0, None, ALU.mult).then_inc(s["mask_made"], 1)
                        vec.wait_ge(s["mask_made"], at(i, "mask_made", n, 1))
                    if VECTORS[ly.name]:
                        vec.wait_ge(vectors_landed, vectors_at(i, g))
                    for k in range(ly.qt // 4):
                        vec.wait_ge(s["q_ready"], at(i, "q_ready", n, k + 1))
                        for t in range(4 * k, 4 * k + 4):
                            last = vec.tensor_scalar(q_t[:, t, :], A[k % 2][:, (t - 4 * k) * L:(t - 4 * k + 1) * L],
                                                     0.0 if ly.name == "L2" else bq[:, t:t + 1], ly.scale,
                                                     ALU.add, ALU.mult)
                        last.then_inc(s["q_taken"], 1)

                    def maxima(q):
                        for j in range(4):
                            h = 4 * q + j
                            c = ly.heads[h]["n"]
                            vec.wait_ge(s["s_ready"], at(i, "s_ready", n, h + 1))
                            if ly.masked:
                                settle(vec)
                                vec.tensor_tensor_reduce(masked[:, q % 2, j, :], Sb[h % 3][0:L, 0:S], mask[:], -1.0,
                                                         FLT_MAX, ALU.add, ALU.min, neg_max[:, c:c + 1])\
                                   .then_inc(s["max_ready"], 1)
                            else:
                                vec.tensor_reduce(neg_max[:, c:c + 1], Sb[h % 3][0:L, 0:KEYS], AX.X, ALU.max,
                                                  negate=True).then_inc(s["max_ready"], 1)

                    def values(t):
                        vec.wait_ge(s["v_ready"], at(i, "v_ready", n, t + 1))
                        src = A[(ly.qt // 4 + ly.kt + t) % 2][0:ROWS[t], 0:ly.vw]
                        dst = v[0:ROWS[t], t, 0:ly.vw]
                        if ly.name == "L2":
                            vec.tensor_copy(dst, src).then_inc(s["v_taken"], 1)
                        else:
                            vec.tensor_tensor(dst, src, bv[0:ROWS[t], 0:ly.vw], ALU.add).then_inc(s["v_taken"], 1)

                    def turned(q):
                        for c in (1, 2):
                            kn = ly.chunks[c][1]
                            vec.wait_ge(s["pt_ready"], at(i, "pt_ready", n, 3 * q + c + 1))
                            vec.tensor_copy(probs_t[0:kn, q % 2, c, :], T[(3 * q + c) % 2][0:kn, 0:4 * L])\
                               .then_inc(s["pt_rest"], 1)

                    maxima(0)
                    values(0)
                    values(1)
                    if ly.quads == 1:
                        turned(0)
                        values(2)
                    else:
                        values(2)
                        for q in range(ly.quads):
                            if q + 1 < ly.quads:
                                maxima(q + 1)
                            turned(q)
                    heads = len(ly.heads)
                    vec.wait_ge(s["exp_done"], at(i, "exp_done", n, heads))
                    chain(vec.reciprocal(inv_sum[:, 0:heads], row_sum[:, 0:heads]))
                    vec.wait_ge(s["o_ready"], at(i, "o_ready", n, 1))
                    vec.tensor_tensor(o[:].rearrange("l (h d) -> l h d", h=heads),
                                      O[0:L, :].rearrange("l (h d) -> l h d", h=heads),
                                      inv_sum[:, 0:heads].unsqueeze(2).broadcast_to([L, heads, ly.dh]), ALU.mult)\
                       .then_inc(s["o_taken"], 1)
                    vec.wait_ge(s["ot_hi"], at(i, "ot_hi", n, 1))
                    u = ly.qt // 4 + ly.kt + 3
                    vec.tensor_tensor(o_l[:], A[u % 2][:, 0:DC * L].rearrange("p (c l) -> p c l", c=DC), o_h[:],
                                      ALU.subtract).then_inc(s["ot_lo"], 1)
                    vec.wait_ge(s["out_ready"], at(i, "out_ready", n, 1))
                    res = A[(u + 1) % 2][0:L, :]
                    if ly.last:
                        vec.tensor_tensor(X[:, b, :], res, X[:, b, :], ALU.add).then_inc(s["x_done"], 1)
                    elif ly.name == "L2":
                        if i == 2:
                            vec.wait_ge(gate_done, 1)
                        vec.scalar_tensor_tensor(X[:, b, :], res, tanh_gate[:, 0:1], X[:, b, :], ALU.mult, ALU.add)\
                           .then_inc(s["x_done"], 1)
                    else:
                        vec.tensor_tensor(y[:], res, X[:, b, :], ALU.add).then_inc(s["x_done"], 1)
                        vec.wait_ge(s["x_done"], at(i, "x_done", n, 1))
                        chain(vec.tensor_tensor(y[:], y[:], bo[0:L, :], ALU.add))
                        norm_rows(vec, chain, stats, y[:], y[:], 1e-6, var_ready, rstd_ready, b + (NORMED[ly.name] + 1), settle)
                        chain(vec.tensor_tensor(y[:], y[:], gamma[0:L, :], ALU.mult))
                        chain(vec.tensor_tensor(X[:, b, :], y[:], beta[0:L, :], ALU.add))
                    assert links[0] == ly.per["link"]

                steps(vec, ly, step)


def feed_forward(nc, a, X, ident, minus_half, out):
    HB = B // 2
    HL = HB * L
    with ExitStack() as ctx:
        def sb(name, shape, dt=F32):
            return ctx.enter_context(nc.sbuf_tensor(name, shape, dt))

        def psum(name):
            return ctx.enter_context(nc.psum_tensor(name, [P, 512], F32))

        def sem(name):
            return ctx.enter_context(nc.semaphore(name))

        rows = sb("mlp_rows", [L, 2, D])
        in_h, in_l = (sb(n, [P, B, DC, L], F32R) for n in ("in_h", "in_l"))
        gamma, beta, b2 = (sb(n, [L, D]) for n in ("mlp_gamma", "mlp_beta", "b2"))
        b1 = sb("b1", [P, FT])
        w1_raw = sb("w1_raw", [P, 2, DC, P])
        w2_raw = sb("w2_raw", [P, 2, D])
        w1_h, w1_l = (sb(n, [P, 2, DC, P], F32R) for n in ("w1_h", "w1_l"))
        w2_h, w2_l = (sb(n, [P, 2, D], F32R) for n in ("w2_h", "w2_l"))
        g = sb("g", [P, 2, HL])
        g_h, g_l = (sb(n, [P, 2, HL], F32R) for n in ("g_h", "g_l"))
        y = sb("mlp_y", [L, HB, D])
        stats = sb("mlp_stats", [L, 9])
        A = [psum(f"mlp_A{i}") for i in range(2)]
        R = [psum(f"mlp_R{i}") for i in range(HB)]
        (vectors_landed, link, rows_made, rows_turned, rows_hi, rows_lo, w_hi, w_lo, fc1_ready, gelu_done, g_hi, g_lo,
         fc2_done, taken, y_made, stored, var_ready, rstd_ready) = (sem("mlp_" + n) for n in (
             "vectors_landed", "link", "rows_made", "rows_turned", "rows_hi", "rows_lo", "w_hi", "w_lo", "fc1_ready",
             "gelu_done", "g_hi", "g_lo", "fc2_done", "taken", "y_made", "stored", "var_ready",
             "rstd_ready"))
        w_landed = [sem(f"mlp_w_landed{u}") for u in range(2)]

        settled = sem("mlp_settled")

        def settle(eng):
            eng.sem_inc(settled, 1)

        block = ctx.enter_context(nc.Block())

        def pairs(eng, half, body):
            body(True, False, half * (FT // 2))
            with eng.Fori(1, FT // 2 - 1) as pair:
                body(False, False, half * (FT // 2) + pair)
            body(False, True, half * (FT // 2) + (FT // 2 - 1))

        @block.sync
        def _(sp):
            for dst, name in ((gamma, "ln_mlp_scale"), (beta, "ln_mlp_offset"), (b2, "b_fc2")):
                sp.dma_start(dst[:], rows_of(a["L3_xattn_" + name], L)).then_inc(vectors_landed, 16)
            sp.dma_start(b1[:], a["L3_xattn_b_fc1"].rearrange("(t p) -> p t", p=P),
                         allow_slow_non_contiguous=True).then_inc(vectors_landed, 16)
            sp.sem_inc(stored, 16)
            w1 = a["L3_xattn_w_fc1"].rearrange("(c p) (t n) -> t p c n", p=P, n=P)
            w2 = a["L3_xattn_w_fc2"].rearrange("(t p) n -> t p n", p=P)
            with sp.Fori(0, 2) as half:
                with sp.Fori(0, FT // 2) as pair:
                    for u in range(2):
                        t = pair * 2 + u
                        sp.wait_ge(w_lo, half * (2 * FT) + t * 2 + 1)
                        settle(sp)
                        sp.dma_start(w1_raw[:, u, :, :], w1[t]).then_inc(w_landed[u], 16)
                        sp.dma_start(w2_raw[:, u, :], w2[t]).then_inc(w_landed[u], 16)
                for j in range(HB):
                    sp.wait_ge(y_made, half * HB + (j + 1))
                    settle(sp)
                    sp.dma_start(out[half * HB + j], y[:, j, :]).then_inc(stored, 16)
            sp.wait_ge(stored, 16 * (1 + B))

        @block.gpsimd
        def _(pool):
            with pool.Fori(0, B) as b:
                pool.wait_ge(var_ready, b + 1)
                pool.tensor_tensor(stats[:, 8:9], stats[:, 8:9], minus_half[0:L, 0:1], ALU.pow)\
                    .then_inc(rstd_ready, 1)

        @block.scalar
        def _(act):
            act.sem_inc(rows_hi, 2)
            act.sem_inc(gelu_done, 2)
            with act.Fori(0, B // 2) as pair:
                for u in range(2):
                    b = pair * 2 + u
                    act.wait_ge(rows_turned, b + 3)
                    act.activation(in_h[:, b], A[u][:, 0:DC * L].rearrange("p (c l) -> p c l", c=DC), ACT.Copy)\
                       .then_inc(rows_hi, 1)
            act.wait_ge(vectors_landed, 64)
            with act.Fori(0, 2) as half:
                def split(u, k):
                    act.wait_ge(w_landed[u], (k - u) * 16 + 32)
                    settle(act)
                    act.activation(w1_h[:, u], w1_raw[:, u], ACT.Copy).then_inc(w_hi, 1)
                    act.wait_ge(fc2_done, k + 1)
                    act.activation(w2_h[:, u], w2_raw[:, u], ACT.Copy).then_inc(w_hi, 1)

                def pair_of(pair, more):
                    for u in range(2):
                        t = pair * 2 + u
                        k = half * FT + t
                        act.wait_ge(fc1_ready, k + 1)
                        act.wait_ge(fc2_done, k + 1)
                        act.activation(g[:, u, :], A[u][:, 0:HL], ACT.Gelu, bias=b1[:, bass.ds(t, 1)])\
                           .then_inc(gelu_done, 1)
                        act.wait_ge(gelu_done, k + 3)
                        act.activation(g_h[:, u, :], g[:, u, :], ACT.Copy).then_inc(g_hi, 1)
                        if more:
                            split(u, k + 2)

                split(0, half * FT)
                split(1, half * FT + 1)
                with act.Fori(0, FT // 2 - 1) as pair:
                    pair_of(pair, True)
                pair_of(FT // 2 - 1, False)

        @block.tensor
        def _(pe):
            pe.sem_inc(rows_turned, 2)
            pe.sem_inc(fc2_done, 2)
            with pe.Fori(0, B // 2) as pair:
                for u in range(2):
                    b = pair * 2 + u
                    pe.wait_ge(rows_made, b + 1)
                    pe.wait_ge(rows_hi, b + 1)
                    pe.wait_ge(rows_lo, b + 1)
                    for c in range(DC):
                        last = pe.transpose(A[u][:, c * L:(c + 1) * L], rows[:, u, c * P:(c + 1) * P], ident[0:L, 0:L])
                    last.then_inc(rows_turned, 1)
            pe.wait_ge(rows_lo, B + 2)
            with pe.Fori(0, 2) as half:
                def second(u, k, first, last):
                    pe.wait_ge(w_lo, k * 2 + 5)
                    pe.wait_ge(g_lo, k + 1)
                    if first:
                        pe.wait_ge(taken, half * HB + 1)
                    for j in range(HB):
                        cols = slice(j * L, (j + 1) * L)
                        terms = [(g_l, w2_h), (g_h, w2_l), (g_h, w2_h)]
                        for m, (l, r) in enumerate(terms):
                            mm = pe.matmul(R[j][0:L, :], l[:, u, cols], r[:, u, :], start=first and m == 0,
                                           stop=last and m == 2)
                    mm.then_inc(fc2_done, 1)

                def pair_of(first, last, pair):
                    for u in range(2):
                        k = pair * 2 + u
                        pe.wait_ge(w_lo, k * 2 + 4)
                        pe.wait_ge(gelu_done, k + 1)
                        terms = [(l[:, u, c, :], r[:, bass.ds(half * HB, HB), c, :]) for c in range(DC)
                                 for l, r in ((w1_l, in_h), (w1_h, in_l), (w1_h, in_h))]
                        for m, (l, r) in enumerate(terms):
                            mm = pe.matmul(A[u][:, 0:HL], l, r, start=m == 0, stop=m == len(terms) - 1)
                        mm.then_inc(fc1_ready, 1)
                        if not (first and u == 0):
                            second(1 - u, k - 1, first and u == 1, False)
                    if last:
                        second(1, pair * 2 + 1, False, True)

                pairs(pe, half, pair_of)

        @block.vector
        def _(vec):
            vec.sem_inc(rows_lo, 2)
            vec.sem_inc(taken, 1)
            vec.sem_inc(w_lo, 3)
            vec.wait_ge(vectors_landed, 64)
            with vec.Fori(0, B // 2) as pair:
                for u in range(2):
                    b = pair * 2 + u
                    links = [0]

                    def chain(ins, settle=None, b=b, links=links):
                        links[0] += 1
                        ins.then_inc(link, 1)
                        vec.wait_ge(link, b * 4 + links[0])
                        if settle:
                            settle(vec)

                    vec.wait_ge(rows_turned, b + 1)
                    norm_rows(vec, chain, stats, X[:, b, :], rows[:, u, :], 1e-5, var_ready, rstd_ready, b + 1,
                              settle)
                    chain(vec.tensor_tensor(rows[:, u, :], rows[:, u, :], gamma[:], ALU.mult))
                    vec.tensor_tensor(rows[:, u, :], rows[:, u, :], beta[:], ALU.add).then_inc(rows_made, 1)
                    vec.wait_ge(rows_hi, b + 3)
                    vec.tensor_tensor(in_l[:, b], A[u][:, 0:DC * L].rearrange("p (c l) -> p c l", c=DC), in_h[:, b],
                                      ALU.subtract).then_inc(rows_lo, 1)
            with vec.Fori(0, 2) as half:
                def split(u, k):
                    vec.wait_ge(w_hi, k * 2 + 1)
                    vec.tensor_tensor(w1_l[:, u], w1_raw[:, u], w1_h[:, u], ALU.subtract).then_inc(w_lo, 1)
                    vec.wait_ge(w_hi, k * 2 + 2)
                    vec.tensor_tensor(w2_l[:, u], w2_raw[:, u], w2_h[:, u], ALU.subtract).then_inc(w_lo, 1)

                def pair_of(pair, more):
                    for u in range(2):
                        k = half * FT + pair * 2 + u
                        vec.wait_ge(g_hi, k + 1)
                        vec.tensor_tensor(g_l[:, u, :], g[:, u, :], g_h[:, u, :], ALU.subtract).then_inc(g_lo, 1)
                        if more:
                            split(u, k + 2)

                split(0, half * FT)
                split(1, half * FT + 1)
                with vec.Fori(0, FT // 2 - 1) as pair:
                    pair_of(pair, True)
                pair_of(FT // 2 - 1, False)
                vec.wait_ge(fc2_done, half * FT + (FT + 2))
                vec.wait_ge(stored, half * (16 * HB) + 16)
                for j in range(HB):
                    b = half * HB + j
                    vec.tensor_tensor(y[:, j, :], R[j][0:L, :], X[:, b, :], ALU.add).then_inc(taken, 1)
                    vec.wait_ge(taken, b + 2)
                    vec.tensor_tensor(y[:, j, :], y[:, j, :], b2[:], ALU.add).then_inc(y_made, 1)


def kernel(**inputs):
    import numpy as _np
    import concourse.bacc as _bacc
    from concourse import mybir as _mybir
    from concourse.bass_utils import run_bass_kernel_spmd as _run

    nc = _bacc.Bacc("TRN2", target_bir_lowering=False, num_devices=1)
    arrays, args = {}, {}
    for name, value in inputs.items():
        array = _np.ascontiguousarray(value)
        if array.dtype == _np.bool_:
            array = array.view(_np.uint8)
        arrays[f"in_{name}"] = array
        args[name] = nc.dram_tensor(f"in_{name}", array.shape, _mybir.dt.from_np(array.dtype),
                                    kind="ExternalInput").ap()
    out = nc.dram_tensor("out", [B, L, D], F32, kind="ExternalOutput").ap()
    build(nc, args, out)
    r = _run(nc, [arrays], core_ids=[0])
    return r.results[0]["out"]
```

```python
from contextlib import ExitStack

import concourse.bass as bass
from concourse import mybir

F32 = mybir.dt.float32
F32R = mybir.dt.float32r
U8 = mybir.dt.uint8
ALU = mybir.AluOpType
ACT = mybir.ActivationFunctionType
AX = mybir.AxisListType

P = 128
B, L, D, S = 8, 112, 512, 375
DC = D // P
KEYS = S + 1
ROWS = [P, P, S - 2 * P]
F = 2048
FT = F // P
FLT_MAX = 3.4e38




def rows_of(vector, n=P):
    return vector.rearrange("(o d) -> o d", o=1).broadcast_to([n, D])


def build(nc, a, out):
    scratch_ctx = nc.dram_tensor("ctx_transposed", [B, P, DC * KEYS], F32, kind="Internal").ap()
    scratch_norm = nc.dram_tensor("ctx_norm_transposed", [B, P, DC * KEYS], F32, kind="Internal").ap()
    scratch_w = nc.dram_tensor("gated_weights_transposed", [4, D, D], F32, kind="Internal").ap()
    with ExitStack() as ctx:
        X = ctx.enter_context(nc.sbuf_tensor("X", [L, B, D], F32))
        ident = ctx.enter_context(nc.sbuf_tensor("ident", [P, P], F32))
        minus_half = ctx.enter_context(nc.sbuf_tensor("minus_half", [P, 3], F32))
        prepare_context(nc, a, scratch_ctx, scratch_norm, scratch_w, X, ident, minus_half)
        for ly in (Small("L0", True, 0.25), Small("L1", True, 0.25), Small("L2", False, 32 ** -0.5)):
            small_attention(nc, a, ly, scratch_ctx if ly.gqa else scratch_norm, scratch_w, X, ident, minus_half)
        wide_attention(nc, a, scratch_ctx, X, ident, minus_half)
        feed_forward(nc, a, X, ident, minus_half, out)


def prepare_context(nc, a, scratch_ctx, scratch_norm, scratch_w, X, ident, minus_half):
    with ExitStack() as ctx:
        def sb(name, shape, dt=F32):
            return ctx.enter_context(nc.sbuf_tensor(name, shape, dt))

        def sem(name):
            return ctx.enter_context(nc.semaphore(name))

        nat = sb("nat", [P, 2, 3, D])
        normed = sb("normed", [P, 3, D])
        ctx_t = sb("ctx_t", [P, DC, KEYS])
        norm_t = sb("norm_t", [P, DC, KEYS])
        gamma = sb("ctx_gamma", [P, DC])
        beta = sb("ctx_beta", [P, DC])
        stats = sb("ctx_stats", [P, 3, 6])
        moments = sb("ctx_moments", [P, 3, 2])
        rstd = sb("ctx_rstd", [P, 3])
        w_nat = sb("w_nat", [P, 4, DC, D])
        w_t = sb("w_t", [P, 4, DC, D])
        bank = [ctx.enter_context(nc.psum_tensor(f"ctx_bank{i}", [P, 512], F32)) for i in range(8)]
        nat_landed = [sem(f"nat{half}_landed") for half in range(2)]
        vectors_landed, w_landed = sem("ctx_vectors_landed"), sem("w_landed")
        var_ready, rstd_ready = sem("ctx_var_ready"), sem("ctx_rstd_ready")
        cleared, ident_made, link = sem("cleared"), sem("ident_made"), sem("ctx_link")
        normed_ready, ctx_turned, norm_turned = sem("normed_ready"), sem("ctx_turned"), sem("norm_turned")
        ctx_copied, norm_copied = sem("ctx_copied"), sem("norm_copied")
        ctx_stored, norm_stored, w_stored = sem("ctx_stored"), sem("norm_stored"), sem("w_stored")
        w_turned, w_copied, x_landed = sem("w_turned"), sem("w_copied"), sem("x_landed")

        settled = sem("head_settled")

        def settle(eng):
            eng.sem_inc(settled, 1)

        LINKS = 6
        block = ctx.enter_context(nc.Block())

        @block.sync
        def _(sp):
            sp.sem_inc(ctx_stored, 16)
            sp.sem_inc(norm_stored, 16)
            for dst, name in (gamma, "L2_xattn_ln_gamma"), (beta, "L2_xattn_ln_beta"):
                sp.dma_start(dst[:], a[name].rearrange("(c p) -> p c", p=P), allow_slow_non_contiguous=True)\
                  .then_inc(vectors_landed, 16)
            sp.wait_ge(cleared, 1)

            def load(b, half):
                c = a["ctx_2048"]
                sp.dma_start(nat[:, half, 0:2, :], c[b, 0:2 * P, :].rearrange("(t p) d -> p t d", p=P))\
                  .then_inc(nat_landed[half], 16)
                sp.dma_start(nat[0:ROWS[2], half, 2, :], c[b, 2 * P:S, :]).then_inc(nat_landed[half], 16)

            def store(b):
                sp.wait_ge(ctx_copied, 4 * b + 5)
                sp.dma_start(scratch_ctx[b], ctx_t[:].rearrange("p c k -> p (c k)")).then_inc(ctx_stored, 16)
                sp.wait_ge(norm_copied, 4 * b + 5)
                sp.dma_start(scratch_norm[b], norm_t[:].rearrange("p c k -> p (c k)")).then_inc(norm_stored, 16)

            load(0, 0)
            sp.dma_start(X[:], a["x"].rearrange("b l d -> l b d")).then_inc(x_landed, 16)
            for i, n in enumerate(("Wq", "Wk", "Wv", "Wo")):
                sp.dma_start(w_nat[:, i, :, :], a[f"L2_xattn_{n}"].rearrange("(t p) d -> p t d", p=P))\
                  .then_inc(w_landed, 16)
            load(1, 1)
            with sp.Fori(0, B // 2 - 1) as pair:
                for half in range(2):
                    store(pair * 2 + half)
                    load(pair * 2 + half + 2, half)
            store(B - 2)
            store(B - 1)
            for i in range(4):
                sp.wait_ge(w_copied, 4 * (i + 1))
                sp.dma_start(scratch_w[i].rearrange("(c p) n -> p c n", p=P), w_t[:, i, :, :])\
                  .then_inc(w_stored, 16)
            sp.wait_ge(ctx_stored, 16 * (1 + B))
            sp.wait_ge(norm_stored, 16 * (1 + B))
            sp.wait_ge(w_stored, 16 * 4)
            sp.wait_ge(x_landed, 16)

        @block.gpsimd
        def _(pool):
            pool.memset(ident[:], 0.0).then_inc(ident_made, 1)
            pool.wait_ge(ident_made, 1)
            pool.affine_select(out=ident[:], in_=ident[:], compare_op=ALU.not_equal, fill=1.0, base=0,
                               pattern=[[-1, P]], channel_multiplier=1).then_inc(ident_made, 1)
            pool.memset(minus_half[:], -0.5).then_inc(ident_made, 1)
            pool.wait_ge(ident_made, 3)
            with pool.Fori(0, B) as b:
                pool.wait_ge(var_ready, b + 1)
                pool.tensor_tensor(rstd[:], rstd[:], minus_half[:], ALU.pow).then_inc(rstd_ready, 1)

        @block.vector
        def _(vec):
            vec.sem_inc(norm_copied, 1)
            vec.memset(nat[:, :, 2, :], 0.0).then_inc(cleared, 1)
            vec.memset(ctx_t[:, :, S:KEYS], 0.0).then_inc(cleared, 1)
            vec.memset(norm_t[:, :, S:KEYS], 0.0).then_inc(cleared, 1)
            vec.wait_ge(vectors_landed, 32)
            with vec.Fori(0, B // 2) as pair:
                for half in range(2):
                    b = pair * 2 + half
                    x = nat[:, half, :, :]
                    vec.wait_ge(nat_landed[half], 32 * pair + 32)
                    for t in range(3):
                        vec.bn_stats(stats[:, t, :], x[:, t, :]).then_inc(link, 1)
                    vec.wait_ge(link, LINKS * b + 3)
                    settle(vec)
                    for t in range(3):
                        vec.bn_aggr(moments[:, t, :], stats[:, t, :]).then_inc(link, 1)
                    vec.wait_ge(link, LINKS * b + 6)
                    vec.tensor_scalar(rstd[:], moments[:, :, 1], 1e-5, None, ALU.add).then_inc(var_ready, 1)
                    vec.wait_ge(rstd_ready, b + 1)
                    if half == 1:
                        vec.wait_ge(norm_turned, 4 * b)
                    else:
                        vec.wait_ge(norm_copied, 4 * b + 1)
                    for t in range(3):
                        last = vec.tensor_scalar(normed[:, t, :], x[:, t, :], moments[:, t, 0:1], rstd[:, t:t + 1],
                                                 ALU.subtract, ALU.mult)
                    last.then_inc(normed_ready, 1)
                    vec.wait_ge(norm_stored, 16 * b + 16)
                    for c in range(DC):
                        vec.wait_ge(norm_turned, 4 * b + c + 1)
                        vec.tensor_scalar(norm_t[:, c, 0:S], bank[4 + c][:, 0:S], gamma[:, c:c + 1], beta[:, c:c + 1],
                                          ALU.mult, ALU.add).then_inc(norm_copied, 1)

        @block.scalar
        def _(act):
            act.sem_inc(ctx_copied, 1)
            act.wait_ge(cleared, 3)
            with act.Fori(0, B) as b:
                act.wait_ge(ctx_stored, 16 * b + 16)
                for c in range(DC):
                    act.wait_ge(ctx_turned, 4 * b + c + 1)
                    act.activation(ctx_t[:, c, 0:S], bank[c][:, 0:S], ACT.Copy).then_inc(ctx_copied, 1)
            for n in range(16):
                act.wait_ge(w_turned, n + 1)
                act.activation(w_t[:, n // 4, n % 4, :], bank[n % 8][:, :], ACT.Copy).then_inc(w_copied, 1)

        @block.tensor
        def _(pe):
            pe.wait_ge(ident_made, 2)
            with pe.Fori(0, B // 2) as pair:
                for half in range(2):
                    b = pair * 2 + half
                    pe.wait_ge(nat_landed[half], 32 * pair + 32)
                    pe.wait_ge(ctx_copied, 4 * b + 1)
                    for c in range(DC):
                        for t in range(3):
                            last = pe.transpose(bank[c][:, t * P:t * P + ROWS[t]],
                                                nat[0:ROWS[t], half, t, c * P:(c + 1) * P],
                                                ident[0:ROWS[t], 0:ROWS[t]])
                        last.then_inc(ctx_turned, 1)
                    pe.wait_ge(normed_ready, b + 1)
                    pe.wait_ge(norm_copied, 4 * b + 1)
                    for c in range(DC):
                        for t in range(3):
                            last = pe.transpose(bank[4 + c][:, t * P:t * P + ROWS[t]],
                                                normed[0:ROWS[t], t, c * P:(c + 1) * P],
                                                ident[0:ROWS[t], 0:ROWS[t]])
                        last.then_inc(norm_turned, 1)
            pe.wait_ge(ctx_copied, 4 * B + 1)
            pe.wait_ge(norm_copied, 4 * B + 1)
            for n in range(16):
                i, c = n // 4, n % 4
                if c == 0:
                    pe.wait_ge(w_landed, 64)
                if n >= 8:
                    pe.wait_ge(w_copied, n - 7)
                for t in range(DC):
                    last = pe.transpose(bank[n % 8][:, t * P:(t + 1) * P], w_nat[:, i, t, c * P:(c + 1) * P], ident[:])
                last.then_inc(w_turned, 1)


class Small:

    def __init__(self, name, gqa, scale):
        self.name, self.gqa, self.scale = name, gqa, scale
        self.heads = 32 if gqa else 16
        self.quads = self.heads // 4
        self.qt = 8 if gqa else 4
        self.kt = 1 if gqa else 4
        self.vw = P if gqa else D
        self.halves = self.quads // 4
        work = [("q", k, t) for k in range(self.qt // 4) for t in range(4)]
        work += [("o", 0, t) for t in range(8)] if gqa else []
        work += [("k", t, p) for t in range(self.kt) for p in range(3)]
        slots = 3 * (5 if gqa else 4)
        slot = [i * slots // len(work) for i in range(len(work))]
        self.fill = [[w for w, at in zip(work, slot) if at == n] for n in range(3 * self.quads)]
        self.query_after = [slot[work.index(("q", k, 3))] // 3 for k in range(self.qt // 4)]
        self.key_after = [slot[work.index(("k", t, 2))] // 3 for t in range(self.kt)]
        self.output_after = slot[work.index(("o", 0, 7))] // 3 if gqa else None
        q, s = self.qt // 4, self.quads
        self.per = dict(
            q_ready=q, k_ready=self.kt, v_ready=3, s_ready=self.heads, pt_ready=3 * s, o_ready=s,
            inv_turned=1, spread=self.halves, out_ready=1,
            ctx_landed=16, mask_landed=16, q_stacked=16 * 12, k_stacked=16 * 12,
            q_hi=q, k_hi=self.kt, v_hi=3, exp_done=self.heads, pt_hi=3 * s, inv_copied=1, o_hi=1,
            q_lo=q, k_lo=self.kt, v_taken=3, max_ready=self.heads, pt_lo=3 * s, o_copied=s, inv_made=1,
            o_scaled=self.halves, o_lo=1, x_done=1, mask_made=1, stat_made=1, moment_made=1, var_ready=1,
            normed=1,
            ctx_split=2, rstd_ready=1, with_gamma=1, row_made=1)

    ZERO = ("q_ready", "k_ready", "v_ready", "s_ready", "pt_ready", "o_ready", "inv_turned", "spread",
            "out_ready", "ctx_landed", "mask_landed", "stat_made", "moment_made", "var_ready", "normed",
            "rstd_ready", "with_gamma")
    BY = dict(
        act=("q_hi", "k_hi", "v_hi", "exp_done", "pt_hi", "inv_copied", "o_hi"),
        vec=("q_lo", "k_lo", "v_taken", "max_ready", "pt_lo", "o_copied", "inv_made", "o_scaled", "o_lo", "x_done",
             "mask_made"),
        pool=("ctx_split", "row_made"), sp=("q_stacked", "k_stacked"))

    def at(self, name, step, count):
        start = 0 if name in self.ZERO else 1
        return step * self.per[name] + (start + count)

    def query(self, q, j):
        return (q // 2, 4 * (q % 2) + j) if self.gqa else (j, q)

    def key(self, q, j):
        return (q // 2, 0) if self.gqa else (j, q)


def load_small(nc, a, ly, scratch_w, X, ident, w, h_t, sems):
    with ExitStack() as ctx:
        def sb(name, shape, dt=F32):
            return ctx.enter_context(nc.sbuf_tensor(f"{ly.name}_{name}", shape, dt))

        def sem(name):
            sems.append(nc.alloc_semaphore(f"{ly.name}_{name}"))
            return sems[-1]

        h_rows = sb("h_rows", [L, 2, D])
        bo = sb("bo", [L, D]) if ly.gqa else None
        stage = {n: sb(f"stage_{n}", [P, DC, ly.vw if n in "kv" else D]) for n in "qkv"}
        stage_o = sb("stage_o", [P, ly.halves, 4, D])
        bank = [ctx.enter_context(nc.psum_tensor(f"{ly.name}_turn{i}", [P, 512], F32)) for i in range(4)]
        landed = {n: sem(f"{n}_landed") for n in "qkvo"}
        h_made, h_turned, h_copied = sem("h_made"), sem("h_turned"), sem("h_copied")
        w_high, w_cleared, sel_made = sem("w_high"), sem("w_cleared"), sem("sel_made")
        w_low, v_landed, sel_cleared = sem("w_low"), sem("vectors_landed"), sem("sel_cleared")
        bo_added, settled = sem("bo_added"), sem("load_settled")

        def settle(eng):
            eng.sem_inc(settled, 1)

        pre = ly.name + "_xattn_"
        gqa = ly.gqa
        block = ctx.enter_context(nc.Block())

        @block.sync
        def _(sp):
            if gqa:
                src = {n: a[f"{pre}W{n}"].rearrange("(c p) n -> p c n", p=P) for n in "qkv"}
                wo = a[pre + "Wo"].rearrange("(kv g d) n -> kv d g n", g=4, d=16)
            else:
                src = {n: scratch_w[i].rearrange("(c p) n -> p c n", p=P) for i, n in enumerate("qkv")}
                wo = scratch_w[3].rearrange("(q j d) n -> q d j n", q=4, j=4)
            for n in "kvq":
                sp.dma_start(stage[n][:], src[n]).then_inc(landed[n], 16)
            if gqa:
                for kv in range(8):
                    for half in range(2):
                        r = 32 * (kv % 4) + 16 * half
                        sp.dma_start(stage_o[r:r + 16, kv // 4, :, :], wo[kv]).then_inc(landed["o"], 16)
                sp.wait_ge(v_landed, 16 * 13)
            else:
                for q in range(4):
                    sp.dma_start(stage_o[32 * q:32 * q + 32, 0, :, :], wo[q]).then_inc(landed["o"], 16)
                sp.dma_start(w["gate"][:], a["L2_xattn_gate"].rearrange("(o d) -> o d", o=1).broadcast_to([L, 1]))\
                  .then_inc(v_landed, 16)

        @block.gpsimd
        def _(pool):
            if gqa:
                pool.wait_ge(w_cleared, 2)
                bq = a[pre + "bq"].rearrange("(kv g d) -> kv d g", g=4, d=16)
                for kv in range(8):
                    r = 16 * kv
                    pool.dma_start(w["bq"][r:r + 16, 4 * (kv % 2):4 * (kv % 2) + 4], bq[kv],
                                   allow_slow_non_contiguous=True).then_inc(v_landed, 16)
                pool.dma_start(w["bk"][:], a[pre + "bk"].rearrange("(p o) -> p o", o=1),
                               allow_slow_non_contiguous=True).then_inc(v_landed, 16)
                pool.dma_start(w["bv"][:], a[pre + "bv"].rearrange("(o d) -> o d", o=1).broadcast_to([P, P]))\
                  .then_inc(v_landed, 16)
                for n in ("bo", "gamma", "beta"):
                    pool.dma_start((bo if n == "bo" else w[n])[:], rows_of(a[pre + n], L)).then_inc(v_landed, 16)
            pool.memset(w["sel"][:], 0.0).then_inc(sel_cleared, 1)
            pool.wait_ge(sel_cleared, 1)
            view = w["sel"][:].rearrange("h j (q r) -> h j q r", r=32)
            pool.affine_select(out=view, in_=view, compare_op=ALU.not_equal, fill=1.0, base=0,
                               pattern=[[-1, 4], [-4, 4], [0, 32]], channel_multiplier=1).then_inc(sel_made, 1)
            pool.wait_ge(sel_made, 1)
            if gqa:
                pool.wait_ge(v_landed, 16 * 13)
                with pool.Fori(0, B) as b:
                    pool.wait_ge(h_made, b + 1)
                    settle(pool)
                    pool.tensor_tensor(X[:, b, :], X[:, b, :], bo[:], ALU.add).then_inc(bo_added, 1)

        @block.scalar
        def _(act):
            act.sem_inc(h_copied, 4)
            if gqa:
                act.wait_ge(w_cleared, 2)
            act.wait_ge(landed["k"], 16)
            act.activation(w["wk_h"][:], stage["k"][:], ACT.Copy).then_inc(w_high, 1)
            act.wait_ge(landed["v"], 16)
            act.activation(w["wv_h"][:], stage["v"][:], ACT.Copy).then_inc(w_high, 1)
            act.wait_ge(landed["o"], 16 * (16 if gqa else 4))
            act.activation(w["wo_h"][:], stage_o[:], ACT.Copy).then_inc(w_high, 1)
            with act.Fori(0, B // 4) as four:
                for u in range(4):
                    b = four * 4 + u
                    act.wait_ge(h_turned, b + 5)
                    act.activation(h_t[:, b, :, :], bank[u][:, 0:DC * L].rearrange("p (c l) -> p c l", c=DC),
                                   ACT.Copy).then_inc(h_copied, 1)
            if not gqa:
                act.wait_ge(v_landed, 16)
                act.activation(w["tanh_gate"][:], w["gate"][:], ACT.Tanh).then_inc(w_high, 1)

        @block.vector
        def _(vec):
            if gqa:
                vec.memset(w["wq"][:], 0.0).then_inc(w_cleared, 1)
                vec.memset(w["bq"][:], 0.0).then_inc(w_cleared, 1)
            with vec.Fori(0, B // 2) as pair:
                for u in range(2):
                    b = pair * 2 + u
                    vec.wait_ge(h_turned, b + 3)
                    vec.tensor_copy(h_rows[:, u, :], X[:, b, :]).then_inc(h_made, 1)
            vec.wait_ge(landed["q"], 16)
            if gqa:
                vec.wait_ge(w_cleared, 2)
                for t in range(8):
                    p, g = t // 4, t % 4
                    for c in range(DC):
                        dst = w["wq"][:, c, t * P:(t + 1) * P].rearrange("k (s p d) -> k s p d", s=4, p=2)[:, :, p, :]
                        src = stage["q"][:, c, :].rearrange("k (s p g d) -> k s p g d", s=4, p=2, g=4)[:, :, p, g, :]
                        vec.tensor_scalar(dst, src, ly.scale, None, ALU.mult).then_inc(w_low, 1)
            else:
                vec.tensor_copy(w["wq"][:], stage["q"][:]).then_inc(w_low, 1)
            for n, raw in enumerate((stage["k"], stage["v"], stage_o)):
                vec.wait_ge(w_high, n + 1)
                name = "kvo"[n]
                vec.tensor_tensor(w[f"w{name}_l"][:], raw[:], w[f"w{name}_h"][:], ALU.subtract).then_inc(w_low, 1)
            if gqa:
                vec.wait_ge(v_landed, 16 * 13)
                vec.tensor_scalar(w["bq"][:], w["bq"][:], ly.scale, None, ALU.mult).then_inc(w_low, 1)

        @block.tensor
        def _(pe):
            pe.sem_inc(h_turned, 4)
            with pe.Fori(0, B // 4) as four:
                for u in range(4):
                    b = four * 4 + u
                    pe.wait_ge(h_made, b + 1)
                    pe.wait_ge(h_copied, b + 1)
                    for c in range(DC):
                        last = pe.transpose(bank[u][:, c * L:(c + 1) * L], h_rows[:, u % 2, c * P:(c + 1) * P],
                                            ident[0:L, 0:L])
                    last.then_inc(h_turned, 1)


def small_attention(nc, a, ly, scratch, scratch_w, X, ident, minus_half):
    sems = []
    with ExitStack() as ctx:
        def sb(name, shape, dt=F32):
            return ctx.enter_context(nc.sbuf_tensor(f"{ly.name}_{name}", shape, dt))

        h_t = sb("h_t", [P, B, DC, L])
        w = dict(wq=sb("wq", [P, DC, ly.qt * P]), sel=sb("sel", [16, 4, P]))
        for n, shape in (("wk", [P, DC, ly.vw]), ("wv", [P, DC, ly.vw]), ("wo", [P, ly.halves, 4, D])):
            w[n + "_h"], w[n + "_l"] = sb(n + "_h", shape, F32R), sb(n + "_l", shape, F32R)
        if ly.gqa:
            w |= dict(bq=sb("bq", [P, 8]), bk=sb("bk", [P, 1]), bv=sb("bv", [P, P]))
            w |= {n: sb(n, [L, D]) for n in ("gamma", "beta")}
        else:
            w |= dict(gate=sb("gate", [L, 1]), tanh_gate=sb("tanh_gate", [L, 1]))
        load_small(nc, a, ly, scratch_w, X, ident, w, h_t, sems)
        small_steps(nc, a, ly, scratch, X, ident, minus_half, w, h_t, sems)
    nc.clear_and_free_semaphores(sems)
    nc.all_engine_barrier()


def small_steps(nc, a, ly, scratch, X, ident, minus_half, w, h_t, sems):
    gqa, quads, heads, at = ly.gqa, ly.quads, ly.heads, ly.at
    with ExitStack() as ctx:
        def sb(name, shape, dt=F32):
            return ctx.enter_context(nc.sbuf_tensor(f"{ly.name}_{name}", shape, dt))

        def psum(name):
            return ctx.enter_context(nc.psum_tensor(f"{ly.name}_{name}", [P, 512], F32))

        def sem(name):
            sems.append(nc.alloc_semaphore(f"{ly.name}_{name}"))
            return sems[-1]

        ctx_h, ctx_l = (sb(n, [P, DC, KEYS], F32R) for n in ("ctx_h", "ctx_l"))
        ctx_raw = ctx_l[:].bitcast(F32) if gqa else sb("ctx_raw", [P, DC, KEYS])[:]
        q_h, q_l = (sb(n, [P, ly.qt, L], F32R) for n in ("q_h", "q_l"))
        k_h, k_l = (sb(n, [P, ly.kt, KEYS], F32R) for n in ("k_h", "k_l"))
        def two(name, shape, dt=F32):
            return [sb(f"{name}{u}", shape, dt) for u in range(2)] if gqa else [sb(name, shape, dt)] * 2

        q_s = two("q_s", [96, 4, ly.qt, L], F32R)
        k_s = two("k_s", [96, 4, ly.kt, KEYS], F32R)
        if gqa:
            v_raw = sb("v_raw", [P, P])
            v_s = sb("v_s", [P, 3, 8, 2, 16], F32R)
        else:
            v_h, v_l = (sb(n, [P, 3, D], F32R) for n in ("v_h", "v_l"))
            mask_u8 = sb("mask_u8", [L, S], U8)
        mask = two("mask", [L, S])
        probs = sb("probs", [L, 2, 4, S])
        pt_h, pt_l = (sb(n, [P, 2, 3, 4 * L], F32R) for n in ("pt_h", "pt_l"))
        o_h, o_l = (sb(n, [P, ly.halves, 4 * L], F32R) for n in ("o_h", "o_l"))
        o = sb("o", [P, ly.halves, 4 * L])[:]
        y = sb("y", [L, D]) if gqa else None
        neg_max, row_sum = two("neg_max", [L, heads]), two("row_sum", [L, heads])
        inv_sum = sb("inv_sum", [L, heads])
        inv_t = sb("inv_t", [16, ly.halves, L])
        stats = sb("stats", [L, 9])
        A = [psum(f"A{i}") for i in range(2)]
        Sb = [psum(f"S{i}") for i in range(2)]
        T = [psum(f"T{i}") for i in range(3)]
        O = psum("O")
        s = {n: sem(n) for n in ly.per}
        masks_landed = [sem(f"mask{u}_landed") for u in range(2)] if gqa else None
        settled, v_link, mask_half = sem("settled"), sem("v_link"), sem("mask_half")

        def settle(eng):
            eng.sem_inc(settled, 1)

        def wait(eng, name, step, count):
            eng.wait_ge(s[name], at(name, step, count))

        def all_steps(eng, body):
            body(0, 0, True, True)
            with eng.Fori(0, B // 2 - 1) as pair:
                body(pair * 2 + 1, 1, False, True)
                body(pair * 2 + 2, 0, False, True)
            body(B - 1, 1, False, False)

        ahead = [("q_lo", 1, k + 1) for k in range(ly.qt // 4)] + [("k_lo", 1, k + 1) for k in range(ly.kt)]
        values_ahead = [("v_taken", 1, t + 1) for t in range(3)]
        spreads = [("o_scaled", 0, k + 1) for k in range(ly.halves)]
        INV, OUT_BEFORE, OUT = ("inv_copied", 0, 1), ("x_done", -1, 1), ("x_done", 0, 1)
        qs = ly.qt // 4 if gqa else 0
        USES = ahead[:qs] + [OUT_BEFORE] + ahead[qs:] + [INV] + values_ahead[:1] + spreads + values_ahead[1:]
        LAST_USES = [OUT_BEFORE, INV] + spreads + [OUT]

        def bank_of(use, more):
            uses = USES if more else LAST_USES
            return A[uses.index(use) % 2]

        FIRST = [(name, k) for name, _, k in ahead + values_ahead]
        block = ctx.enter_context(nc.Block())

        @block.sync
        def _(sp):
            for name in ly.BY["sp"]:
                sp.sem_inc(s[name], 1)

            def load_context(n):
                wait(sp, "ctx_split", n, 0)
                settle(sp)
                if gqa and not (isinstance(n, int) and n == 0):
                    wait(sp, "v_ready", n, 0)
                    settle(sp)
                sp.dma_start(ctx_raw.rearrange("p c k -> p (c k)"), scratch[n]).then_inc(s["ctx_landed"], 16)

            def load_mask(n, u):
                if gqa:
                    if not (isinstance(n, int) and n == 0):
                        wait(sp, "max_ready", n - 1, 0)
                        settle(sp)
                    sp.dma_start(mask[u][:], a["mask_Bx1xSxS2_ff0"][n, 0]).then_inc(masks_landed[u], 16)
                else:
                    wait(sp, "mask_made", n, 0)
                    settle(sp)
                    sp.dma_start(mask_u8[:], a["mask_BxS2_bf1"][bass.ds(n, 1), :].broadcast_to([L, S]))\
                      .then_inc(s["mask_landed"], 16)

            def stack(n, u):
                if not gqa and not (isinstance(n, int) and n == 0):
                    wait(sp, "s_ready", n, 0)
                    settle(sp)
                for name, low, hi, lo, dst, order in (("q_stacked", "q_lo", q_h, q_l, q_s[u], "hhl"),
                                                      ("k_stacked", "k_lo", k_h, k_l, k_s[u], "hlh")):
                    wait(sp, low, n, ly.per[low])
                    settle(sp)
                    for part, src in enumerate(order):
                        for slot in range(4):
                            sp.dma_start(dst[32 * part:32 * part + 32, slot, :, :].bitcast(F32),
                                         (hi if src == "h" else lo)[32 * slot:32 * slot + 32, :, :].bitcast(F32))\
                              .then_inc(s[name], 16)

            def step(n, u, first, more):
                if more:
                    load_context(n + 1)
                    load_mask(n + 1, 1 - u)
                    stack(n + 1, 1 - u)

            load_context(0)
            load_mask(0, 0)
            stack(0, 0)
            all_steps(sp, step)

        @block.gpsimd
        def _(pool):
            for name in ly.BY["pool"]:
                pool.sem_inc(s[name], 1)

            def split_context(n):
                wait(pool, "ctx_landed", n, 16)
                if not isinstance(n, int) or n > 0:
                    wait(pool, "v_ready", n, 0)
                settle(pool)
                pool.tensor_copy(ctx_h[:], ctx_raw).then_inc(s["ctx_split"], 1)
                wait(pool, "ctx_split", n, 1)
                pool.tensor_tensor(ctx_l[:], ctx_raw, ctx_h[:], ALU.subtract).then_inc(s["ctx_split"], 1)

            def power(n):
                wait(pool, "var_ready", n, 1)
                pool.tensor_tensor(stats[:, 8:9], stats[:, 8:9], minus_half[0:L, 0:1], ALU.pow)\
                    .then_inc(s["rstd_ready"], 1)

            def new_row(n):
                wait(pool, "normed", n, 1)
                settle(pool)
                pool.tensor_tensor(y[:], y[:], w["gamma"][:], ALU.mult).then_inc(s["with_gamma"], 1)
                wait(pool, "with_gamma", n, 1)
                settle(pool)
                pool.tensor_tensor(X[:, n, :], y[:], w["beta"][:], ALU.add).then_inc(s["row_made"], 1)

            split_context(0)
            split_context(1)
            with pool.Fori(1, B - 1) as n:
                split_context(n + 1)
                if gqa:
                    power(n - 1)
                    new_row(n - 1)
            if gqa:
                for n in (B - 2, B - 1):
                    power(n)
                    new_row(n)

        @block.scalar
        def _(act):
            for name in ly.BY["act"]:
                act.sem_inc(s[name], 1)

            def project(n, bank, quad=None):
                for k in range(ly.qt // 4):
                    if quad not in (None, ly.query_after[k]):
                        continue
                    wait(act, "q_ready", n, k + 1)
                    if k == 0:
                        wait(act, "q_stacked", n, 0)
                    for t in range(4 * k, 4 * k + 4):
                        src = bank("q_lo", k + 1)[:, (t - 4 * k) * L:(t - 4 * k + 1) * L]
                        if gqa:
                            last = act.activation(q_h[:, t, :], src, ACT.Identity, bias=w["bq"][:, t:t + 1])
                        else:
                            last = act.activation(q_h[:, t, :], src, ACT.Copy)
                    last.then_inc(s["q_hi"], 1)
                for t in range(ly.kt):
                    if quad not in (None, ly.key_after[t]):
                        continue
                    wait(act, "k_ready", n, t + 1)
                    if t == 0:
                        wait(act, "k_stacked", n, 0)
                    src = bank("k_lo", t + 1)[:, 0:KEYS]
                    if gqa:
                        last = act.activation(k_h[:, t, :], src, ACT.Identity, bias=w["bk"][:])
                    else:
                        last = act.activation(k_h[:, t, :], src, ACT.Copy)
                    last.then_inc(s["k_hi"], 1)

            def values(n, bank, chunks=(0, 1, 2)):
                if gqa:
                    return
                if not (isinstance(n, int) and n == 0):
                    wait(act, "o_ready", n, 0)
                for t in chunks:
                    wait(act, "v_ready", n, t + 1)
                    act.activation(v_h[0:ROWS[t], t, :], bank("v_taken", t + 1)[0:ROWS[t], :], ACT.Copy)\
                       .then_inc(s["v_hi"], 1)

            def step(n, u, first, more):
                def exp(q, j):
                    v = u
                    if q == quads:
                        if not (gqa and more):
                            return
                        q, v = 0, 1 - u
                    c = 4 * q + j
                    wait(act, "max_ready", n if v == u else n + 1, c + 1)
                    p = probs[:, q % 2, j, :]
                    act.activation(p, p, ACT.Exp, bias=neg_max[v][:, c:c + 1], scale=-1.0,
                                   accum_out=row_sum[v][:, c:c + 1]).then_inc(s["exp_done"], 1)

                def turned(q, c):
                    rows = ROWS[c]
                    wait(act, "pt_ready", n, 3 * q + c + 1)
                    if q >= 2 and c == 0:
                        wait(act, "o_ready", n, q - 1)
                    act.activation(pt_h[0:rows, q % 2, c, :], T[c][0:rows, 0:4 * L], ACT.Copy)\
                       .then_inc(s["pt_hi"], 1)

                if first or not gqa:
                    for j in range(4):
                        exp(0, j)
                for q in range(quads):
                    turned(q, 0)
                    exp(q + 1, 0)
                    turned(q, 1)
                    exp(q + 1, 1)
                    turned(q, 2)
                    exp(q + 1, 2)
                    exp(q + 1, 3)
                    if more:
                        project(n + 1, lambda name, k: bank_of((name, 1, k), more), q)
                wait(act, "inv_turned", n, 1)
                act.activation(inv_t[:], bank_of(INV, more)[0:16, 0:ly.halves * L].rearrange("h (u l) -> h u l", u=ly.halves),
                               ACT.Copy)\
                   .then_inc(s["inv_copied"], 1)
                if more:
                    values(n + 1, lambda name, k: bank_of((name, 1, k), more), (0,))
                wait(act, "o_scaled", n, ly.halves)
                if not first:
                    wait(act, "out_ready", n - 1, 1)
                act.activation(o_h[:], o, ACT.Copy).then_inc(s["o_hi"], 1)
                if more:
                    values(n + 1, lambda name, k: bank_of((name, 1, k), more), (1, 2))

            first = lambda name, k: A[FIRST.index((name, k)) % 2]
            project(0, first)
            values(0, first)
            all_steps(act, step)

        @block.tensor
        def _(pe):
            def product(out, pairs):
                terms = [(l, r) for (lh, ll), (rh, rl) in pairs for l, r in ((ll, rh), (lh, rl), (lh, rh))]
                for k, (l, r) in enumerate(terms):
                    last = pe.matmul(out, l, r, start=k == 0, stop=k == len(terms) - 1)
                return last

            def queries(n, k, j, to):
                t = 4 * k + j
                for c in range(DC):
                    last = pe.matmul(to[:, j * L:(j + 1) * L], w["wq"][:, c, t * P:(t + 1) * P], h_t[:, n, c, :],
                                     start=c == 0, stop=c == DC - 1)
                if j == 3:
                    last.then_inc(s["q_ready"], 1)

            def keys(n, t, part, to):
                if t == 0 and part == 0:
                    wait(pe, "ctx_split", n, 2)
                wk = w["wk_l" if part == 0 else "wk_h"]
                right = ctx_l if part == 1 else ctx_h
                for c in range(DC):
                    last = pe.matmul(to[:, 0:KEYS], wk[:, c, t * P:(t + 1) * P], right[:, c, :],
                                     start=part == 0 and c == 0, stop=part == 2 and c == DC - 1)
                if part == 2:
                    last.then_inc(s["k_ready"], 1)

            def values(n, t, to):
                rows = ROWS[t]
                product(to[0:rows, 0:ly.vw],
                        [((ctx_h[:, c, t * P:t * P + rows], ctx_l[:, c, t * P:t * P + rows]),
                          (w["wv_h"][:, c, :], w["wv_l"][:, c, :])) for c in range(DC)]).then_inc(s["v_ready"], 1)

            for i, (name, k) in enumerate(FIRST):
                if i >= 2:
                    wait(pe, *(FIRST[i - 2][0], 0, FIRST[i - 2][1]))
                if name == "q_lo":
                    for j in range(4):
                        queries(0, k - 1, j, A[i % 2])
                elif name == "k_lo":
                    for part in range(3):
                        keys(0, k - 1, part, A[i % 2])
                else:
                    values(0, k - 1, A[i % 2])

            def output(n, to, tiles=range(4 * ly.halves)):
                if tiles[0] == 0:
                    wait(pe, "o_lo", n, 1)
                for t in tiles:
                    half, j = t // 4, t % 4
                    lh, ll = o_h[:, half, j * L:(j + 1) * L], o_l[:, half, j * L:(j + 1) * L]
                    rh, rl = w["wo_h"][:, half, j, :], w["wo_l"][:, half, j, :]
                    for k, (l, r) in enumerate(((ll, rh), (lh, rl), (lh, rh))):
                        last = pe.matmul(to[0:L, :], l, r, start=t == 0 and k == 0,
                                         stop=t == 4 * ly.halves - 1 and k == 2)
                if tiles[-1] == 4 * ly.halves - 1:
                    last.then_inc(s["out_ready"], 1)

            def step(n, u, first, more):
                uses = USES if more else LAST_USES

                def bank(use):
                    i = uses.index(use)
                    if i >= 2:
                        name, d, k = uses[i - 2]
                        if not (first and d < 0):
                            wait(pe, name, n + d, k)
                    else:
                        j = max(j for j in range(len(USES)) if j % 2 == i % 2)
                        name, d, k = USES[j]
                        wait(pe, name, n + d - 1, k)
                    return A[i % 2]

                def score(q, j):
                    m, v = n, u
                    if q == quads:
                        if not (gqa and more):
                            return
                        q, m, v = 0, n + 1, 1 - u
                    h = 4 * q + j
                    if h == 0:
                        wait(pe, "k_stacked", m, ly.per["k_stacked"])
                        wait(pe, "q_stacked", m, ly.per["q_stacked"])
                    wait(pe, "max_ready", m, max(h - 1, 0) if isinstance(m, int) and m == 0 else h - 1)
                    (qs, qt), (ks, kt) = ly.query(q, j), ly.key(q, j)
                    pe.matmul(Sb[h % 2][0:L, 0:KEYS], q_s[v][:, qs, qt, :], k_s[v][:, ks, kt, :],
                              start=True, stop=True).then_inc(s["s_ready"], 1)

                def turn(q, c):
                    if c == 0:
                        wait(pe, "exp_done", n, 4 * q + 4)
                    wait(pe, "pt_lo", n, max(3 * (q - 1) + c + 1, 0))
                    for j in range(4):
                        last = pe.transpose(T[c][0:ROWS[c], j * L:(j + 1) * L],
                                            probs[:, q % 2, j, c * P:c * P + ROWS[c]], ident[0:L, 0:L])
                    last.then_inc(s["pt_ready"], 1)

                def weigh(q):
                    wait(pe, "pt_lo", n, 3 * q + 3)
                    wait(pe, "o_copied", n, q)
                    if q == 0:
                        wait(pe, "v_taken", n, 3)
                    to = O
                    if gqa:
                        terms = [(v_s[0:ROWS[c], c, q, :, :], p[0:ROWS[c], q % 2, c, :]) for c in range(3) for p in (pt_l, pt_h)]
                        for i, (l, r) in enumerate(terms):
                            last = pe.matmul(to[0:32, 0:4 * L], l, r, start=i == 0, stop=i == len(terms) - 1)
                    else:
                        for j in range(4):
                            col = slice(32 * (4 * q + j), 32 * (4 * q + j) + 32)
                            last = product(to[0:32, j * L:(j + 1) * L],
                                           [((v_h[0:ROWS[c], c, col], v_l[0:ROWS[c], c, col]),
                                             (pt_h[0:ROWS[c], q % 2, c, j * L:(j + 1) * L],
                                              pt_l[0:ROWS[c], q % 2, c, j * L:(j + 1) * L]))
                                            for c in range(3)])
                    last.then_inc(s["o_ready"], 1)

                def fill(slot):
                    for kind, k, part in ly.fill[slot]:
                        if kind == "o":
                            if not first:
                                output(n - 1, bank(OUT_BEFORE) if part == 0 else bank_of(OUT_BEFORE, more), [part])
                            continue
                        if not more:
                            continue
                        use = ("q_lo" if kind == "q" else "k_lo", 1, k + 1)
                        to = bank(use) if part == 0 else bank_of(use, more)
                        (queries if kind == "q" else keys)(n + 1, k, part, to)

                if first or not gqa:
                    for j in range(4):
                        score(0, j)
                if first:
                    wait(pe, "v_taken", n, 3)
                elif not gqa:
                    output(n - 1, bank(OUT_BEFORE))
                for q in range(quads):
                    score(q + 1, 0)
                    score(q + 1, 1)
                    turn(q, 0)
                    turn(q, 1)
                    fill(3 * q)
                    score(q + 1, 2)
                    turn(q, 2)
                    fill(3 * q + 1)
                    if q >= 1:
                        weigh(q - 1)
                    score(q + 1, 3)
                    fill(3 * q + 2)
                weigh(quads - 1)
                wait(pe, "inv_made", n, 1)
                to = bank(INV)
                for half in range(ly.halves):
                    last = pe.transpose(to[0:16, half * L:(half + 1) * L], inv_sum[:, 16 * half:16 * half + 16],
                                        ident[0:L, 0:L])
                last.then_inc(s["inv_turned"], 1)
                if more:
                    values(n + 1, 0, bank(values_ahead[0]))
                wait(pe, "inv_copied", n, 1)
                for half, use in enumerate(spreads):
                    to = bank(use)
                    for j in range(4):
                        last = pe.matmul(to[:, j * L:(j + 1) * L], w["sel"][:, j, :], inv_t[:, half, :], start=True, stop=True)
                    last.then_inc(s["spread"], 1)
                if more:
                    for use in values_ahead[1:]:
                        values(n + 1, use[2] - 1, bank(use))
                else:
                    output(n, bank(OUT))

            all_steps(pe, step)

        @block.vector
        def _(vec):
            for name in ly.BY["vec"]:
                vec.sem_inc(s[name], 1)

            def project(n, bank, quad=None):
                for k in range(ly.qt // 4):
                    if quad not in (None, ly.query_after[k]):
                        continue
                    wait(vec, "q_hi", n, k + 1)
                    for t in range(4 * k, 4 * k + 4):
                        src = bank("q_lo", k + 1)[:, (t - 4 * k) * L:(t - 4 * k + 1) * L]
                        last = vec.scalar_tensor_tensor(q_l[:, t, :], src, w["bq"][:, t:t + 1] if gqa else 0.0,
                                                        q_h[:, t, :], ALU.add, ALU.subtract)
                    last.then_inc(s["q_lo"], 1)
                for t in range(ly.kt):
                    if quad not in (None, ly.key_after[t]):
                        continue
                    wait(vec, "k_hi", n, t + 1)
                    vec.scalar_tensor_tensor(k_l[:, t, :], bank("k_lo", t + 1)[:, 0:KEYS], w["bk"][:] if gqa else 0.0,
                                             k_h[:, t, :], ALU.add, ALU.subtract).then_inc(s["k_lo"], 1)

            def values(n, bank, chain, chunks=(0, 1, 2)):
                for t in chunks:
                    if gqa:
                        wait(vec, "v_taken", n, t)
                    rows = ROWS[t]
                    src = bank("v_taken", t + 1)[0:rows, 0:ly.vw]
                    if gqa:
                        wait(vec, "v_ready", n, t + 1)
                        chain(vec.tensor_tensor(v_raw[0:rows, :], src, w["bv"][0:rows, :], ALU.add))
                        raw = v_raw[0:rows, :].rearrange("k (h d) -> k h d", h=8)
                        chain(vec.tensor_copy(v_s[0:rows, t, :, 0, :], raw))
                        vec.tensor_tensor(v_s[0:rows, t, :, 1, :], raw, v_s[0:rows, t, :, 0, :], ALU.subtract)\
                           .then_inc(s["v_taken"], 1)
                    else:
                        wait(vec, "v_hi", n, t + 1)
                        vec.tensor_tensor(v_l[0:rows, t, :], src, v_h[0:rows, t, :], ALU.subtract)\
                           .then_inc(s["v_taken"], 1)

            def value_chain(n):
                count = [0]

                def chain(ins):
                    count[0] += 1
                    ins.then_inc(v_link, 1)
                    vec.wait_ge(v_link, n * 6 + count[0])
                return chain

            def take_output(n, bank):
                if gqa and not (isinstance(n, int) and n == 0):
                    wait(vec, "row_made", n, 0)
                wait(vec, "out_ready", n, 1)
                if gqa:
                    vec.tensor_tensor(y[:], bank[0:L, :], X[:, n, :], ALU.add).then_inc(s["x_done"], 1)
                else:
                    vec.scalar_tensor_tensor(X[:, n, :], bank[0:L, :], w["tanh_gate"][:], X[:, n, :], ALU.mult, ALU.add)\
                       .then_inc(s["x_done"], 1)

            def norm(n, part):
                if part == 0:
                    wait(vec, "x_done", n, 1)
                    settle(vec)
                    vec.bn_stats(stats[:, 0:6], y[:]).then_inc(s["stat_made"], 1)
                elif part == 1:
                    wait(vec, "stat_made", n, 1)
                    settle(vec)
                    vec.bn_aggr(stats[:, 6:8], stats[:, 0:6]).then_inc(s["moment_made"], 1)
                elif part == 2:
                    wait(vec, "moment_made", n, 1)
                    vec.tensor_scalar(stats[:, 8:9], stats[:, 7:8], 1e-6, None, ALU.add).then_inc(s["var_ready"], 1)
                else:
                    wait(vec, "rstd_ready", n, 1)
                    vec.tensor_scalar(y[:], y[:], stats[:, 6:7], stats[:, 8:9], ALU.subtract, ALU.mult)\
                       .then_inc(s["normed"], 1)

            def step(n, u, first, more):
                if not gqa:
                    wait(vec, "mask_landed", n, 16)
                    vec.tensor_scalar(mask[0][:], mask_u8[:], 1.0, FLT_MAX, ALU.subtract, ALU.mult).then_inc(mask_half, 1)
                    vec.wait_ge(mask_half, n + 1)
                    vec.tensor_scalar(mask[0][:], mask[0][:], 10.0, None, ALU.mult).then_inc(s["mask_made"], 1)
                    wait(vec, "mask_made", n, 1)

                def maximum(q, j):
                    m, v = n, u
                    if q == quads:
                        if not (gqa and more):
                            return
                        q, m, v = 0, n + 1, 1 - u
                    c = 4 * q + j
                    if gqa and c == 0:
                        vec.wait_ge(masks_landed[v], m * 8 + (16 - 8 * v))
                    wait(vec, "s_ready", m, c + 1)
                    settle(vec)
                    vec.tensor_tensor_reduce(probs[:, q % 2, j, :], Sb[c % 2][0:L, 0:S], mask[v][:],
                                             -1.0 if gqa else -ly.scale, FLT_MAX, ALU.add, ALU.min,
                                             neg_max[v][:, c:c + 1]).then_inc(s["max_ready"], 1)

                def copy_output(q):
                    wait(vec, "o_ready", n, q + 1)
                    vec.tensor_copy(o[32 * (q % 4):32 * (q % 4) + 32, q // 4, :], O[0:32, 0:4 * L])\
                       .then_inc(s["o_copied"], 1)

                def turned(q, c):
                    rows = ROWS[c]
                    wait(vec, "pt_hi", n, 3 * q + c + 1)
                    vec.tensor_tensor(pt_l[0:rows, q % 2, c, :], T[c][0:rows, 0:4 * L],
                                      pt_h[0:rows, q % 2, c, :], ALU.subtract).then_inc(s["pt_lo"], 1)

                if first or not gqa:
                    for j in range(4):
                        maximum(0, j)
                if not gqa and not first:
                    take_output(n - 1, bank_of(OUT_BEFORE, more))
                for q in range(quads):
                    maximum(q + 1, 0)
                    maximum(q + 1, 1)
                    turned(q, 0)
                    turned(q, 1)
                    maximum(q + 1, 2)
                    turned(q, 2)
                    maximum(q + 1, 3)
                    if q >= 1:
                        copy_output(q - 1)
                    if gqa and not first:
                        if q == ly.output_after:
                            take_output(n - 1, bank_of(OUT_BEFORE, more))
                        for part in {1: (0,), 2: (1, 2), 3: (3,)}.get(q - ly.output_after, ()):
                            norm(n - 1, part)
                    if more:
                        project(n + 1, lambda name, k: bank_of((name, 1, k), more), q)
                wait(vec, "exp_done", n, heads)
                vec.reciprocal(inv_sum[:], row_sum[u][:]).then_inc(s["inv_made"], 1)
                copy_output(quads - 1)
                chain = value_chain(n + 1)
                if more:
                    values(n + 1, lambda name, k: bank_of((name, 1, k), more), chain, (0,))
                wait(vec, "o_copied", n, quads)
                for half in range(ly.halves):
                    wait(vec, "spread", n, half + 1)
                    vec.tensor_tensor(o[:, half, :], bank_of(("o_scaled", 0, half + 1), more)[:, 0:4 * L], o[:, half, :],
                                      ALU.mult).then_inc(s["o_scaled"], 1)
                if more:
                    values(n + 1, lambda name, k: bank_of((name, 1, k), more), chain, (1,))
                wait(vec, "o_hi", n, 1)
                vec.tensor_tensor(o_l[:], o, o_h[:], ALU.subtract).then_inc(s["o_lo"], 1)
                if more:
                    values(n + 1, lambda name, k: bank_of((name, 1, k), more), chain, (2,))

            first = lambda name, k: A[FIRST.index((name, k)) % 2]
            project(0, first)
            values(0, first, value_chain(0))
            all_steps(vec, step)
            take_output(B - 1, bank_of(OUT, False))
            if gqa:
                for part in range(4):
                    norm(B - 1, part)


GROUPS = 4
SCALE = P ** -0.5
WIDE = dict(
    k_ready=4, v_ready=3, q_ready=1, s_ready=4, pt_ready=3, o_ready=1, out_ready=1,
    ctx_landed=16,
    k_hi=4, q_hi=1, exp_done=4, pt_act=2, o_hi=1, ctx_hi=4,
    k_lo=4, q_lo=1, max_ready=4, inverse=4, scaled=4, v_taken=3, pt_vec=1, o_lo=1, x_done=1, ctx_lo=4)
WIDE_ZERO = ("k_ready", "v_ready", "q_ready", "s_ready", "pt_ready", "o_ready", "out_ready", "ctx_landed")
WIDE_BY = dict(act=("k_hi", "q_hi", "exp_done", "pt_act", "o_hi", "ctx_hi"),
               vec=("k_lo", "q_lo", "max_ready", "inverse", "scaled", "v_taken", "pt_vec", "o_lo", "x_done",
                    "ctx_lo"))


def wide_attention(nc, a, scratch_ctx, X, ident, minus_half):
    with ExitStack() as ctx:
        def sb(name, shape, dt=F32):
            return ctx.enter_context(nc.sbuf_tensor("wide_" + name, shape, dt))

        def psum(name):
            return ctx.enter_context(nc.psum_tensor("wide_" + name, [P, 512], F32))

        def sem(name):
            return ctx.enter_context(nc.semaphore("wide_" + name))

        h_rows = sb("h_rows", [L, 2, D])
        h_t = sb("h_t", [P, B, DC, L])
        ctx_raw = sb("ctx_raw", [P, DC, KEYS])
        ctx_h, ctx_l = (sb(n, [P, DC, KEYS], F32R) for n in ("ctx_h", "ctx_l"))
        stage = {x: sb("stage_" + x, [P, DC, D]) for x in "qkvo"}
        wq = sb("wq", [P, DC, D])
        wk_h, wk_l, wv_h, wv_l, wo_h, wo_l = (
            sb(n, [P, DC, D], F32R) for n in ("wk_h", "wk_l", "wv_h", "wv_l", "wo_h", "wo_l"))
        q_h, q_l = (sb(n, [P, 4, L], F32R) for n in ("q_h", "q_l"))
        k_h, k_l = (sb(n, [P, 4, KEYS], F32R) for n in ("k_h", "k_l"))
        v = sb("v", [P, 3, D])
        probs = sb("probs", [L, 4, KEYS])
        probs_t = sb("probs_t", [P, 3, 4 * L])
        o_h, o_l = (sb(n, [P, 4, L], F32R) for n in ("o_h", "o_l"))
        bv = sb("bv", [P, D])
        bo, gamma, beta = (sb(n, [L, D]) for n in ("bo", "gamma", "beta"))
        bq, bq_scaled, bk, bias_k = (sb(n, [P, 4]) for n in ("bq", "bq_scaled", "bk", "bias_k"))
        neg_max, row_sum, inv_sum = (sb(n, [L, 4]) for n in ("neg_max", "row_sum", "inv_sum"))
        stats = sb("stats", [L, B, 6])
        moments = sb("moments", [L, B, 2])
        rstd = sb("rstd", [L, B])
        power_of = sb("power", [L, B])

        A = [psum(f"A{i}") for i in range(3)]
        Sb = [psum(f"S{i}") for i in range(2)]
        T = [psum(f"T{i}") for i in range(2)]
        O = psum("O")

        s = {n: sem(n) for n in WIDE}
        w_landed = {x: sem(f"w{x}_landed") for x in "qkvo"}
        w_hi = {x: sem(f"w{x}_hi") for x in "qkvo"}
        w_lo = {x: sem(f"w{x}_lo") for x in "kvo"}
        bq_landed, bk_landed, bv_landed, bias_k_landed, bias_v_landed, bq_made, bias_hi, bias_lo = (
            sem(n) for n in ("bq_landed", "bk_landed", "bv_landed", "bias_k_landed", "bias_v_landed", "bq_made",
                             "bias_hi", "bias_lo"))
        norm_landed, stat_made, moment_made, var_ready, rstd_ready, centred, h_made, h_turned, h_copied, bo_added = (
            sem(n) for n in ("norm_landed", "stat_made", "moment_made", "var_ready", "rstd_ready", "centred", "h_made",
                             "h_turned", "h_copied", "bo_added"))
        power_made, settled = sem("power_made"), sem("settled")

        def settle(eng):
            eng.sem_inc(settled, 1)

        def at(name, n, count):
            return n * WIDE[name] + ((0 if name in WIDE_ZERO else 1) + count)

        def wait(eng, name, n, count):
            eng.wait_ge(s[name], at(name, n, count))

        def steps(eng, i, step):
            base = i * GROUPS * B
            with eng.Fori(0, GROUPS - 1) as g:
                with eng.Fori(0, B - 1) as b:
                    step(g * B + b + base, b, g + i * GROUPS, False, False)
                step(g * B + (base + B - 1), B - 1, g + i * GROUPS, False, True)
            last = base + (GROUPS - 1) * B
            with eng.Fori(0, B - 1) as b:
                step(b + last, b, (i + 1) * GROUPS - 1, False, False)
            step(last + B - 1, B - 1, (i + 1) * GROUPS - 1, True, True)

        FINAL = 2 * GROUPS * B - 1

        def final(n):
            return isinstance(n, int) and n == FINAL

        block = ctx.enter_context(nc.Block())

        @block.sync
        def _(sp):
            def load_weights(i, g, G):
                cols = bass.ds(g * D, D)
                for x in "kvqo":
                    if x == "o":
                        src = a[f"L3_xattn_wo{i + 1}"].rearrange("(g c p) n -> g p c n", g=GROUPS, p=P)[g]
                    else:
                        src = a[f"L3_xattn_w{x}{i + 1}"].rearrange("(c p) n -> p c n", p=P)[:, :, cols]
                    if not (isinstance(G, int) and G == 0):
                        sp.wait_ge((w_hi if x == "q" else w_lo)[x], G)
                        settle(sp)
                    sp.dma_start(stage[x][:], src).then_inc(w_landed[x], 16)

            def load_vectors(i, g, G, n):
                def part(name):
                    return a[f"L3_xattn_{name}{i + 1}"].rearrange("(g c p) -> g p c", g=GROUPS, p=P)[g]

                first = isinstance(G, int) and G == 0

                def used(name, count):
                    if not first:
                        wait(sp, name, n, count)
                        settle(sp)

                used("q_lo", 1)
                sp.dma_start(bq[:], part("bq"), allow_slow_non_contiguous=True).then_inc(bq_landed, 16)
                if not first:
                    sp.wait_ge(bias_lo, G)
                    settle(sp)
                sp.dma_start(bias_k[:].rearrange("p (c o) -> p c o", o=1),
                             a[f"L3_xattn_bias_k{i + 1}"].rearrange("x y (g c) (p o) -> (x y g) p c o", g=GROUPS, o=1)[g],
                             allow_slow_non_contiguous=True).then_inc(bias_k_landed, 16)
                used("k_lo", 4)
                sp.dma_start(bk[:], part("bk"), allow_slow_non_contiguous=True).then_inc(bk_landed, 16)
                used("v_taken", 3)
                sp.dma_start(bv[:], a[f"L3_xattn_bv{i + 1}"].rearrange("(g o d) -> g o d", g=GROUPS, o=1)[g]
                             .broadcast_to([P, D])).then_inc(bv_landed, 16)
                used("o_ready", 1)
                sp.dma_start(v[ROWS[2]:ROWS[2] + 1, 2, :],
                             a[f"L3_xattn_bias_v{i + 1}"].rearrange("x y (g c) p -> (x y g) (c p)", g=GROUPS)[
                                 bass.ds(g, 1), :]).then_inc(bias_v_landed, 16)

            def load_context(n, b):
                wait(sp, "ctx_lo", n, 0)
                settle(sp)
                sp.dma_start(ctx_raw[:].rearrange("p c k -> p (c k)"), scratch_ctx[b]).then_inc(s["ctx_landed"], 16)

            def load_norm(i):
                for dst, name in (bo, f"bo{i + 1}"), (gamma, f"ln{i + 1}_scale"), (beta, f"ln{i + 1}_offset"):
                    sp.dma_start(dst[:], rows_of(a["L3_xattn_" + name], L)).then_inc(norm_landed, 16)

            load_norm(0)
            load_context(0, 0)
            load_weights(0, 0, 0)
            load_vectors(0, 0, 0, None)
            for i in range(2):
                base = i * GROUPS * B

                def group(g, G, following, i=i):
                    n = g * B + base
                    load_context(n + 1, 1)
                    if following:
                        load_weights(*following)
                    with sp.Fori(1, B - 1) as b:
                        load_context(n + b + 1, b + 1)
                    if following:
                        load_context(n + B, 0)
                        load_vectors(*following, n + B - 1)

                with sp.Fori(0, GROUPS - 1) as g:
                    group(g, g + i * GROUPS, (i, g + 1, g + (i * GROUPS + 1)))
                if i == 0:
                    sp.wait_ge(bo_added, B)
                    load_norm(1)
                group(GROUPS - 1, (i + 1) * GROUPS - 1, (1, 0, GROUPS) if i == 0 else None)

        @block.gpsimd
        def _(pool):
            pool.memset(power_of[:], -0.5).then_inc(power_made, 1)
            pool.wait_ge(power_made, 1)
            for i in range(2):
                pool.wait_ge(var_ready, i + 1)
                pool.tensor_tensor(rstd[:], rstd[:], power_of[:], ALU.pow).then_inc(rstd_ready, 1)
                with pool.Fori(0, B) as b:
                    pool.wait_ge(h_made, b + (i * B + 1))
                    settle(pool)
                    pool.tensor_tensor(X[:, b, :], X[:, b, :], bo[:], ALU.add).then_inc(bo_added, 1)

        @block.scalar
        def _(act):
            for name in WIDE_BY["act"]:
                act.sem_inc(s[name], 1)

            def high(x, dst, G):
                act.wait_ge(w_landed[x], G * 16 + 16)
                settle(act)
                act.activation(dst[:], stage[x][:], ACT.Copy).then_inc(w_hi[x], 1)

            def queries_weight(G):
                act.wait_ge(w_landed["q"], G * 16 + 16)
                settle(act)
                act.activation(wq[:], stage["q"][:], ACT.Copy, scale=SCALE).then_inc(w_hi["q"], 1)
                act.wait_ge(bq_landed, G * 16 + 16)
                settle(act)
                act.activation(bq_scaled[:], bq[:], ACT.Copy, scale=SCALE).then_inc(bq_made, 1)

            def appended_key(G):
                act.wait_ge(bias_k_landed, G * 16 + 16)
                settle(act)
                act.activation(k_h[:, :, S:KEYS], bias_k[:].rearrange("p (c o) -> p c o", o=1), ACT.Copy)\
                   .then_inc(bias_hi, 1)

            def context(n):
                wait(act, "ctx_landed", n, 16)
                for c in range(DC):
                    act.activation(ctx_h[:, c, :], ctx_raw[:, c, :], ACT.Copy).then_inc(s["ctx_hi"], 1)

            def queries(n, G):
                act.wait_ge(bq_made, G + 1)
                wait(act, "q_ready", n, 1)
                for t in range(4):
                    last = act.activation(q_h[:, t, :], A[1][:, t * L:(t + 1) * L], ACT.Identity,
                                          bias=bq_scaled[:, t:t + 1])
                last.then_inc(s["q_hi"], 1)

            def step(n, b, G, layer_ends, group_ends):
                def key(t):
                    if t == 0:
                        act.wait_ge(bk_landed, G * 16 + 16)
                    wait(act, "k_ready", n, t + 1)
                    act.activation(k_h[:, t, 0:S], A[t % 3][:, 0:S], ACT.Identity, bias=bk[:, t:t + 1])\
                       .then_inc(s["k_hi"], 1)

                def exp(j):
                    wait(act, "max_ready", n, j + 1)
                    act.activation(probs[:, j, :], Sb[j % 2][0:L, 0:KEYS], ACT.Exp, bias=neg_max[:, j:j + 1],
                                   accum_out=row_sum[:, j:j + 1]).then_inc(s["exp_done"], 1)

                key(0)
                key(1)
                key(2)
                exp(0)
                key(3)
                exp(1)
                exp(2)
                exp(3)
                if group_ends and not final(n):
                    queries_weight(G + 1)
                for k, c in enumerate((0, 2)):
                    wait(act, "pt_ready", n, c + 1)
                    act.activation(probs_t[0:ROWS[c] + c // 2, c, :], T[0][0:ROWS[c] + c // 2, 0:4 * L], ACT.Copy)\
                       .then_inc(s["pt_act"], 1)
                if not final(n):
                    if group_ends:
                        high("k", wk_h, G + 1)
                    wait(act, "v_ready", n, 3)
                    context(n + 1)
                wait(act, "o_ready", n, 1)
                act.activation(o_h[:], O[:, 0:4 * L].rearrange("p (h l) -> p h l", h=4), ACT.Copy).then_inc(s["o_hi"], 1)
                if not layer_ends:
                    queries(n + 1, G + 1 if group_ends else G)
                if group_ends and not final(n):
                    high("v", wv_h, G + 1)
                    wait(act, "out_ready", n, 1)
                    high("o", wo_h, G + 1)
                    appended_key(G + 1)

            act.sem_inc(h_copied, 2)
            high("k", wk_h, 0)
            high("v", wv_h, 0)
            queries_weight(0)
            for i in range(2):
                with act.Fori(0, B // 2) as pair:
                    for u in range(2):
                        b = pair * 2 + u
                        act.wait_ge(h_turned, b + (B * i + 3))
                        act.activation(h_t[:, b, :, :], A[u][:, 0:DC * L].rearrange("p (c l) -> p c l", c=DC),
                                       ACT.Copy).then_inc(h_copied, 1)
                if i == 0:
                    context(0)
                queries(i * GROUPS * B, i * GROUPS)
                if i == 0:
                    high("o", wo_h, 0)
                    appended_key(0)
                steps(act, i, step)

        @block.tensor
        def _(pe):
            def product(out, pairs):
                terms = [(l, r) for (lh, ll), (rh, rl) in pairs for l, r in ((ll, rh), (lh, rl), (lh, rh))]
                for k, (l, r) in enumerate(terms):
                    last = pe.matmul(out, l, r, start=k == 0, stop=k == len(terms) - 1)
                return last

            def queries(n, b, G, tiles=range(4)):
                if tiles[0] == 0:
                    pe.wait_ge(w_hi["q"], G + 1)
                    if not (isinstance(n, int) and n == 0):
                        wait(pe, "v_taken", n - 1, 1)
                for t in tiles:
                    for c in range(DC):
                        last = pe.matmul(A[1][:, t * L:(t + 1) * L], wq[:, c, t * P:(t + 1) * P], h_t[:, b, c, :],
                                         start=c == 0, stop=c == DC - 1)
                if tiles[-1] == 3:
                    last.then_inc(s["q_ready"], 1)

            def step(n, b, G, layer_ends, group_ends):
                following = (n + 1, 0 if group_ends else b + 1, G + 1 if group_ends else G)
                def key(t):
                    if t == 0:
                        pe.wait_ge(w_lo["k"], G + 1)
                        wait(pe, "v_taken", n, 0)
                    elif t == 1:
                        wait(pe, "q_lo", n, 1)
                    elif t == 2:
                        wait(pe, "x_done", n, 0)
                    else:
                        wait(pe, "k_lo", n, 1)
                    cols = slice(t * P, (t + 1) * P)
                    for c in range(DC):
                        if t == 0:
                            wait(pe, "ctx_lo", n, c + 1)
                        for k, (l, r) in enumerate(((wk_l, ctx_h), (wk_h, ctx_l), (wk_h, ctx_h))):
                            last = pe.matmul(A[t % 3][:, 0:KEYS], l[:, c, cols], r[:, c, :],
                                             start=c == 0 and k == 0, stop=c == DC - 1 and k == 2)
                    last.then_inc(s["k_ready"], 1)

                def score(j):
                    if j == 0:
                        wait(pe, "q_lo", n, 1)
                        pe.wait_ge(bias_lo, G + 1)
                    wait(pe, "k_lo", n, j + 1)
                    wait(pe, "exp_done", n, max(j - 1, 0))
                    product(Sb[j % 2][0:L, 0:KEYS], [((q_h[:, j, :], q_l[:, j, :]), (k_h[:, j, :], k_l[:, j, :]))])\
                        .then_inc(s["s_ready"], 1)

                def value(t):
                    if t == 0:
                        pe.wait_ge(w_lo["v"], G + 1)
                        wait(pe, "k_lo", n, 2)
                    elif t == 1:
                        wait(pe, "k_lo", n, 3)
                    else:
                        wait(pe, "k_lo", n, 4)
                    rows = ROWS[t]
                    product(A[(t + 1) % 3][0:rows, :],
                            [((ctx_h[:, c, t * P:t * P + rows], ctx_l[:, c, t * P:t * P + rows]),
                              (wv_h[:, c, :], wv_l[:, c, :])) for c in range(DC)]).then_inc(s["v_ready"], 1)

                def turn(c):
                    if c == 0:
                        wait(pe, "scaled", n, 4)
                        wait(pe, "pt_act", n, 0)
                    elif c == 1:
                        wait(pe, "pt_vec", n, 0)
                    else:
                        wait(pe, "pt_act", n, 1)
                    rows = ROWS[c] + c // 2
                    for j in range(4):
                        last = pe.transpose(T[c % 2][0:rows, j * L:(j + 1) * L], probs[:, j, c * P:c * P + rows],
                                            ident[0:L, 0:L])
                    last.then_inc(s["pt_ready"], 1)

                key(0)
                key(1)
                score(0)
                key(2)
                score(1)
                key(3)
                score(2)
                value(0)
                score(3)
                value(1)
                turn(0)
                turn(1)
                value(2)
                turn(2)
                if not layer_ends:
                    queries(*following, range(0, 2))
                wait(pe, "v_taken", n, 3)
                wait(pe, "pt_vec", n, 1)
                wait(pe, "pt_act", n, 2)
                wait(pe, "o_lo", n, 0)
                pe.wait_ge(bias_v_landed, G * 16 + 16)
                for j in range(4):
                    for c in range(3):
                        rows = ROWS[c] + c // 2
                        last = pe.matmul(O[:, j * L:(j + 1) * L], v[0:rows, c, j * P:(j + 1) * P],
                                         probs_t[0:rows, c, j * L:(j + 1) * L], start=c == 0, stop=c == 2)
                last.then_inc(s["o_ready"], 1)
                if not layer_ends:
                    queries(*following, range(2, 4))
                pe.wait_ge(w_lo["o"], G + 1)
                wait(pe, "v_taken", n, 2)
                wait(pe, "o_lo", n, 1)
                product(A[2][0:L, :], [((o_h[:, j, :], o_l[:, j, :]), (wo_h[:, j, :], wo_l[:, j, :]))
                                       for j in range(4)]).then_inc(s["out_ready"], 1)

            pe.sem_inc(h_turned, 2)
            for i in range(2):
                n = i * GROUPS * B
                wait(pe, "v_taken", n, 0)
                with pe.Fori(0, B // 2) as pair:
                    for u in range(2):
                        b = pair * 2 + u
                        pe.wait_ge(h_made, b + (B * i + 1))
                        pe.wait_ge(h_copied, b + (B * i + 1))
                        for c in range(DC):
                            last = pe.transpose(A[u][:, c * L:(c + 1) * L], h_rows[:, u, c * P:(c + 1) * P],
                                                ident[0:L, 0:L])
                        last.then_inc(h_turned, 1)
                pe.wait_ge(h_copied, B * (i + 1) + 2)
                queries(n, 0, i * GROUPS)
                steps(pe, i, step)

        @block.vector
        def _(vec):
            for name in WIDE_BY["vec"]:
                vec.sem_inc(s[name], 1)

            def low(x, hi, lo, G):
                vec.wait_ge(w_hi[x], G + 1)
                vec.tensor_tensor(lo[:], stage[x][:], hi[:], ALU.subtract).then_inc(w_lo[x], 1)

            def appended_key(G):
                vec.wait_ge(bias_hi, G + 1)
                vec.tensor_tensor(k_l[:, :, S:KEYS], bias_k[:].rearrange("p (c o) -> p c o", o=1), k_h[:, :, S:KEYS],
                                  ALU.subtract).then_inc(bias_lo, 1)

            def context(n):
                for c in range(DC):
                    wait(vec, "ctx_hi", n, c + 1)
                    vec.tensor_tensor(ctx_l[:, c, :], ctx_raw[:, c, :], ctx_h[:, c, :], ALU.subtract)\
                       .then_inc(s["ctx_lo"], 1)

            def queries(n):
                wait(vec, "q_hi", n, 1)
                for t in range(4):
                    last = vec.scalar_tensor_tensor(q_l[:, t, :], A[1][:, t * L:(t + 1) * L], bq_scaled[:, t:t + 1],
                                                    q_h[:, t, :], ALU.add, ALU.subtract)
                last.then_inc(s["q_lo"], 1)

            def step(n, b, G, layer_ends, group_ends):
                def key(t):
                    wait(vec, "k_hi", n, t + 1)
                    vec.scalar_tensor_tensor(k_l[:, t, 0:S], A[t % 3][:, 0:S], bk[:, t:t + 1], k_h[:, t, 0:S],
                                             ALU.add, ALU.subtract).then_inc(s["k_lo"], 1)

                def maximum(j):
                    wait(vec, "s_ready", n, j + 1)
                    vec.tensor_reduce(neg_max[:, j:j + 1], Sb[j % 2][0:L, 0:KEYS], AX.X, ALU.max, negate=True)\
                       .then_inc(s["max_ready"], 1)

                def invert(j):
                    wait(vec, "exp_done", n, j + 1)
                    vec.reciprocal(inv_sum[:, j:j + 1], row_sum[:, j:j + 1]).then_inc(s["inverse"], 1)

                def scale(j):
                    wait(vec, "inverse", n, j + 1)
                    vec.tensor_scalar(probs[:, j, :], probs[:, j, :], inv_sum[:, j:j + 1], None, ALU.mult)\
                       .then_inc(s["scaled"], 1)

                def value(t):
                    if t == 0:
                        vec.wait_ge(bv_landed, G * 16 + 16)
                    wait(vec, "v_ready", n, t + 1)
                    vec.tensor_tensor(v[0:ROWS[t], t, :], A[(t + 1) % 3][0:ROWS[t], :], bv[0:ROWS[t], :], ALU.add)\
                       .then_inc(s["v_taken"], 1)

                key(0)
                key(1)
                maximum(0)
                key(2)
                maximum(1)
                key(3)
                invert(0)
                maximum(2)
                scale(0)
                invert(1)
                value(0)
                scale(1)
                maximum(3)
                invert(2)
                scale(2)
                invert(3)
                scale(3)
                value(1)
                wait(vec, "pt_ready", n, 2)
                vec.tensor_copy(probs_t[:, 1, :], T[1][:, 0:4 * L]).then_inc(s["pt_vec"], 1)
                value(2)
                if not final(n):
                    if group_ends:
                        low("k", wk_h, wk_l, G + 1)
                    context(n + 1)
                wait(vec, "o_hi", n, 1)
                vec.tensor_tensor(o_l[:], O[:, 0:4 * L].rearrange("p (h l) -> p h l", h=4), o_h[:], ALU.subtract)\
                   .then_inc(s["o_lo"], 1)
                if not layer_ends:
                    queries(n + 1)
                wait(vec, "out_ready", n, 1)
                wait(vec, "x_done", n, 0)
                vec.tensor_tensor(X[:, b, :], A[2][0:L, :], X[:, b, :], ALU.add).then_inc(s["x_done"], 1)
                if group_ends and not final(n):
                    low("v", wv_h, wv_l, G + 1)
                    low("o", wo_h, wo_l, G + 1)
                    appended_key(G + 1)

            for i in range(2):
                vec.wait_ge(norm_landed, 48 * (i + 1))
                wait(vec, "x_done", i * GROUPS * B, 0)
                with vec.Fori(0, B) as b:
                    vec.bn_stats(stats[:, b, :], X[:, b, :]).then_inc(stat_made, 1)
                vec.wait_ge(stat_made, B * (i + 1))
                for b in range(B):
                    vec.bn_aggr(moments[:, b, :], stats[:, b, :]).then_inc(moment_made, 1)
                vec.wait_ge(moment_made, B * (i + 1))
                vec.tensor_scalar(rstd[:], moments[:, :, 1], 1e-5, None, ALU.add).then_inc(var_ready, 1)
                if i == 0:
                    low("k", wk_h, wk_l, 0)
                vec.wait_ge(rstd_ready, i + 1)
                for b in range(B):
                    if B * i + b >= 2:
                        vec.wait_ge(h_turned, B * i + b + 1)
                    vec.scalar_tensor_tensor(h_rows[:, b % 2, :], X[:, b, :], moments[:, b, 0:1], gamma[:],
                                             ALU.subtract, ALU.mult).then_inc(centred, 1)
                    vec.wait_ge(centred, B * i + b + 1)
                    vec.scalar_tensor_tensor(h_rows[:, b % 2, :], h_rows[:, b % 2, :], rstd[:, b:b + 1], beta[:],
                                             ALU.mult, ALU.add).then_inc(h_made, 1)
                vec.wait_ge(bo_added, B * (i + 1))
                if i == 0:
                    context(0)
                queries(i * GROUPS * B)
                if i == 0:
                    low("v", wv_h, wv_l, 0)
                    low("o", wo_h, wo_l, 0)
                    appended_key(0)
                steps(vec, i, step)


def feed_forward(nc, a, X, ident, minus_half, out):
    HB = B // 2
    HL = HB * L
    with ExitStack() as ctx:
        def sb(name, shape, dt=F32):
            return ctx.enter_context(nc.sbuf_tensor(name, shape, dt))

        def psum(name):
            return ctx.enter_context(nc.psum_tensor(name, [P, 512], F32))

        def sem(name):
            return ctx.enter_context(nc.semaphore(name))

        rows = sb("mlp_rows", [L, 2, D])
        in_h, in_l = (sb(n, [P, B, DC, L], F32R) for n in ("in_h", "in_l"))
        gamma, beta, b2 = (sb(n, [L, D]) for n in ("mlp_gamma", "mlp_beta", "b2"))
        b1 = sb("b1", [P, FT])
        w1_raw = sb("w1_raw", [P, 4, DC, P])
        w2_raw = sb("w2_raw", [P, 4, D])
        w1_h, w1_l = (sb(n, [P, 2, DC, P], F32R) for n in ("w1_h", "w1_l"))
        w2_h, w2_l = (sb(n, [P, 2, D], F32R) for n in ("w2_h", "w2_l"))
        g = sb("g", [P, 2, HL])
        g_h, g_l = (sb(n, [P, 2, HL], F32R) for n in ("g_h", "g_l"))
        y = sb("mlp_y", [L, B, D])
        stats = sb("mlp_stats", [L, B, 6])
        moments = sb("mlp_moments", [L, B, 2])
        rstd = sb("mlp_rstd", [L, B])
        power_of = sb("mlp_power", [L, B])
        A = [psum(f"mlp_A{i}") for i in range(2)]
        R = [psum(f"mlp_R{i}") for i in range(HB)]
        (vectors_landed, stat_made, moment_made, centred, power_made, rows_made, rows_turned, rows_hi, rows_lo, w1_hi, w2_hi, w1_lo, w2_lo, fc1_ready, gelu_done, g_hi, g_lo,
         fc2_done, taken, y_made, stored, var_ready, rstd_ready) = (sem("mlp_" + n) for n in (
             "vectors_landed", "stat_made", "moment_made", "centred", "power_made", "rows_made", "rows_turned", "rows_hi", "rows_lo", "w1_hi", "w2_hi", "w1_lo", "w2_lo", "fc1_ready",
             "gelu_done", "g_hi", "g_lo", "fc2_done", "taken", "y_made", "stored", "var_ready",
             "rstd_ready"))
        w_landed = [sem(f"mlp_w_landed{u}") for u in range(4)]

        settled = sem("mlp_settled")

        def settle(eng):
            eng.sem_inc(settled, 1)

        block = ctx.enter_context(nc.Block())

        def pairs(eng, half, body):
            body(True, False, half * (FT // 2))
            with eng.Fori(1, FT // 2 - 1) as pair:
                body(False, False, half * (FT // 2) + pair)
            body(False, True, half * (FT // 2) + (FT // 2 - 1))

        @block.sync
        def _(sp):
            for dst, name in ((gamma, "ln_mlp_scale"), (beta, "ln_mlp_offset"), (b2, "b_fc2")):
                sp.dma_start(dst[:], rows_of(a["L3_xattn_" + name], L)).then_inc(vectors_landed, 16)
            sp.dma_start(b1[:], a["L3_xattn_b_fc1"].rearrange("(t p) -> p t", p=P),
                         allow_slow_non_contiguous=True).then_inc(vectors_landed, 16)
            w1 = a["L3_xattn_w_fc1"].rearrange("(c p) (t n) -> t p c n", p=P, n=P)
            w2 = a["L3_xattn_w_fc2"].rearrange("(t p) n -> t p n", p=P)
            with sp.Fori(0, 2) as half:
                with sp.Fori(0, FT // 4) as four:
                    for u in range(4):
                        t = four * 4 + u
                        sp.wait_ge(w2_lo, half * FT + t + 1)
                        settle(sp)
                        sp.dma_start(w1_raw[:, u, :, :], w1[t]).then_inc(w_landed[u], 16)
                        sp.dma_start(w2_raw[:, u, :], w2[t]).then_inc(w_landed[u], 16)

        @block.gpsimd
        def _(pool):
            pool.memset(power_of[:], -0.5).then_inc(power_made, 1)
            pool.wait_ge(power_made, 1)
            pool.wait_ge(var_ready, 1)
            pool.tensor_tensor(rstd[:], rstd[:], power_of[:], ALU.pow).then_inc(rstd_ready, 1)
            with pool.Fori(0, 2) as half:
                for j in range(HB):
                    pool.wait_ge(y_made, half * HB + (j + 1))
                    settle(pool)
                    pool.dma_start(out[half * HB + j], y[:, half * HB + j, :]).then_inc(stored, 16)
            pool.wait_ge(stored, 16 * B)

        @block.scalar
        def _(act):
            act.sem_inc(rows_hi, 2)
            act.sem_inc(gelu_done, 2)
            with act.Fori(0, B // 2) as pair:
                for u in range(2):
                    b = pair * 2 + u
                    act.wait_ge(rows_turned, b + 3)
                    act.activation(in_h[:, b], A[u][:, 0:DC * L].rearrange("p (c l) -> p c l", c=DC), ACT.Copy)\
                       .then_inc(rows_hi, 1)
            act.wait_ge(vectors_landed, 64)
            with act.Fori(0, 2) as half:
                def split_first(u, k):
                    act.wait_ge(w_landed[u], (k - u) * 8 + 32)
                    settle(act)
                    act.activation(w1_h[:, u % 2], w1_raw[:, u], ACT.Copy).then_inc(w1_hi, 1)

                def split_second(u, k):
                    act.wait_ge(fc2_done, k + 1)
                    settle(act)
                    act.activation(w2_h[:, u % 2], w2_raw[:, u], ACT.Copy).then_inc(w2_hi, 1)

                def four_of(four, more):
                    for u in range(4):
                        v, t = u % 2, four * 4 + u
                        k = half * FT + t
                        act.wait_ge(fc1_ready, k + 1)
                        act.wait_ge(fc2_done, k + 1)
                        act.activation(g[:, v, :], A[v][:, 0:HL], ACT.Gelu, bias=b1[:, bass.ds(t, 1)])\
                           .then_inc(gelu_done, 1)
                        act.wait_ge(gelu_done, k + 3)
                        act.activation(g_h[:, v, :], g[:, v, :], ACT.Copy).then_inc(g_hi, 1)
                        if more or u < 2:
                            split_first((u + 2) % 4, k + 2)
                        if more or u < 3:
                            split_second((u + 1) % 4, k + 1)

                split_first(0, half * FT)
                split_first(1, half * FT + 1)
                split_second(0, half * FT)
                with act.Fori(0, FT // 4 - 1) as four:
                    four_of(four, True)
                four_of(FT // 4 - 1, False)

        @block.tensor
        def _(pe):
            pe.sem_inc(rows_turned, 2)
            pe.sem_inc(fc2_done, 2)
            with pe.Fori(0, B // 2) as pair:
                for u in range(2):
                    b = pair * 2 + u
                    pe.wait_ge(rows_made, b + 1)
                    pe.wait_ge(rows_hi, b + 1)
                    pe.wait_ge(rows_lo, b + 1)
                    for c in range(DC):
                        last = pe.transpose(A[u][:, c * L:(c + 1) * L], rows[:, u, c * P:(c + 1) * P], ident[0:L, 0:L])
                    last.then_inc(rows_turned, 1)
            pe.wait_ge(rows_lo, B + 2)
            with pe.Fori(0, 2) as half:
                def second(u, k, first, last):
                    pe.wait_ge(w2_lo, k + 5)
                    pe.wait_ge(g_lo, k + 1)
                    if first:
                        pe.wait_ge(taken, half * HB + 1)
                    for j in range(HB):
                        cols = slice(j * L, (j + 1) * L)
                        terms = [(g_l, w2_h), (g_h, w2_l), (g_h, w2_h)]
                        for m, (l, r) in enumerate(terms):
                            mm = pe.matmul(R[j][0:L, :], l[:, u, cols], r[:, u, :], start=first and m == 0,
                                           stop=last and m == 2)
                    mm.then_inc(fc2_done, 1)

                def pair_of(first, last, pair):
                    for u in range(2):
                        k = pair * 2 + u
                        pe.wait_ge(w1_lo, k + 1)
                        pe.wait_ge(gelu_done, k + 1)
                        terms = [(l[:, u, c, :], r[:, bass.ds(half * HB, HB), c, :]) for c in range(DC)
                                 for l, r in ((w1_l, in_h), (w1_h, in_l), (w1_h, in_h))]
                        for m, (l, r) in enumerate(terms):
                            mm = pe.matmul(A[u][:, 0:HL], l, r, start=m == 0, stop=m == len(terms) - 1)
                        mm.then_inc(fc1_ready, 1)
                        if not (first and u == 0):
                            second(1 - u, k - 1, first and u == 1, False)
                    if last:
                        second(1, pair * 2 + 1, False, True)

                pairs(pe, half, pair_of)

        @block.vector
        def _(vec):
            vec.sem_inc(rows_lo, 2)
            vec.sem_inc(taken, 1)
            vec.sem_inc(w2_lo, 4)
            with vec.Fori(0, B) as b:
                vec.bn_stats(stats[:, b, :], X[:, b, :]).then_inc(stat_made, 1)
            vec.wait_ge(stat_made, B)
            for b in range(B):
                vec.bn_aggr(moments[:, b, :], stats[:, b, :]).then_inc(moment_made, 1)
            vec.wait_ge(moment_made, B)
            vec.tensor_scalar(rstd[:], moments[:, :, 1], 1e-5, None, ALU.add).then_inc(var_ready, 1)
            vec.wait_ge(vectors_landed, 64)
            vec.wait_ge(rstd_ready, 1)

            def centre(b):
                vec.wait_ge(rows_turned, b + 1)
                vec.scalar_tensor_tensor(rows[:, b % 2, :], X[:, b, :], moments[:, b, 0:1], gamma[:],
                                         ALU.subtract, ALU.mult).then_inc(centred, 1)

            def low(b):
                vec.wait_ge(rows_hi, b + 3)
                vec.tensor_tensor(in_l[:, b], A[b % 2][:, 0:DC * L].rearrange("p (c l) -> p c l", c=DC), in_h[:, b],
                                  ALU.subtract).then_inc(rows_lo, 1)

            centre(0)
            for b in range(B):
                vec.wait_ge(centred, b + 1)
                vec.scalar_tensor_tensor(rows[:, b % 2, :], rows[:, b % 2, :], rstd[:, b:b + 1], beta[:],
                                         ALU.mult, ALU.add).then_inc(rows_made, 1)
                if b + 1 < B:
                    centre(b + 1)
                if b >= 1:
                    low(b - 1)
            low(B - 1)
            with vec.Fori(0, 2) as half:
                def split_first(u, k):
                    vec.wait_ge(w1_hi, k + 1)
                    vec.tensor_tensor(w1_l[:, u % 2], w1_raw[:, u], w1_h[:, u % 2], ALU.subtract).then_inc(w1_lo, 1)

                def split_second(u, k):
                    vec.wait_ge(w2_hi, k + 1)
                    vec.tensor_tensor(w2_l[:, u % 2], w2_raw[:, u], w2_h[:, u % 2], ALU.subtract).then_inc(w2_lo, 1)

                def four_of(four, more):
                    for u in range(4):
                        v, k = u % 2, half * FT + four * 4 + u
                        vec.wait_ge(g_hi, k + 1)
                        vec.tensor_tensor(g_l[:, v, :], g[:, v, :], g_h[:, v, :], ALU.subtract).then_inc(g_lo, 1)
                        if more or u < 2:
                            split_first((u + 2) % 4, k + 2)
                        if more or u < 3:
                            split_second((u + 1) % 4, k + 1)

                split_first(0, half * FT)
                split_first(1, half * FT + 1)
                split_second(0, half * FT)
                with vec.Fori(0, FT // 4 - 1) as four:
                    four_of(four, True)
                four_of(FT // 4 - 1, False)
                vec.wait_ge(fc2_done, half * FT + (FT + 2))
                for j in range(HB):
                    b = half * HB + j
                    vec.tensor_tensor(y[:, b, :], R[j][0:L, :], X[:, b, :], ALU.add).then_inc(taken, 1)
                    vec.wait_ge(taken, b + 2)
                    vec.tensor_tensor(y[:, b, :], y[:, b, :], b2[:], ALU.add).then_inc(y_made, 1)


def kernel(**inputs):
    import numpy as _np
    import concourse.bacc as _bacc
    from concourse import mybir as _mybir
    from concourse.bass_utils import run_bass_kernel_spmd as _run

    nc = _bacc.Bacc("TRN2", target_bir_lowering=False, num_devices=1)
    arrays, args = {}, {}
    for name, value in inputs.items():
        array = _np.ascontiguousarray(value)
        if array.dtype == _np.bool_:
            array = array.view(_np.uint8)
        arrays[f"in_{name}"] = array
        args[name] = nc.dram_tensor(f"in_{name}", array.shape, _mybir.dt.from_np(array.dtype),
                                    kind="ExternalInput").ap()
    out = nc.dram_tensor("out", [B, L, D], F32, kind="ExternalOutput").ap()
    build(nc, args, out)
    r = _run(nc, [arrays], core_ids=[0])
    return r.results[0]["out"]
```
